# Optimizing a Trainium2 kernel written in Bass

```python
import numpy as np
import jax
import jax.numpy as jnp

def _softmax(x, axis=-1):
    return jax.nn.softmax(x, axis=axis)

def _gelu(x):
    return jax.nn.gelu(x, approximate=True)

def _silu(x):
    return jax.nn.silu(x)

def _sigmoid(x):
    return jax.nn.sigmoid(x)

def _layernorm(x, axis=-1, eps=1e-05):
    m = jnp.mean(x, axis=axis, keepdims=True)
    v = jnp.var(x, axis=axis, keepdims=True)
    return (x - m) / jnp.sqrt(v + eps)

def _scatter_add(tgt, idx, src, axis=0):
    return tgt.at[idx].add(src)

def _segment_sum(src, seg, n):
    return jax.ops.segment_sum(src, seg, n)
kernel_name = 'mk_conv_preact_d4_conv_nchw384_r2_580d46'

def setup_inputs(seed: int=0):
    np.random.seed(seed)
    _w = jnp.asarray

    def _rec_inputs():
        import jax
        import jax.numpy as jnp
        _gk = jax.random.key(seed)
        x = -4.65e-05 + 0.9999 * jax.random.normal(jax.random.fold_in(_gk, 1), (1, 192, 128, 128), jnp.float32)
        return x
    x = _rec_inputs()

    def _L0_conv_setup():
        import jax, jax.numpy as jnp
        import numpy as np
        B, DIM, H, W = (2, 192, 128, 128)
        HID = DIM * 1
        P = 8
        key = jax.random.key(seed)
        k0, k1, k2, k3, k4 = jax.random.split(key, 5)
        x = jax.random.normal(k0, (B, DIM, H, W), jnp.float32)
        fft_filter = jax.random.normal(k1, (HID, P, P // 2 + 1), jnp.float32)
        w_in = jax.random.normal(k2, (HID, DIM), jnp.float32) * (1.0 / np.sqrt(DIM))
        w_dw = jax.random.normal(k3, (HID, 1, 3, 3), jnp.float32) * (1.0 / 3.0)
        w_out = jax.random.normal(k4, (DIM, HID // 2), jnp.float32) * (1.0 / np.sqrt(HID // 2))
        return {'x': x, 'fft_filter': fft_filter, 'w_in': w_in, 'w_dw': w_dw, 'w_out': w_out}
    _L0_conv_all = _L0_conv_setup()
    _L0_conv_in = {k: v for k, v in _L0_conv_all.items() if k in ('fft_filter', 'w_in', 'w_dw', 'w_out')}
    del _L0_conv_all

    def _L1_conv_setup():
        import jax, jax.numpy as jnp
        import numpy as np
        D_MODEL = 192
        D_STATE = 32
        D_CONV = 3
        EXPAND = 2
        HEADDIM = 32
        NGROUPS = 1
        CHUNK = 128
        D_INNER = EXPAND * D_MODEL
        NHEADS = D_INNER // HEADDIM
        CONV_DIM = D_INNER + 2 * NGROUPS * D_STATE
        D_IN_PROJ = 2 * D_INNER + 2 * NGROUPS * D_STATE + NHEADS
        EPS = 1e-05

        def _chunk_scan(x, dt, A, Bm, Cm):
            b, l, h, p = x.shape
            nc = l // CHUNK
            xc = x.reshape(b, nc, CHUNK, h, p)
            dtc = dt.reshape(b, nc, CHUNK, h)
            hpg = h // NGROUPS
            Bh = jnp.repeat(Bm.reshape(b, nc, CHUNK, NGROUPS, D_STATE), hpg, axis=3)
            Ch = jnp.repeat(Cm.reshape(b, nc, CHUNK, NGROUPS, D_STATE), hpg, axis=3)
            dA = dtc * A
            dA_cs = jnp.cumsum(dA, axis=2)
            Lmat = jnp.exp(dA_cs[:, :, :, None, :] - dA_cs[:, :, None, :, :])
            causal = jnp.tril(jnp.ones((CHUNK, CHUNK), bool))
            att = jnp.einsum('bcihn,bcjhn->bcijh', Ch, Bh) * Lmat * dtc[:, :, None, :, :]
            att = jnp.where(causal[None, None, :, :, None], att, 0.0)
            y_intra = jnp.einsum('bcijh,bcjhp->bcihp', att, xc)
            decay_to_end = jnp.exp(dA_cs[:, :, -1:, :] - dA_cs)
            states = jnp.einsum('bcjhn,bcjh,bcjhp->bchpn', Bh, decay_to_end * dtc, xc)
            chunk_decay = jnp.exp(dA_cs[:, :, -1, :])

            def step(carry, inp):
                st, dec = inp
                new = carry * dec[:, :, None, None] + st
                return (new, carry)
            init = jnp.zeros((b, h, p, D_STATE), x.dtype)
            _, prevs = jax.lax.scan(step, init, (jnp.moveaxis(states, 1, 0), jnp.moveaxis(chunk_decay, 1, 0)))
            prev_states = jnp.moveaxis(prevs, 0, 1)
            y_inter = jnp.einsum('bcihn,bcih,bchpn->bcihp', Ch, jnp.exp(dA_cs), prev_states)
            return (y_intra + y_inter).reshape(b, l, h, p)
        key = jax.random.key(seed)
        ks = jax.random.split(key, 8)
        B, H, W = (16, 32, 32)
        u = jax.random.normal(ks[0], (B, D_MODEL, H, W), jnp.float32)
        in_proj_w = jax.random.normal(ks[1], (D_IN_PROJ, D_MODEL), jnp.float32) / np.sqrt(D_MODEL)
        conv_w = jax.random.normal(ks[2], (CONV_DIM, 1, D_CONV, D_CONV), jnp.float32) / np.sqrt(D_CONV * D_CONV)
        conv_b = jax.random.normal(ks[3], (CONV_DIM,), jnp.float32) * 0.01
        dt = jnp.exp(jax.random.uniform(ks[4], (NHEADS,)) * (np.log(0.1) - np.log(0.001)) + np.log(0.001))
        dt = jnp.clip(dt, 0.0001, None)
        dt_bias = dt + jnp.log(-jnp.expm1(-dt))
        A_log = jnp.log(jax.random.uniform(ks[5], (NHEADS,), minval=1.0, maxval=16.0))
        D = jnp.ones((NHEADS,), jnp.float32)
        norm_w = jnp.ones((D_INNER,), jnp.float32)
        norm_b = jnp.zeros((D_INNER,), jnp.float32)
        out_proj_w = jax.random.normal(ks[6], (D_MODEL, D_INNER), jnp.float32) / np.sqrt(D_INNER)
        return {'u': u, 'in_proj_w': in_proj_w, 'conv_w': conv_w, 'conv_b': conv_b, 'dt_bias': dt_bias, 'A_log': A_log, 'D': D, 'norm_w': norm_w, 'norm_b': norm_b, 'out_proj_w': out_proj_w}
    _L1_conv_all = _L1_conv_setup()
    _L1_conv_in = {k: v for k, v in _L1_conv_all.items() if k in ('in_proj_w', 'conv_w', 'conv_b', 'dt_bias', 'A_log', 'D', 'norm_w', 'norm_b', 'out_proj_w')}
    del _L1_conv_all

    def _L2_conv_setup():
        import jax, jax.numpy as jnp
        import numpy as np
        B, DIM, H, W = (2, 192, 128, 128)
        HID = DIM * 1
        P = 8
        key = jax.random.key(seed)
        k0, k1, k2, k3, k4 = jax.random.split(key, 5)
        x = jax.random.normal(k0, (B, DIM, H, W), jnp.float32)
        fft_filter = jax.random.normal(k1, (HID, P, P // 2 + 1), jnp.float32)
        w_in = jax.random.normal(k2, (HID, DIM), jnp.float32) * (1.0 / np.sqrt(DIM))
        w_dw = jax.random.normal(k3, (HID, 1, 3, 3), jnp.float32) * (1.0 / 3.0)
        w_out = jax.random.normal(k4, (DIM, HID // 2), jnp.float32) * (1.0 / np.sqrt(HID // 2))
        return {'x': x, 'fft_filter': fft_filter, 'w_in': w_in, 'w_dw': w_dw, 'w_out': w_out}
    _L2_conv_all = _L2_conv_setup()
    _L2_conv_in = {k: v for k, v in _L2_conv_all.items() if k in ('fft_filter', 'w_in', 'w_dw', 'w_out')}
    del _L2_conv_all

    def _L3_conv_setup():
        import jax, jax.numpy as jnp
        import numpy as np
        B, DIM, H, W = (2, 192, 128, 128)
        HID = DIM * 1
        P = 8
        key = jax.random.key(seed)
        k0, k1, k2, k3, k4 = jax.random.split(key, 5)
        x = jax.random.normal(k0, (B, DIM, H, W), jnp.float32)
        fft_filter = jax.random.normal(k1, (HID, P, P // 2 + 1), jnp.float32)
        w_in = jax.random.normal(k2, (HID, DIM), jnp.float32) * (1.0 / np.sqrt(DIM))
        w_dw = jax.random.normal(k3, (HID, 1, 3, 3), jnp.float32) * (1.0 / 3.0)
        w_out = jax.random.normal(k4, (DIM, HID // 2), jnp.float32) * (1.0 / np.sqrt(HID // 2))
        return {'x': x, 'fft_filter': fft_filter, 'w_in': w_in, 'w_dw': w_dw, 'w_out': w_out}
    _L3_conv_all = _L3_conv_setup()
    _L3_conv_in = {k: v for k, v in _L3_conv_all.items() if k in ('fft_filter', 'w_in', 'w_dw', 'w_out')}
    del _L3_conv_all
    return {'x': x, 'L0_conv_fft_filter': _L0_conv_in['fft_filter'], 'L0_conv_w_in': _L0_conv_in['w_in'], 'L0_conv_w_dw': _L0_conv_in['w_dw'], 'L0_conv_w_out': _L0_conv_in['w_out'], 'L1_conv_in_proj_w': _L1_conv_in['in_proj_w'], 'L1_conv_conv_w': _L1_conv_in['conv_w'], 'L1_conv_conv_b': _L1_conv_in['conv_b'], 'L1_conv_dt_bias': _L1_conv_in['dt_bias'], 'L1_conv_A_log': _L1_conv_in['A_log'], 'L1_conv_D': _L1_conv_in['D'], 'L1_conv_norm_w': _L1_conv_in['norm_w'], 'L1_conv_norm_b': _L1_conv_in['norm_b'], 'L1_conv_out_proj_w': _L1_conv_in['out_proj_w'], 'L2_conv_fft_filter': _L2_conv_in['fft_filter'], 'L2_conv_w_in': _L2_conv_in['w_in'], 'L2_conv_w_dw': _L2_conv_in['w_dw'], 'L2_conv_w_out': _L2_conv_in['w_out'], 'L3_conv_fft_filter': _L3_conv_in['fft_filter'], 'L3_conv_w_in': _L3_conv_in['w_in'], 'L3_conv_w_dw': _L3_conv_in['w_dw'], 'L3_conv_w_out': _L3_conv_in['w_out']}

def reference(x, L0_conv_fft_filter, L0_conv_w_in, L0_conv_w_dw, L0_conv_w_out, L1_conv_in_proj_w, L1_conv_conv_w, L1_conv_conv_b, L1_conv_dt_bias, L1_conv_A_log, L1_conv_D, L1_conv_norm_w, L1_conv_norm_b, L1_conv_out_proj_w, L2_conv_fft_filter, L2_conv_w_in, L2_conv_w_dw, L2_conv_w_out, L3_conv_fft_filter, L3_conv_w_in, L3_conv_w_dw, L3_conv_w_out):
    import jax
    import jax.numpy as jnp

    def _L0_conv_ref(x, fft_filter, w_in, w_dw, w_out):
        import jax, jax.numpy as jnp
        import numpy as np
        B, DIM, H, W = (2, 192, 128, 128)
        HID = DIM * 1
        P = 8
        b, c, h, w = x.shape
        hid = w_in.shape[0]
        hb, wb = (h // P, w // P)
        t = jnp.einsum('bchw,oc->bohw', x, w_in)
        tp = t.reshape(b, hid, hb, P, wb, P)
        tf = jnp.fft.rfft2(tp, axes=(3, 5))
        tf = tf * fft_filter[None, :, None, :, None, :]
        tp = jnp.fft.irfft2(tf, s=(P, P), axes=(3, 5))
        t = tp.reshape(b, hid, h, w)
        t = jax.lax.conv_general_dilated(t, w_dw, window_strides=(1, 1), padding='SAME', feature_group_count=hid, dimension_numbers=('NCHW', 'OIHW', 'NCHW'))
        x1, x2 = (t[:, :hid // 2], t[:, hid // 2:])
        g = jax.nn.gelu(x1, approximate=False) * x2
        return jnp.einsum('bchw,oc->bohw', g, w_out)

    def _L1_conv_ref(u, in_proj_w, conv_w, conv_b, dt_bias, A_log, D, norm_w, norm_b, out_proj_w):
        import jax, jax.numpy as jnp
        import numpy as np
        D_MODEL = 192
        D_STATE = 32
        D_CONV = 3
        EXPAND = 2
        HEADDIM = 32
        NGROUPS = 1
        CHUNK = 128
        D_INNER = EXPAND * D_MODEL
        NHEADS = D_INNER // HEADDIM
        CONV_DIM = D_INNER + 2 * NGROUPS * D_STATE
        D_IN_PROJ = 2 * D_INNER + 2 * NGROUPS * D_STATE + NHEADS
        EPS = 1e-05

        def _chunk_scan(x, dt, A, Bm, Cm):
            b, l, h, p = x.shape
            nc = l // CHUNK
            xc = x.reshape(b, nc, CHUNK, h, p)
            dtc = dt.reshape(b, nc, CHUNK, h)
            hpg = h // NGROUPS
            Bh = jnp.repeat(Bm.reshape(b, nc, CHUNK, NGROUPS, D_STATE), hpg, axis=3)
            Ch = jnp.repeat(Cm.reshape(b, nc, CHUNK, NGROUPS, D_STATE), hpg, axis=3)
            dA = dtc * A
            dA_cs = jnp.cumsum(dA, axis=2)
            Lmat = jnp.exp(dA_cs[:, :, :, None, :] - dA_cs[:, :, None, :, :])
            causal = jnp.tril(jnp.ones((CHUNK, CHUNK), bool))
            att = jnp.einsum('bcihn,bcjhn->bcijh', Ch, Bh) * Lmat * dtc[:, :, None, :, :]
            att = jnp.where(causal[None, None, :, :, None], att, 0.0)
            y_intra = jnp.einsum('bcijh,bcjhp->bcihp', att, xc)
            decay_to_end = jnp.exp(dA_cs[:, :, -1:, :] - dA_cs)
            states = jnp.einsum('bcjhn,bcjh,bcjhp->bchpn', Bh, decay_to_end * dtc, xc)
            chunk_decay = jnp.exp(dA_cs[:, :, -1, :])

            def step(carry, inp):
                st, dec = inp
                new = carry * dec[:, :, None, None] + st
                return (new, carry)
            init = jnp.zeros((b, h, p, D_STATE), x.dtype)
            _, prevs = jax.lax.scan(step, init, (jnp.moveaxis(states, 1, 0), jnp.moveaxis(chunk_decay, 1, 0)))
            prev_states = jnp.moveaxis(prevs, 0, 1)
            y_inter = jnp.einsum('bcihn,bcih,bchpn->bcihp', Ch, jnp.exp(dA_cs), prev_states)
            return (y_intra + y_inter).reshape(b, l, h, p)
        B, C, H, W = u.shape
        L = H * W
        useq = u.reshape(B, C, L).transpose(0, 2, 1)
        zxbcdt = useq @ in_proj_w.T
        z = zxbcdt[..., :D_INNER]
        xBC = zxbcdt[..., D_INNER:D_INNER + CONV_DIM]
        dt = jax.nn.softplus(zxbcdt[..., D_INNER + CONV_DIM:] + dt_bias)
        xBC = xBC.reshape(B, H, W, CONV_DIM)
        kern = jnp.transpose(conv_w, (2, 3, 1, 0))
        xBC = jax.lax.conv_general_dilated(xBC, kern, (1, 1), 'SAME', dimension_numbers=('NHWC', 'HWIO', 'NHWC'), feature_group_count=CONV_DIM) + conv_b
        xBC = jax.nn.silu(xBC).reshape(B, L, CONV_DIM)
        x = xBC[..., :D_INNER].reshape(B, L, NHEADS, HEADDIM)
        Bm = xBC[..., D_INNER:D_INNER + NGROUPS * D_STATE].reshape(B, L, NGROUPS, D_STATE)
        Cm = xBC[..., D_INNER + NGROUPS * D_STATE:].reshape(B, L, NGROUPS, D_STATE)
        A = -jnp.exp(A_log)
        y = _chunk_scan(x, dt, A, Bm, Cm) + D[None, None, :, None] * x
        y = y.reshape(B, L, D_INNER)
        mu = jnp.mean(y, axis=-1, keepdims=True)
        var = jnp.var(y, axis=-1, keepdims=True)
        y = (y - mu) / jnp.sqrt(var + EPS) * norm_w + norm_b
        y = y * z
        out = y @ out_proj_w.T
        return out.reshape(B, H, W, C).transpose(0, 3, 1, 2)

    def _L2_conv_ref(x, fft_filter, w_in, w_dw, w_out):
        import jax, jax.numpy as jnp
        import numpy as np
        B, DIM, H, W = (2, 192, 128, 128)
        HID = DIM * 1
        P = 8
        b, c, h, w = x.shape
        hid = w_in.shape[0]
        hb, wb = (h // P, w // P)
        t = jnp.einsum('bchw,oc->bohw', x, w_in)
        tp = t.reshape(b, hid, hb, P, wb, P)
        tf = jnp.fft.rfft2(tp, axes=(3, 5))
        tf = tf * fft_filter[None, :, None, :, None, :]
        tp = jnp.fft.irfft2(tf, s=(P, P), axes=(3, 5))
        t = tp.reshape(b, hid, h, w)
        t = jax.lax.conv_general_dilated(t, w_dw, window_strides=(1, 1), padding='SAME', feature_group_count=hid, dimension_numbers=('NCHW', 'OIHW', 'NCHW'))
        x1, x2 = (t[:, :hid // 2], t[:, hid // 2:])
        g = jax.nn.gelu(x1, approximate=False) * x2
        return jnp.einsum('bchw,oc->bohw', g, w_out)

    def _L3_conv_ref(x, fft_filter, w_in, w_dw, w_out):
        import jax, jax.numpy as jnp
        import numpy as np
        B, DIM, H, W = (2, 192, 128, 128)
        HID = DIM * 1
        P = 8
        b, c, h, w = x.shape
        hid = w_in.shape[0]
        hb, wb = (h // P, w // P)
        t = jnp.einsum('bchw,oc->bohw', x, w_in)
        tp = t.reshape(b, hid, hb, P, wb, P)
        tf = jnp.fft.rfft2(tp, axes=(3, 5))
        tf = tf * fft_filter[None, :, None, :, None, :]
        tp = jnp.fft.irfft2(tf, s=(P, P), axes=(3, 5))
        t = tp.reshape(b, hid, h, w)
        t = jax.lax.conv_general_dilated(t, w_dw, window_strides=(1, 1), padding='SAME', feature_group_count=hid, dimension_numbers=('NCHW', 'OIHW', 'NCHW'))
        x1, x2 = (t[:, :hid // 2], t[:, hid // 2:])
        g = jax.nn.gelu(x1, approximate=False) * x2
        return jnp.einsum('bchw,oc->bohw', g, w_out)

    def _gn(v, G=32, eps=1e-05):
        B_, C_, H_, W_ = v.shape
        g = v.reshape(B_, G, C_ // G, H_, W_)
        m = jnp.mean(g, axis=(2, 3, 4), keepdims=True)
        s = jnp.var(g, axis=(2, 3, 4), keepdims=True)
        return ((g - m) / jnp.sqrt(s + eps)).reshape(v.shape)

    def _ln_c(v, eps=1e-06):
        m = jnp.mean(v, axis=1, keepdims=True)
        s = jnp.var(v, axis=1, keepdims=True)
        return (v - m) / jnp.sqrt(s + eps)

    def _ln_t(v, eps=1e-05):
        m = jnp.mean(v, axis=-1, keepdims=True)
        s = jnp.var(v, axis=-1, keepdims=True)
        return (v - m) / jnp.sqrt(s + eps)

    def _to_tokens(v):
        B_, C_, H_, W_ = v.shape
        return v.reshape(B_, C_, H_ * W_).transpose(0, 2, 1)

    def _from_tokens(t, like):
        B_, C_, H_, W_ = like.shape
        return t.transpose(0, 2, 1).reshape(B_, C_, H_, W_)
    x = x + _L0_conv_ref(_gn(x), L0_conv_fft_filter, L0_conv_w_in, L0_conv_w_dw, L0_conv_w_out)
    x = x + _L1_conv_ref(_gn(x), L1_conv_in_proj_w, L1_conv_conv_w, L1_conv_conv_b, L1_conv_dt_bias, L1_conv_A_log, L1_conv_D, L1_conv_norm_w, L1_conv_norm_b, L1_conv_out_proj_w)
    x = x + _L2_conv_ref(_gn(x), L2_conv_fft_filter, L2_conv_w_in, L2_conv_w_dw, L2_conv_w_out)
    x = x + _L3_conv_ref(_gn(x), L3_conv_fft_filter, L3_conv_w_in, L3_conv_w_dw, L3_conv_w_out)
    return x

_drawn_inputs = setup_inputs


def setup_inputs(seed=0):
    import zlib

    import numpy as np

    out = dict(_drawn_inputs(seed))
    spreads = {'L1_conv_D': (1.0, 0.2), 'L1_conv_norm_w': (1.0, 0.2), 'L1_conv_norm_b': (0.0, 0.1)}
    factors = {'L1_conv_conv_b': 6.815}
    for name, (base, spread) in spreads.items():
        noise = np.random.default_rng([zlib.crc32(name.encode()), seed]).standard_normal(out[name].shape)
        drawn = base * np.exp(spread * noise) if base else spread * noise
        out[name] = jnp.asarray(drawn.astype(out[name].dtype))
    for name, factor in factors.items():
        out[name] = (out[name] * factor).astype(out[name].dtype)
    return out
```

```python
from contextlib import ExitStack

import numpy as np
import concourse.bass as bass
from concourse import mybir

ALU = mybir.AluOpType
ACT = mybir.ActivationFunctionType
F32 = mybir.dt.float32
BF16 = mybir.dt.bfloat16

W = 128
C = 192
CH = C // 2
PS = 8
SLAB = 2 * PS
NPC = W // PS
NF = PS * (PS // 2 + 1)
GROUPS = 32
GN_EPS = 1e-5

D_INNER = 384
N_STATE = 32
N_HEADS = 12
HEAD = 32
CONV_DIM = D_INNER + 2 * N_STATE
LN_EPS = 1e-5

LAYERS = (0, 1, 2, 3)

CC = 16
BANK = 512
OPB = 8


class Phase:

    def __init__(self, nc, name):
        self.nc, self.name = nc, name

    def __enter__(self):
        self.stack = ExitStack()
        self.sems = []
        return self

    def sb(self, name, shape, dt=F32):
        return self.stack.enter_context(self.nc.sbuf_tensor(f"{self.name}_{name}", shape, dt))

    def ps(self, name, shape, dt=F32):
        return self.stack.enter_context(self.nc.psum_tensor(f"{self.name}_{name}", shape, dt))

    def sem(self, name, credit=0):
        s = self.nc.alloc_semaphore(name=f"{self.name}_{name}")
        self.sems.append(s)
        if credit:
            self.nc.sync.sem_inc(s, credit)
        return s

    def __exit__(self, *exc):
        if exc[0] is None:
            self.nc.clear_and_free_semaphores(self.sems)
            self.nc.all_engine_barrier()
        self.stack.close()


def hold(eng, sem, value, passed):
    eng.wait_ge(sem, value)
    eng.sem_inc(passed, 1)


def load_constants(nc, name, pairs):
    with Phase(nc, name) as ph:
        landed, rounded = ph.sem("landed"), ph.sem("rounded")
        exact = [tile if tile.dtype == F32 else ph.sb(f"exact{n}", list(tile.shape)) for n, (tile, _) in enumerate(pairs)]
        with nc.Block() as block:
            @block.sync
            def _(sp):
                for target, (_, source) in zip(exact, pairs):
                    sp.dma_start(target[:], source).then_inc(landed, 16)
                sp.wait_ge(landed, 16 * len(pairs))

            @block.vector
            def _(dve):
                dve.wait_ge(landed, 16 * len(pairs))
                for target, (tile, _) in zip(exact, pairs):
                    if tile.dtype != F32:
                        nc.vector.tensor_copy(tile[:], target[:]).then_inc(rounded, 1)


def input_stats(nc, x, stats, H):
    slabs = H // SLAB
    n = SLAB * W // BANK
    with Phase(nc, "instat") as ph:
        xt = ph.sb("xt", [CH, 2, 2, SLAB * W])
        landed = [ph.sem(f"slab_landed{b}") for b in range(2)]
        counted = [ph.sem(f"slab_counted{b}", credit=1) for b in range(2)]
        with nc.Block() as block:
            @block.sync
            def _(sp):
                with sp.Fori(0, slabs // 2) as i:
                    for b in range(2):
                        sp.wait_ge(counted[b], i * 2 * n + 1)
                        sp.dma_start(xt[:, b], x[:, :, bass.ds((i * 2 + b) * SLAB * W, SLAB * W)]).then_inc(landed[b], 16)

            @block.vector
            def _(dve):
                with dve.Fori(0, slabs // 2) as i:
                    for b in range(2):
                        dve.wait_ge(landed[b], i * 16 + 16)
                        for k in range(2):
                            for q in range(n):
                                nc.vector.bn_stats(stats[:, k, bass.ds((i * 2 + b) * n + q, 1), :],
                                                   xt[:, b, k, q * BANK:(q + 1) * BANK]).then_inc(counted[b], 1)


def fold_norm(nc, name, stats, group_mean, wT, wf, O, extra=None):
    with Phase(nc, name) as ph:
        raw = ph.sb("raw", [CH, 2, O])
        mv = ph.sb("mv", [CH, 2, 2])
        gm = ph.sb("gm", [CH, 2])
        dev = ph.sb("dev", [CH, 2])
        dev2 = ph.sb("dev2", [CH, 2])
        var = ph.sb("var", [CH, 2])
        vare = ph.sb("vare", [CH, 2])
        std = ph.sb("std", [CH, 2])
        rstd = ph.sb("rstd", [CH, 2])
        negm = ph.sb("negm", [CH, 2, CH + 1])
        xrow = ph.sb("xrow", [CH + 1, 16])
        pm = ph.ps("pm", [CH, BANK])
        pv = ph.ps("pv", [CH, BANK])
        pb = [ph.ps(f"pb{j}", [CH + 1, BANK]) for j in range((O + BANK - 1) // BANK)]
        landed, zero, agg, mean, dv, pvar, sd, r, scaled, bias, d2, done = (ph.sem(s) for s in (
            "weights_landed", "negm_zeroed", "aggregated", "group_mean", "deviation", "group_var",
            "std_ready", "rstd_ready", "weights_scaled", "bias_ready", "square_ready", "done"))
        with nc.Block() as block:
            @block.sync
            def _(sp):
                sp.dma_start(raw[:], wT).then_inc(landed, 16)
                if extra is not None:
                    sp.dma_start(xrow[CH:CH + 1, 0:extra.shape[1]], extra).then_inc(landed, 16)
                sp.wait_ge(landed, 16 if extra is None else 32)

            @block.vector
            def _(dve):
                nc.vector.memset(negm[:], 0.0).then_inc(zero, 1)
                for k in range(2):
                    nc.vector.bn_aggr(mv[:, k, :], stats[:, k]).then_inc(agg, 1)
                dve.wait_ge(mean, 1)
                dve.wait_ge(agg, 2)
                nc.vector.tensor_copy(gm[:], pm[:, 0:2]).then_inc(dv, 1)
                dve.wait_ge(dv, 1)
                nc.vector.tensor_tensor(dev[:], mv[:, :, 0], gm[:], ALU.subtract).then_inc(dv, 1)
                dve.wait_ge(dv, 2)
                nc.vector.tensor_tensor(dev2[:], dev[:], dev[:], ALU.mult).then_inc(dv, 1)
                dve.wait_ge(dv, 3)
                nc.vector.tensor_tensor(var[:], dev2[:], mv[:, :, 1], ALU.add).then_inc(d2, 1)
                dve.wait_ge(pvar, 1)
                nc.vector.tensor_scalar(vare[:], pv[:, 0:2], GN_EPS, None, ALU.add).then_inc(dv, 1)
                dve.wait_ge(sd, 1)
                nc.vector.reciprocal(rstd[:], std[:]).then_inc(r, 1)
                dve.wait_ge(r, 1)
                dve.wait_ge(zero, 1)
                dve.wait_ge(landed, 16 if extra is None else 32)
                for k in range(2):
                    nc.vector.tensor_scalar(wf[0:CH, k, :], raw[:, k, :], rstd[:, k:k + 1], None, ALU.mult).then_inc(scaled, 1)
                    nc.vector.tensor_scalar(negm[:, k, CH:CH + 1], gm[:, k:k + 1], -1.0, None, ALU.mult).then_inc(scaled, 1)
                dve.wait_ge(bias, 1)
                for j in range(len(pb)):
                    n = min(BANK, O - j * BANK)
                    nc.vector.tensor_copy(wf[CH:CH + 1, 0, j * BANK:j * BANK + n], pb[j][CH:CH + 1, 0:n]).then_inc(done, 1)
                if extra is not None:
                    dve.wait_ge(done, len(pb))
                    nc.vector.tensor_tensor(wf[CH:CH + 1, 0, O - N_HEADS:O], wf[CH:CH + 1, 0, O - N_HEADS:O],
                                            xrow[CH:CH + 1, 0:N_HEADS], ALU.add).then_inc(done, 1)

            @block.scalar
            def _(act):
                act.wait_ge(dv, 4)
                nc.scalar.activation(std[:], vare[:], ACT.Sqrt).then_inc(sd, 1)

            @block.tensor
            def _(pe):
                pe.wait_ge(agg, 2)
                nc.tensor.matmul(pm[:, 0:2], group_mean[:], mv[:, :, 0], start=True, stop=True).then_inc(mean, 1)
                pe.wait_ge(d2, 1)
                nc.tensor.matmul(pv[:, 0:2], group_mean[:], var[:], start=True, stop=True).then_inc(pvar, 1)
                pe.wait_ge(scaled, 4)
                for j in range(len(pb)):
                    n = min(BANK, O - j * BANK)
                    for k in range(2):
                        last = nc.tensor.matmul(pb[j][:, 0:n], negm[:, k, :], wf[0:CH, k, j * BANK:j * BANK + n],
                                                start=(k == 0), stop=(k == 1))
                last.then_inc(bias, 1)


def project_patches(nc, name, x, wf, t, H):
    slabs = H // SLAB
    fills = NPC // 2
    half = fills // 2
    with Phase(nc, name) as ph:
        xt = ph.sb("xt", [CH, 2, 2, SLAB, W])
        xp = ph.sb("xp", [CH + 1, 2, 2, NPC, SLAB * PS])
        banks = [ph.ps(f"p{j}", [128, 2, C]) for j in range(fills)]
        landed = [ph.sem(f"slab_landed{b}") for b in range(2)]
        ordered = [ph.sem(f"slab_ordered{b}", credit=1) for b in range(2)]
        filled = [ph.sem(f"banks_filled{b}", credit=1) for b in range(2)]
        free = [ph.sem("even_banks_free"), ph.sem("odd_banks_free")]
        ones, passed = ph.sem("ones_set"), ph.sem("waits_passed")
        with nc.Block() as block:
            @block.sync
            def _(sp):
                with sp.Fori(0, slabs // 2) as i:
                    for b in range(2):
                        sp.wait_ge(ordered[b], i * 2 + 1)
                        sp.dma_start(xt[:, b], x[:, :, bass.ds((i * 2 + b) * SLAB * W, SLAB * W)]
                                     .rearrange("p k (h w) -> p k h w", w=W)).then_inc(landed[b], 16)

            @block.gpsimd
            def _(pool):
                nc.gpsimd.memset(xp[CH:CH + 1], 1.0).then_inc(ones, 1)
                with pool.Fori(0, slabs // 2) as i:
                    for b in range(2):
                        pool.wait_ge(landed[b], i * 16 + 16)
                        hold(pool, filled[b], i * fills + 1, passed)
                        for k in range(2):
                            nc.gpsimd.tensor_copy(xp[0:CH, b, k].rearrange("p pc (h w) -> p pc h w", w=PS),
                                                  xt[:, b, k].rearrange("p h (pc w) -> p pc h w", w=PS)).then_inc(ordered[b], 1)

            @block.tensor
            def _(pe):
                pe.wait_ge(ones, 1)
                with pe.Fori(0, slabs // 2) as i:
                    for b in range(2):
                        pe.wait_ge(ordered[b], i * 2 + 3)
                        for j in range(fills):
                            pe.wait_ge(free[j % 2], (i * 2 + b) * half + j // 2 + 1)
                            for q in range(2):
                                for k in range(2):
                                    rows = CH + 1 - k
                                    last = nc.tensor.matmul(banks[j][:, q, :], xp[0:rows, b, k, 2 * j + q, :], wf[0:rows, k, :],
                                                            start=(k == 0), stop=(k == 1))
                            last.then_inc(filled[b], 1)

            def evacuate(eng, copy, parity):
                eng.sem_inc(free[parity], half)
                with eng.Fori(0, slabs // 2) as i:
                    for b in range(2):
                        for j in range(parity, fills, 2):
                            eng.wait_ge(filled[b], i * fills + j + 2)
                            copy(t[:, bass.ds((i * 2 + b) * NPC + 2 * j, 2), :], banks[j][:]).then_inc(free[parity], 1)

            @block.vector
            def _(dve):
                evacuate(dve, nc.vector.tensor_copy, 0)

            @block.scalar
            def _(act):
                evacuate(act, nc.scalar.copy, 1)


def filter_patches(nc, name, t, patch_table, spectrum, f_dram, H):
    CF = 48
    nblk = H // SLAB * NPC
    npix = PS * PS
    fills = npix // OPB
    with Phase(nc, name) as ph:
        table = ph.sb("cosines", [96, npix, 128])
        spec = ph.sb("spectrum", [96, C])
        wc = ph.sb("matrices", [128, 2, CF, 128])
        gen = [ph.ps(f"gen{j}", [128, OPB, CF]) for j in range(4)]
        fb = [ph.ps(f"out{j}", [128, 4, nblk]) for j in range(4)]
        landed, padded, zeroed, built, genlow, genhigh, filled, frd, fra, stored = (ph.sem(s) for s in (
            "tables_landed", "tables_padded", "matrices_zeroed", "gen_bank_built", "upper_patch_copied", "lower_patch_copied",
            "out_bank_filled", "even_out_banks_free", "odd_out_banks_free", "rows_stored"))
        with nc.Block() as block:
            @block.sync
            def _(sp):
                sp.wait_ge(padded, 2)
                sp.dma_start(table[0:NF], patch_table).then_inc(landed, 16)
                sp.dma_start(spec[0:NF], spectrum).then_inc(landed, 16)
                sp.wait_ge(frd, 2 + C // 8)
                sp.wait_ge(fra, 2 + C // 8)
                for s in range(H // SLAB):
                    for hh in range(PS * 2):
                        dst = f_dram[s * SLAB + hh, :, :].rearrange("(pc ww) c -> ww pc c", ww=PS)
                        sp.dma_start(dst, t[hh * PS:(hh + 1) * PS, s * NPC:(s + 1) * NPC, :]).then_inc(stored, 16)
                sp.wait_ge(stored, 16 * H)

            @block.gpsimd
            def _(pool):
                nc.gpsimd.memset(wc[:], 0.0).then_inc(zeroed, 1)

            @block.tensor
            def _(pe):
                pe.wait_ge(landed, 32)
                with pe.Fori(0, C // CF // 2) as i:
                    for b in range(2):
                        s = i * 2 + b
                        for f in range(fills):
                            pe.wait_ge(genlow, s * fills + f + 1)
                            pe.wait_ge(genhigh, s * fills + f + 1)
                            for o in range(OPB):
                                last = nc.tensor.matmul(gen[f % 4][:, o, :], table[:, f * OPB + o, :],
                                                        spec[:, bass.ds(s * CF, CF)], start=True, stop=True)
                            last.then_inc(built, 1)
                        pe.wait_ge(genlow, s * fills + fills + 4)
                        pe.wait_ge(genhigh, s * fills + fills + 4)
                        for q in range(CF // 4):
                            fr = frd if q % 2 == 0 else fra
                            pe.wait_ge(fr, s * (CF // 8) + q // 2 + 1)
                            for c in range(4):
                                last = nc.tensor.matmul(fb[q % 4][:, c, :], wc[:, b, 4 * q + c, :],
                                                        t[:, :, bass.ds(s * CF + 4 * q + c, 1)].rearrange("p n o -> p (n o)"),
                                                        start=True, stop=True)
                            last.then_inc(filled, 1)

            def evacuate(eng, copy, lo, copied, free, parity):
                eng.sem_inc(copied, 4)
                eng.sem_inc(free, 2)
                eng.wait_ge(zeroed, 1)
                with eng.Fori(0, C // CF // 2) as i:
                    for b in range(2):
                        s = i * 2 + b
                        for f in range(fills):
                            eng.wait_ge(built, s * fills + f + 1)
                            copy(wc[lo:lo + 64, b, :, lo + f * OPB:lo + (f + 1) * OPB].rearrange("p c o -> p o c"),
                                 gen[f % 4][lo:lo + 64]).then_inc(copied, 1)
                        for q in range(parity, CF // 4, 2):
                            eng.wait_ge(filled, s * (CF // 4) + q + 1)
                            copy(t[:, :, bass.ds(s * CF + 4 * q, 4)].rearrange("p n c -> p c n"), fb[q % 4][:]).then_inc(free, 1)

            @block.vector
            def _(dve):
                nc.vector.memset(table[:], 0.0).then_inc(padded, 1)
                nc.vector.memset(spec[:], 0.0).then_inc(padded, 1)
                evacuate(dve, nc.vector.tensor_copy, 0, genlow, frd, 0)

            @block.scalar
            def _(act):
                evacuate(act, nc.scalar.copy, 64, genhigh, fra, 1)


def split_taps(nc, name, taps_dram, taps, n):
    with Phase(nc, name) as ph:
        raw = ph.sb("raw", [96, 3, n])
        rest = ph.sb("rest", [96, 3, n])
        rest2 = ph.sb("rest2", [96, 3, n])
        hi = ph.sb("hi", [96, 3, n], BF16)
        mid = ph.sb("mid", [96, 3, n], BF16)
        zeroed, landed, step = ph.sem("zeroed"), ph.sem("taps_landed"), ph.sem("step")
        cols = taps_dram.shape[2]
        with nc.Block() as block:
            @block.sync
            def _(sp):
                sp.wait_ge(zeroed, 1)
                for part in range(3):
                    sp.dma_start(raw[32 * part:32 * part + 3, :, 0:cols], taps_dram).then_inc(landed, 16)
                sp.wait_ge(landed, 48)

            @block.vector
            def _(dve):
                nc.vector.memset(raw[:], 0.0).then_inc(zeroed, 1)
                dve.wait_ge(landed, 48)
                nc.vector.tensor_copy(hi[:], raw[:]).then_inc(step, 1)
                dve.wait_ge(step, 1)
                nc.vector.tensor_tensor(rest[:], raw[:], hi[:], ALU.subtract).then_inc(step, 1)
                dve.wait_ge(step, 2)
                nc.vector.tensor_copy(mid[:], rest[:]).then_inc(step, 1)
                dve.wait_ge(step, 3)
                nc.vector.tensor_tensor(rest2[:], rest[:], mid[:], ALU.subtract).then_inc(step, 1)
                dve.wait_ge(step, 4)
                nc.vector.tensor_copy(taps[0:32], hi[0:32]).then_inc(step, 1)
                nc.vector.tensor_copy(taps[32:64], mid[32:64]).then_inc(step, 1)
                nc.vector.tensor_copy(taps[64:96], rest2[64:96]).then_inc(step, 1)


class Bands:
    FILLS = W // OPB
    CONVS = CC // 4

    def __init__(self, nc, ph, table, taps, rows):
        self.nc, self.table, self.taps, self.rows = nc, table, taps, rows
        self.mats = ph.sb("bands", [128, 2, 3 * CC, W])
        self.gen = [ph.ps(f"gen{j}", [128, OPB, 3 * CC]) for j in range(4)]
        self.out = [ph.ps(f"conv{j}", [128, 4, rows]) for j in range(4)]
        self.built = ph.sem("gen_bank_built")
        self.copied = ph.sem("gen_bank_copied")
        self.filled = ph.sem("conv_bank_filled", credit=1)
        self.free = ph.sem("conv_bank_free")

    def build(self, pe, t, f):
        pe.wait_ge(self.copied, t * self.FILLS + f + 1)
        for o in range(OPB):
            start = W - (f * OPB + o)
            last = self.nc.tensor.matmul(self.gen[f % 4][:, o, :], self.table[:, start:start + W],
                                         self.taps[:, :, bass.ds(t * CC, CC)], start=True, stop=True)
        last.then_inc(self.built, 1)

    def convolve(self, pe, s, b, image, c0):
        nc = self.nc
        pe.wait_ge(self.copied, s * self.FILLS + self.FILLS + 4)
        for q in range(self.CONVS):
            pe.wait_ge(self.free, s * self.CONVS + q + 1)
            for c in range(4):
                for a in range(3):
                    last = nc.tensor.matmul(
                        self.out[q][:, c, :], self.mats[:, b, a * CC + 4 * q + c, :],
                        image[:, a:a + self.rows, bass.ds(c0 + 4 * q + c, 1)].rearrange("p n o -> p (n o)"),
                        start=(a == 0), stop=(a == 2))
                if c == 3:
                    last.then_inc(self.filled, 1)
                self.build(pe, s + 1, 4 * q + c)

    def copy_matrices(self, eng, copy, t, b):
        for f in range(self.FILLS):
            eng.wait_ge(self.built, t * self.FILLS + f + 1)
            if f == 0:
                eng.wait_ge(self.filled, (t - 1) * self.CONVS + 1)
            copy(self.mats[:, b, :, f * OPB:(f + 1) * OPB].rearrange("p c o -> p o c"), self.gen[f % 4][:])\
                .then_inc(self.copied, 1)


def convolve_gate(nc, name, table, taps, f_dram, image, H):
    with Phase(nc, name) as ph:
        bands = Bands(nc, ph, table, taps, H)
        landed, border, gated, done = (ph.sem(s) for s in ("rows_landed", "border_zeroed", "gelu_done", "product_done"))
        pairs = CH // CC // 2
        n_half = CH // CC
        with nc.Block() as block:
            @block.sync
            def _(sp):
                for s in range(H // SLAB):
                    sp.dma_start(image[:, 1 + s * SLAB:1 + (s + 1) * SLAB, :],
                                 f_dram[s * SLAB:(s + 1) * SLAB].rearrange("h w c -> w h c")).then_inc(landed, 16)
                sp.wait_ge(landed, 16 * (H // SLAB))

            @block.gpsimd
            def _(pool):
                nc.gpsimd.memset(image[:, 0, :], 0.0).then_inc(border, 1)
                nc.gpsimd.memset(image[:, H + 1, :], 0.0).then_inc(border, 1)

            @block.tensor
            def _(pe):
                for f in range(bands.FILLS):
                    bands.build(pe, 0, f)
                pe.wait_ge(border, 2)
                pe.wait_ge(landed, 16 * (H // SLAB))
                with pe.Fori(0, 2 * pairs) as i:
                    for b in range(2):
                        bands.convolve(pe, i * 2 + b, b, image, (i * 2 + b) * CC)

            @block.vector
            def _(dve):
                dve.sem_inc(bands.copied, 4)
                for f in range(bands.FILLS):
                    dve.wait_ge(bands.built, f + 1)
                    nc.vector.tensor_copy(bands.mats[:, 0, :, f * OPB:(f + 1) * OPB].rearrange("p c o -> p o c"),
                                          bands.gen[f % 4][:]).then_inc(bands.copied, 1)
                with dve.Fori(0, pairs) as i:
                    for b in range(2):
                        bands.copy_matrices(dve, nc.vector.tensor_copy, i * 2 + b + 1, 1 - b)
                dve.wait_ge(gated, n_half * bands.CONVS)
                with dve.Fori(0, pairs) as i:
                    for b in range(2):
                        for q in range(bands.CONVS):
                            s = i * 2 + b + n_half
                            dve.wait_ge(bands.filled, s * bands.CONVS + q + 2)
                            g = image[:, 1:1 + H, bass.ds((i * 2 + b) * CC + 4 * q, 4)].rearrange("p n c -> p c n")
                            nc.vector.tensor_tensor(g, bands.out[q][:], g, ALU.mult).then_inc(bands.free, 1)

            @block.scalar
            def _(act):
                act.sem_inc(bands.free, 4)
                with act.Fori(0, pairs) as i:
                    for b in range(2):
                        for q in range(bands.CONVS):
                            s = i * 2 + b
                            act.wait_ge(bands.filled, s * bands.CONVS + q + 2)
                            g = image[:, 1:1 + H, bass.ds(s * CC + 4 * q, 4)].rearrange("p n c -> p c n")
                            ins = nc.scalar.activation(g, bands.out[q][:], ACT.Gelu)
                            ins.then_inc(gated, 1)
                            act.wait_ge(gated, s * bands.CONVS + q + 1)
                            act.sem_inc(bands.free, 1)
                act.wait_ge(bands.copied, 4 + (n_half + 1) * bands.FILLS)
                with act.Fori(0, pairs) as i:
                    for b in range(2):
                        bands.copy_matrices(act, nc.scalar.copy, i * 2 + b + n_half + 1, 1 - b)


def project_out(nc, name, image, ident, wo_dram, x, x_new, stats, H):
    R = 4
    tiles = H // R
    with Phase(nc, name) as ph:
        wo = ph.sb("wo", [CH, C])
        gs = ph.sb("gs", [128, 2, R, CH])
        gt = ph.sb("gt", [CH, 2, R * W])
        xt = ph.sb("xt", [CH, 2, 2, R * W])
        xo = ph.sb("xo", [CH, 2, 2, R * W])
        tp = [ph.ps(f"tp{b}", [CH, R * W]) for b in range(2)]
        po = [[ph.ps(f"po{b}{k}", [CH, R * W]) for k in range(2)] for b in range(2)]
        wl, staged, counted, passed = (ph.sem(s) for s in ("weights_landed", "rows_staged", "sum_counted", "waits_passed"))
        turned, copied, product, added = (ph.sem(s, credit=1) for s in ("rows_turned", "turned_copied", "product_done", "sum_done"))
        landed = [ph.sem(f"x_landed{b}") for b in range(2)]
        stored = [ph.sem(f"x_stored{b}", credit=16) for b in range(2)]
        with nc.Block() as block:
            @block.sync
            def _(sp):
                sp.dma_start(wo[:], wo_dram).then_inc(wl, 16)
                with sp.Fori(0, tiles // 2) as i:
                    for b in range(2):
                        s = i * 2 + b
                        sp.wait_ge(added, s * 2 + 1)
                        sp.dma_start(xt[:, b], x[:, :, bass.ds(s * R * W, R * W)]).then_inc(landed[b], 16)
                sp.wait_ge(wl, 16)

            @block.gpsimd
            def _(pool):
                with pool.Fori(0, tiles // 2) as i:
                    for b in range(2):
                        s = i * 2 + b
                        hold(pool, turned, s * R + 1 if b == 0 else s * R - R + 1, passed)
                        nc.gpsimd.tensor_copy(gs[:, b], image[:, bass.ds(s * R + 1, R), 0:CH]).then_inc(staged, 1)

            @block.tensor
            def _(pe):
                pe.wait_ge(wl, 16)
                with pe.Fori(0, tiles // 2) as i:
                    for b in range(2):
                        s = i * 2 + b
                        pe.wait_ge(staged, s + 1)
                        pe.wait_ge(copied, i * 2 + 1)
                        for r in range(R):
                            nc.tensor.transpose(tp[b][:, r * W:(r + 1) * W], gs[:, b, r, :], ident[:]).then_inc(turned, 1)
                    for b in range(2):
                        s = i * 2 + b
                        pe.wait_ge(copied, s + 2)
                        pe.wait_ge(added, i * 4 + 1)
                        for k in range(2):
                            nc.tensor.matmul(po[b][k][:], wo[:, k * CH:(k + 1) * CH], gt[:, b, :], start=True, stop=True)\
                                .then_inc(product, 1)

            @block.scalar
            def _(act):
                with act.Fori(0, tiles // 2) as i:
                    for b in range(2):
                        s = i * 2 + b
                        act.wait_ge(turned, s * R + R + 1)
                        act.wait_ge(product, i * 4 + 1)
                        nc.scalar.copy(gt[:, b, :], tp[b][:]).then_inc(copied, 1)
                        if b == 1:
                            for bb in range(2):
                                ss = i * 2 + bb
                                act.wait_ge(added, ss * 2 + 3)
                                act.dma_start(x_new[:, :, bass.ds(ss * R * W, R * W)], xo[:, bb]).then_inc(stored[bb], 16)
                for b in range(2):
                    act.wait_ge(stored[b], 16 * (tiles // 2) + 16)

            @block.vector
            def _(dve):
                with dve.Fori(0, tiles // 2) as i:
                    for b in range(2):
                        s = i * 2 + b
                        dve.wait_ge(landed[b], i * 16 + 16)
                        dve.wait_ge(stored[b], i * 16 + 16)
                        for k in range(2):
                            dve.wait_ge(product, s * 2 + k + 2)
                            nc.vector.tensor_tensor(xo[:, b, k, :], po[b][k][:], xt[:, b, k, :], ALU.add).then_inc(added, 1)
                        dve.wait_ge(added, s * 2 + 3)
                        for k in range(2):
                            nc.vector.bn_stats(stats[:, k, bass.ds(s, 1), :], xo[:, b, k, :]).then_inc(counted, 1)


def patch_layer(nc, name, x, x_new, p, k, f_dram, stats_in, stats, H):
    T = H * W
    with nc.sbuf_tensor(f"{name}_taps", [96, 3, C + CC], BF16) as taps:
        with nc.sbuf_tensor(f"{name}_wf", [CH + 1, 2, C], F32) as wf, \
                nc.sbuf_tensor(f"{name}_t", [128, H // SLAB * NPC, C], F32) as t:
            fold_norm(nc, f"{name}_fold", stats_in, k["group_mean"], p["w_in"], wf, C)
            split_taps(nc, f"{name}_split", p["w_dw"], taps, C + CC)
            project_patches(nc, f"{name}_in", x, wf, t, H)
            filter_patches(nc, f"{name}_filter", t, k["patch_table"], p["fft_filter"], f_dram, H)
        with nc.sbuf_tensor(f"{name}_image", [128, H + 2, C], F32) as image:
            with nc.sbuf_tensor(f"{name}_table", [96, 2 * W], BF16) as table:
                load_constants(nc, f"{name}_table", [(table, k["band_table"])])
                convolve_gate(nc, f"{name}_conv", table, taps, f_dram, image, H)
            project_out(nc, f"{name}_out", image, k["ident"], p["w_out"], x, x_new, stats, H)


def spread(ap, n):
    return ap.unsqueeze(2).broadcast_to([ap.shape[0], ap.shape[1], n])


def project_rows(nc, name, x, wf, dt_raw, proj, H):
    slabs = H // SLAB
    R = 4
    tiles = SLAB // R
    O = CONV_DIM + N_HEADS
    with Phase(nc, name) as ph:
        xt = ph.sb("xt", [CH + 1, 2, 2, SLAB, W])
        stage = ph.sb("stage", [128, 4, R, O])
        banks = [ph.ps(f"row{j}", [128, O]) for j in range(8)]
        landed = [ph.sem(f"slab_landed{b}") for b in range(2)]
        filled = ph.sem("row_projected")
        used = [ph.sem(f"slab_used{b}", credit=1) for b in range(2)]
        copied = [ph.sem("even_rows_copied"), ph.sem("odd_rows_copied")]
        steps = [ph.sem(f"steps_taken{q}", credit=1) for q in range(4)]
        stored = [ph.sem(f"rows_stored{q}", credit=16) for q in range(4)]
        ones, passed = ph.sem("ones_set"), ph.sem("waits_passed")
        with nc.Block() as block:
            @block.sync
            def _(sp):
                with sp.Fori(0, slabs // 2) as i:
                    for b in range(2):
                        sp.wait_ge(used[b], i + 1)
                        sp.dma_start(xt[0:CH, b], x[:, :, bass.ds((i * 2 + b) * SLAB * W, SLAB * W)]
                                     .rearrange("p k (h w) -> p k h w", w=W)).then_inc(landed[b], 16)

            @block.gpsimd
            def _(pool):
                nc.gpsimd.memset(xt[CH:CH + 1], 1.0).then_inc(ones, 1)
                with pool.Fori(0, slabs // 2) as i:
                    for b in range(2):
                        for q in range(tiles):
                            rows = (i * 2 + b) * (SLAB // 2) + (q + 1) * (R // 2)
                            for par in range(2):
                                hold(pool, copied[par], rows + 4, passed)
                            h0 = (i * 2 + b) * SLAB + q * R
                            nc.gpsimd.tensor_copy(dt_raw[:, bass.ds(h0, R), :], stage[:, q, :, CONV_DIM:O]).then_inc(steps[q], 1)

            @block.tensor
            def _(pe):
                pe.wait_ge(ones, 1)
                with pe.Fori(0, slabs // 2) as i:
                    for b in range(2):
                        pe.wait_ge(landed[b], i * 16 + 16)
                        for r in range(SLAB):
                            pe.wait_ge(copied[r % 2], (i * 2 + b) * (SLAB // 2) + r // 2 + 1)
                            for k in range(2):
                                rows = CH + 1 - k
                                last = nc.tensor.matmul(banks[r % 8][:], xt[0:rows, b, k, r, :], wf[0:rows, k, D_INNER:D_INNER + O],
                                                        start=(k == 0), stop=(k == 1))
                            last.then_inc(filled, 1)
                        pe.wait_ge(filled, (i * 2 + b) * SLAB + SLAB)
                        pe.sem_inc(used[b], 1)

            def evacuate(eng, copy, par, store=None):
                eng.sem_inc(copied[par], 4)
                with eng.Fori(0, slabs // 2) as i:
                    for b in range(2):
                        for r in range(par, SLAB, 2):
                            if r % R == par:
                                eng.wait_ge(stored[r // R], (i * 2 + b) * 16 + 16)
                                eng.wait_ge(steps[r // R], i * 2 + b + 1)
                            eng.wait_ge(filled, (i * 2 + b) * SLAB + r + 1)
                            copy(stage[:, r // R, r % R, :], banks[r % 8][:]).then_inc(copied[par], 1)
                            if store and r % R == R - 1:
                                for p2 in range(2):
                                    eng.wait_ge(copied[p2], (i * 2 + b) * (SLAB // 2) + (r + 1) // 2 + 4)
                                store(r // R, (i * 2 + b) * SLAB + r + 1 - R)

            @block.vector
            def _(dve):
                evacuate(dve, nc.vector.tensor_copy, 0)

            @block.scalar
            def _(act):
                def store(q, h0):
                    act.dma_start(proj[bass.ds(h0, R)].rearrange("h w c -> w h c"), stage[:, q, :, 0:CONV_DIM])\
                        .then_inc(stored[q], 16)

                evacuate(act, nc.scalar.copy, 1, store)
                for q in range(4):
                    act.wait_ge(stored[q], 16 * slabs + 16)


def convolve_rows(nc, name, table, taps, bias_dram, proj, xbc, H):
    CG = CONV_DIM // 4
    slabs = H // SLAB
    chunks = CG // CC
    with Phase(nc, name) as ph:
        bias = ph.sb("bias", [128, CONV_DIM])
        image = [ph.sb(f"image{g}", [128, H + 2, CG]) for g in range(2)]
        bands = Bands(nc, ph, table, taps, H)
        landed = [ph.sem(f"rows_landed{g}") for g in range(2)]
        stored = [ph.sem(f"rows_stored{g}", credit=16) for g in range(2)]
        passed = ph.sem("waits_passed")
        border, activated, bias_landed = ph.sem("border_zeroed"), ph.sem("silu_done"), ph.sem("bias_landed")

        def chunk_steps(eng, i, g, step):
            base = i * 2 * chunks + g * chunks
            with eng.Fori(0, chunks // 2) as j:
                for b in range(2):
                    step(base + j * 2 + b, (g + b) % 2, (j * 2 + b) * CC)
            step(base + chunks - 1, g, (chunks - 1) * CC)

        with nc.Block() as block:
            @block.sync
            def _(sp):
                sp.dma_start(bias[:], bias_dram).then_inc(bias_landed, 16)
                with sp.Fori(0, 2) as i:
                    for g in range(2):
                        sp.wait_ge(stored[g], i * 16 * slabs + 16)
                        for s in range(slabs):
                            sp.dma_start(image[g][:, 1 + s * SLAB:1 + (s + 1) * SLAB, :],
                                         proj[s * SLAB:(s + 1) * SLAB, :, bass.ds((i * 2 + g) * CG, CG)]
                                         .rearrange("h w c -> w h c")).then_inc(landed[g], 16)

            @block.gpsimd
            def _(pool):
                for g in range(2):
                    nc.gpsimd.memset(image[g][:, 0, :], 0.0).then_inc(border, 1)
                    nc.gpsimd.memset(image[g][:, H + 1, :], 0.0).then_inc(border, 1)

            @block.tensor
            def _(pe):
                for f in range(bands.FILLS):
                    bands.build(pe, 0, f)
                pe.wait_ge(border, 4)
                with pe.Fori(0, 2) as i:
                    for g in range(2):
                        hold(pe, landed[g], (i + 1) * 16 * slabs, passed)
                        chunk_steps(pe, i, g, lambda s, b, c0: bands.convolve(pe, s, b, image[g], c0))

            @block.vector
            def _(dve):
                dve.sem_inc(bands.copied, 4)
                for f in range(bands.FILLS):
                    dve.wait_ge(bands.built, f + 1)
                    nc.vector.tensor_copy(bands.mats[:, 0, :, f * OPB:(f + 1) * OPB].rearrange("p c o -> p o c"),
                                          bands.gen[f % 4][:]).then_inc(bands.copied, 1)
                with dve.Fori(0, 2) as i:
                    for g in range(2):
                        chunk_steps(dve, i, g, lambda s, b, c0: bands.copy_matrices(dve, nc.vector.tensor_copy, s + 1, 1 - b))

            @block.scalar
            def _(act):
                act.wait_ge(bias_landed, 16)
                act.sem_inc(bands.free, 4)

                def silu(i, g, s, c0):
                    for q in range(bands.CONVS):
                        act.wait_ge(bands.filled, s * bands.CONVS + q + 2)
                        for c in range(4):
                            ch = c0 + 4 * q + c
                            last = nc.scalar.activation(
                                image[g][:, 1:1 + H, bass.ds(ch, 1)].rearrange("p n o -> p (n o)"), bands.out[q][:, c, :], ACT.Silu,
                                bias=bias[:, bass.ds((i * 2 + g) * CG + ch, 1)])
                            last.then_inc(activated, 1)
                        act.wait_ge(activated, s * CC + 4 * q + 4)
                        act.sem_inc(bands.free, 1)

                with act.Fori(0, 2) as i:
                    for g in range(2):
                        chunk_steps(act, i, g, lambda s, b, c0: silu(i, g, s, c0))
                        act.wait_ge(activated, (i * 2 + g + 1) * CG)
                        for s in range(slabs):
                            act.dma_start(xbc[s * SLAB:(s + 1) * SLAB, :, bass.ds((i * 2 + g) * CG, CG)].rearrange("h w c -> w h c"),
                                          image[g][:, 1 + s * SLAB:1 + (s + 1) * SLAB, :]).then_inc(stored[g], 16)
                for g in range(2):
                    act.wait_ge(stored[g], 32 * slabs + 16)


SCAL = 5


def step_sizes(nc, name, dt_raw, a_log_dram, tri, ones, scal, end_decay, H):
    N = H * N_HEADS
    B = (N + BANK - 1) // BANK
    with Phase(nc, name) as ph:
        alog = ph.sb("alog", [128, N_HEADS])
        ea = ph.sb("ea", [128, N_HEADS])
        t = {n: ph.sb(n, [128, N]) for n in ("abs", "e", "u", "l", "relu", "dt", "da", "cs", "rest", "erest")}
        cp = [ph.ps(f"cum{j}", [128, BANK]) for j in range(B)]
        tp = [ph.ps(f"tot{j}", [128, BANK]) for j in range(B)]
        landed, a, v, p = ph.sem("landed"), ph.sem("act_step"), ph.sem("dve_step"), ph.sem("sums_done")
        raw = dt_raw[:].rearrange("p h n -> p (h n)")

        def part(j):
            return slice(j * BANK, min(N, (j + 1) * BANK))

        def field(n):
            return scal[:, :, n, :]

        def rows(tile):
            return tile[:].rearrange("p (h n) -> p h n", n=N_HEADS)

        with nc.Block() as block:
            @block.sync
            def _(sp):
                sp.dma_start(alog[:], a_log_dram).then_inc(landed, 16)

            @block.scalar
            def _(act):
                nc.scalar.activation(t["abs"][:], raw, ACT.Abs).then_inc(a, 1)
                act.wait_ge(a, 1)
                nc.scalar.activation(t["e"][:], t["abs"][:], ACT.Exp, scale=-1.0).then_inc(a, 1)
                act.wait_ge(landed, 16)
                nc.scalar.activation(ea[:], alog[:], ACT.Exp).then_inc(a, 1)
                act.wait_ge(v, 1)
                nc.scalar.activation(t["l"][:], t["u"][:], ACT.Ln).then_inc(a, 1)
                act.wait_ge(v, 6)
                nc.scalar.activation(field(2), rows(t["cs"]), ACT.Exp).then_inc(a, 1)
                act.wait_ge(v, 8)
                nc.scalar.activation(t["erest"][:], t["rest"][:], ACT.Exp).then_inc(a, 1)
                for j in range(B):
                    nc.scalar.activation(end_decay[:].rearrange("p h n -> p (h n)")[:, part(j)],
                                         tp[j][:, 0:part(j).stop - part(j).start], ACT.Exp).then_inc(a, 1)

            @block.vector
            def _(dve):
                dve.wait_ge(a, 2)
                nc.vector.tensor_scalar(t["u"][:], t["e"][:], 1.0, None, ALU.add).then_inc(v, 1)
                nc.vector.tensor_scalar(t["relu"][:], raw, 0.0, None, ALU.max).then_inc(v, 1)
                dve.wait_ge(a, 4)
                dve.wait_ge(v, 2)
                nc.vector.tensor_tensor(t["dt"][:], t["relu"][:], t["l"][:], ALU.add).then_inc(v, 1)
                dve.wait_ge(v, 3)
                nc.vector.tensor_copy(field(3), rows(t["dt"])).then_inc(v, 1)
                for_heads = ea[:].unsqueeze(1).broadcast_to([128, H, N_HEADS])
                nc.vector.scalar_tensor_tensor(out=rows(t["da"]), in0=rows(t["dt"]), scalar=-1.0, in1=for_heads,
                                               op0=ALU.mult, op1=ALU.mult).then_inc(v, 1)
                dve.wait_ge(p, 1)
                for j in range(B):
                    last = nc.vector.tensor_copy(t["cs"][:, part(j)], cp[j][:, 0:part(j).stop - part(j).start])
                last.then_inc(v, 1)
                dve.wait_ge(v, 6)
                nc.vector.tensor_scalar(field(1), rows(t["cs"]), -1.0, None, ALU.mult).then_inc(v, 1)
                for j in range(B):
                    last = nc.vector.tensor_tensor(t["rest"][:, part(j)], tp[j][:, 0:part(j).stop - part(j).start],
                                                   t["cs"][:, part(j)], ALU.subtract)
                last.then_inc(v, 1)
                nc.vector.tensor_copy(field(0), rows(t["da"])).then_inc(v, 1)
                dve.wait_ge(a, 6)
                nc.vector.tensor_tensor(field(4), rows(t["erest"]), rows(t["dt"]), ALU.mult).then_inc(v, 1)

            @block.tensor
            def _(pe):
                pe.wait_ge(v, 5)
                for j in range(B):
                    n = part(j).stop - part(j).start
                    nc.tensor.matmul(cp[j][:, 0:n], tri[:], t["da"][:, part(j)], start=True, stop=True)
                    last = nc.tensor.matmul(tp[j][:, 0:n], ones[:], t["da"][:, part(j)], start=True, stop=True)
                last.then_inc(p, 1)


def scan_rows(nc, name, p, k, x, x_new, wf, xbc, scal, end_decay, tri, stats, H):
    with Phase(nc, name) as ph:
        ident, ident_bf, mask = k["ident"], k["ident_bf_sb"], k["mask_sb"]
        wo = ph.sb("wo", [128, 3, C])
        nw = ph.sb("norm_w", [128, 3])
        nb = ph.sb("norm_b", [128, 3])
        dskip = ph.sb("dskip", [128, N_HEADS])
        half = ph.sb("minus_half", [128, 1])
        xc = ph.sb("xc", [128, 2, CONV_DIM])
        xr = ph.sb("xr", [CH + 1, 2, 2, W])
        rs = ph.sb("row_scalars", [128, 2, SCAL, N_HEADS])
        xdt = ph.sb("xdt", [128, 2, D_INNER])
        xw = ph.sb("xw", [128, 2, D_INNER])
        xd = ph.sb("xd", [128, 2, D_INNER])
        bct = ph.sb("bct", [N_STATE, 2, 2, W])
        decay = ph.sb("decay", [128, 2, N_HEADS, W])
        att = ph.sb("att", [128, 2, N_HEADS, W])
        state = ph.sb("state", [N_STATE, D_INNER])
        faded = ph.sb("faded", [N_STATE, D_INNER])
        inter = ph.sb("inter", [128, 2, D_INNER])
        y = ph.sb("y", [128, 2, D_INNER])
        yn = ph.sb("yn", [128, 2, D_INNER])
        st6 = ph.sb("st6", [128, 2, 6])
        mv = ph.sb("mv", [128, 2, 2])
        rstd = ph.sb("rstd", [128, 2, 1])
        yw = ph.sb("yw", [128, 3, W])
        yz = ph.sb("yz", [128, 3, W])
        xo = ph.sb("xo", [CH, 2, 2, W])
        cum = [ph.ps(f"cum{j}", [128, 4, W]) for j in range(2)]
        p_bcg = ph.ps("bcg", [128, 3, W])
        p_y = ph.ps("y_intra", [128, D_INNER])
        p_i = ph.ps("y_inter", [128, D_INNER])
        p_t = ph.ps("turned", [128, 3, W])
        p_z = ph.ps("gate", [128, 3, W])
        p_o = ph.ps("projected", [CH, 2, W])
        exp_done, att_done = ph.sem("exp_done", credit=8), ph.sem("att_done", credit=3)
        inter_done, yi_done, skipped = (ph.sem(n, credit=1) for n in ("inter_done", "intra_done", "skip_added"))
        (ready, bc_turned, bc_copied, cum_done, scores, xs_ready, rs_ready, scaled, y_done, counted, agg, rstd_done, yn_done,
         turned, yw_done, z_done, yz_done, o_done, xo_done, st_done, state_ready, faded_done, stats_done) = (
            ph.sem(n) for n in (
                "constants_ready", "bc_turned", "bc_copied", "cum_done", "scores_done", "xs_ready", "row_scalars_ready",
                "inter_scaled", "y_done", "y_counted", "y_aggregated", "rstd_done", "yn_done", "yn_turned", "yw_done", "z_done",
                "yz_done", "projected", "xo_done", "chunk_state_done", "state_ready", "state_faded", "xo_counted"))
        passed = ph.sem("waits_passed")
        xc_landed = [ph.sem(f"xc_landed{b}") for b in range(2)]
        xr_landed = [ph.sem(f"xr_landed{b}") for b in range(2)]
        stored = [ph.sem(f"xo_stored{b}", credit=16) for b in range(2)]
        consts = [(wo, p["out_proj_w"]), (nw, p["norm_w"]), (nb, p["norm_b"]),
                  (dskip, p["D"])]
        CONST = 16 * len(consts) + 2

        def rows_of(eng, row):
            for r in range(2):
                row(r, r, 0, r > 0, False)
            with eng.Fori(1, H // 2) as i:
                for b in range(2):
                    row(i * 2 + b, b, i, True, True)

        with nc.Block() as block:
            @block.sync
            def _(sp):
                for tile, source in consts:
                    sp.dma_start(tile[:], source).then_inc(ready, 16)

                def store(r, b):
                    hold(sp, xo_done, (r + 1) * 2, passed)
                    sp.dma_start(x_new[:, :, bass.ds(r * W, W)], xo[:, b]).then_inc(stored[b], 16)

                def row(r, b, i, tail, storing):
                    if storing:
                        hold(sp, st_done, r - 1, passed)
                        hold(sp, xs_ready, 3 * (r - 1), passed)
                    sp.dma_start(xc[:, b, :], xbc[bass.ds(r, 1)].rearrange("h w c -> (h w) c")).then_inc(xc_landed[b], 16)
                    if storing:
                        hold(sp, xo_done, 2 * (r - 1), passed)
                    sp.dma_start(xr[0:CH, b], x[:, :, bass.ds(r * W, W)]).then_inc(xr_landed[b], 16)
                    if storing:
                        store(r - 2, b)

                rows_of(sp, row)
                for r in (H - 2, H - 1):
                    store(r, r % 2)
                for b in range(2):
                    sp.wait_ge(stored[b], 16 * (H // 2) + 16)

            @block.gpsimd
            def _(pool):
                nc.gpsimd.memset(half[:], -0.5).then_inc(ready, 1)
                nc.gpsimd.memset(state[:], 0.0).then_inc(state_ready, 1)
                pool.wait_ge(ready, CONST)

                def row(r, b, i, tail, storing):
                    if tail and storing:
                        pool.wait_ge(exp_done, 8 + 12 * (r - 1))
                        pool.wait_ge(scaled, r - 1)
                        pool.wait_ge(yi_done, 1 + r - 1)
                        hold(pool, st_done, r - 1, passed)
                    nc.gpsimd.tensor_copy(rs[:, b], scal[:, bass.ds(r, 1)].rearrange("p o s n -> p (o s) n")).then_inc(rs_ready, 1)
                    pool.wait_ge(rs_ready, r + 1)
                    pool.wait_ge(xc_landed[b], i * 16 + 16)
                    heads = xc[:, b, 0:D_INNER].rearrange("p (n d) -> p n d", d=HEAD)
                    for out, by in ((xdt, rs[:, b, 3, :]), (xw, rs[:, b, 4, :]), (xd, dskip[:])):
                        nc.gpsimd.tensor_tensor(out[:, b].rearrange("p (n d) -> p n d", d=HEAD), heads, spread(by, HEAD),
                                                ALU.mult).then_inc(xs_ready, 1)
                    pool.wait_ge(state_ready, r + 1)
                    if tail:
                        pool.wait_ge(state_ready, r + 1)
                    ed = end_decay[0:N_STATE, bass.ds(r, 1), :].rearrange("p o n -> p (o n)")
                    nc.gpsimd.tensor_tensor(faded[:].rearrange("p (n d) -> p n d", d=HEAD),
                                            state[:].rearrange("p (n d) -> p n d", d=HEAD), spread(ed, HEAD), ALU.mult)\
                        .then_inc(faded_done, 1)
                    pool.wait_ge(scaled, r + 1)
                    pool.wait_ge(xs_ready, 3 * r + 3)
                    nc.gpsimd.tensor_tensor(inter[:, b], inter[:, b], xd[:, b], ALU.add).then_inc(skipped, 1)
                    hold(pool, agg, r + 1, passed)
                    nc.gpsimd.tensor_scalar(rstd[:, b], mv[:, b, 1:2], LN_EPS, None, ALU.add).then_inc(rstd_done, 1)
                    pool.wait_ge(rstd_done, 2 * r + 1)
                    nc.gpsimd.tensor_tensor(rstd[:, b], rstd[:, b], half[:], ALU.pow).then_inc(rstd_done, 1)

                rows_of(pool, row)

            @block.tensor
            def _(pe):
                def cumulative(b, g, bank, q):
                    pe.wait_ge(exp_done, 4 * q + 4)
                    for h in range(4):
                        nc.tensor.matmul(cum[bank][:, h, :], rs[:, b, 0, 4 * g + h:4 * g + h + 1].broadcast_to([128, 128]),
                                         tri[:], start=True, stop=False, skip_group_check=True)
                        last = nc.tensor.matmul(cum[bank][:, h, :], ident_bf[:], mask[:], start=False, stop=True, skip_group_check=True)
                    last.then_inc(cum_done, 1)

                def tail_gate(r, b, i):
                    pe.wait_ge(xr_landed[b], i * 16 + 16)
                    pe.wait_ge(yz_done, r)
                    for m in range(3):
                        for kk in range(2):
                            rows = CH + 1 - kk
                            last = nc.tensor.matmul(p_z[:, m, :], wf[0:rows, kk, m * 128:(m + 1) * 128], xr[0:rows, b, kk, :],
                                                    start=(kk == 0), stop=(kk == 1))
                    last.then_inc(z_done, 1)

                def tail_out(r, b):
                    pe.wait_ge(yn_done, r + 1)
                    pe.wait_ge(yw_done, 3 * r)
                    for m in range(3):
                        last = nc.tensor.transpose(p_t[:, m, :], yn[:, b, m * 128:(m + 1) * 128], ident[:])
                    last.then_inc(turned, 1)
                    pe.wait_ge(yz_done, r + 1)
                    pe.wait_ge(xo_done, 2 * r)
                    for kk in range(2):
                        for m in range(3):
                            last = nc.tensor.matmul(p_o[:, kk, :], wo[:, m, kk * CH:(kk + 1) * CH], yz[:, m, :],
                                                    start=(m == 0), stop=(m == 2))
                    last.then_inc(o_done, 1)

                def row(r, b, i, tail, storing):
                    pe.wait_ge(xc_landed[b], i * 16 + 16)
                    pe.wait_ge(att_done, 3 * r + 3)
                    for n in range(2):
                        last = nc.tensor.transpose(p_bcg[0:N_STATE, n, :],
                                                   xc[:, b, D_INNER + n * N_STATE:D_INNER + (n + 1) * N_STATE], ident[:])
                    last.then_inc(bc_turned, 1)
                    pe.wait_ge(rs_ready, r + 1)
                    for g in range(3):
                        cumulative(b, g, (b + g) % 2, r * 3 + g)
                        if g == 0:
                            pe.wait_ge(bc_copied, r + 1)
                            nc.tensor.matmul(p_bcg[:, 2, :], bct[:, b, 0, :], bct[:, b, 1, :], start=True, stop=True)\
                                .then_inc(scores, 1)
                        if g == 1 and tail:
                            tail_gate(r - 1, 1 - b, i if b == 1 else i - 1)
                    if tail:
                        tail_out(r - 1, 1 - b)
                    pe.wait_ge(state_ready, r + 1)
                    nc.tensor.matmul(p_i[:], bct[:, b, 1, :], state[:], start=True, stop=True).then_inc(inter_done, 1)
                    pe.wait_ge(xs_ready, 3 * r + 3)
                    pe.wait_ge(y_done, r)
                    for h in range(N_HEADS):
                        if h % 4 == 0:
                            pe.wait_ge(att_done, 3 * r + 4 + h // 4)
                        last = nc.tensor.matmul(p_y[:, h * HEAD:(h + 1) * HEAD], att[:, b, h, :], xdt[:, b, h * HEAD:(h + 1) * HEAD],
                                                start=True, stop=True)
                    last.then_inc(yi_done, 1)
                    pe.wait_ge(scaled, r + 1)
                    nc.tensor.matmul(p_i[0:N_STATE], xc[:, b, D_INNER:D_INNER + N_STATE], xw[:, b], start=True, stop=True)\
                        .then_inc(st_done, 1)

                pe.wait_ge(ready, CONST)
                rows_of(pe, row)
                tail_gate(H - 1, 1, H // 2 - 1)
                tail_out(H - 1, 1)

            @block.scalar
            def _(act):
                act.wait_ge(ready, CONST)

                def tail_scale(r):
                    act.wait_ge(turned, r + 1)
                    act.wait_ge(yz_done, r)
                    for m in range(3):
                        nc.scalar.activation(yw[:, m, :], p_t[:, m, :], ACT.Identity, bias=nb[:, m:m + 1], scale=nw[:, m:m + 1])\
                            .then_inc(yw_done, 1)

                def row(r, b, i, tail, storing):
                    act.wait_ge(bc_turned, r + 1)
                    act.wait_ge(inter_done, r)
                    nc.scalar.copy(bct[:, b], p_bcg[0:N_STATE, 0:2, :]).then_inc(bc_copied, 1)
                    act.wait_ge(att_done, 3 * r)
                    act.wait_ge(rs_ready, r + 1)
                    for g in range(3):
                        act.wait_ge(cum_done, 3 * r + g + 1)
                        for h in range(4):
                            nc.scalar.activation(decay[:, b, 4 * g + h, :], cum[(b + g) % 2][:, h, :], ACT.Exp,
                                                 bias=rs[:, b, 1, 4 * g + h:4 * g + h + 1]).then_inc(exp_done, 1)
                    if tail:
                        tail_scale(r - 1)

                rows_of(act, row)
                tail_scale(H - 1)

            @block.vector
            def _(dve):
                nc.vector.memset(xr[CH:CH + 1], 1.0).then_inc(ready, 1)
                dve.wait_ge(ready, CONST)

                def tail_gate(r, b, i):
                    dve.wait_ge(yw_done, 3 * r + 3)
                    dve.wait_ge(z_done, r + 1)
                    dve.wait_ge(o_done, r)
                    nc.vector.tensor_tensor(yz[:], p_z[:], yw[:], ALU.mult).then_inc(yz_done, 1)

                def tail_add(r, b, i):
                    dve.wait_ge(o_done, r + 1)
                    dve.wait_ge(xr_landed[b], i * 16 + 16)
                    dve.wait_ge(stored[b], i * 16 + 16)
                    for kk in range(2):
                        nc.vector.tensor_tensor(xo[:, b, kk, :], p_o[:, kk, :], xr[0:CH, b, kk, :], ALU.add).then_inc(xo_done, 1)
                    dve.wait_ge(xo_done, 2 * r + 2)
                    for kk in range(2):
                        nc.vector.bn_stats(stats[:, kk, bass.ds(r, 1), :], xo[:, b, kk, :]).then_inc(stats_done, 1)

                def row(r, b, i, tail, storing):
                    dve.wait_ge(scores, r + 1)
                    dve.wait_ge(yi_done, r)
                    for g in range(3):
                        dve.wait_ge(exp_done, 8 + 12 * r + 4 * g + 4)
                        nc.vector.tensor_tensor(att[:, b, 4 * g:4 * g + 4, :], decay[:, b, 4 * g:4 * g + 4, :],
                                                p_bcg[:, 2, :].unsqueeze(1).broadcast_to([128, 4, W]), ALU.mult).then_inc(att_done, 1)
                    if tail:
                        tail_gate(r - 1, 1 - b, i if b == 1 else i - 1)
                    dve.wait_ge(inter_done, r + 2)
                    dve.wait_ge(skipped, r)
                    dve.wait_ge(y_done, r)
                    nc.vector.tensor_tensor(inter[:, b].rearrange("p (n d) -> p n d", d=HEAD),
                                            p_i[:].rearrange("p (n d) -> p n d", d=HEAD), spread(rs[:, b, 2, :], HEAD),
                                            ALU.mult).then_inc(scaled, 1)
                    if tail:
                        tail_add(r - 1, 1 - b, i if b == 1 else i - 1)
                    dve.wait_ge(st_done, r + 1)
                    dve.wait_ge(faded_done, r + 1)
                    nc.vector.tensor_tensor(state[:], p_i[0:N_STATE], faded[:], ALU.add).then_inc(state_ready, 1)
                    dve.wait_ge(yi_done, r + 2)
                    dve.wait_ge(skipped, r + 2)
                    nc.vector.tensor_tensor(y[:, b], p_y[:], inter[:, b], ALU.add).then_inc(y_done, 1)
                    dve.wait_ge(y_done, r + 1)
                    nc.vector.bn_stats(st6[:, b], y[:, b]).then_inc(counted, 1)
                    hold(dve, counted, r + 1, passed)
                    nc.vector.bn_aggr(mv[:, b], st6[:, b]).then_inc(agg, 1)
                    dve.wait_ge(rstd_done, 2 * r + 2)
                    dve.wait_ge(turned, r - 1 if storing else 0)
                    nc.vector.tensor_scalar(yn[:, b], y[:, b], mv[:, b, 0:1], rstd[:, b], ALU.subtract, ALU.mult).then_inc(yn_done, 1)

                rows_of(dve, row)
                tail_gate(H - 1, 1, H // 2 - 1)
                tail_add(H - 1, 1, H // 2 - 1)


def mamba_layer(nc, name, x, x_new, p, k, proj, xbc, stats, H):
    with nc.sbuf_tensor(f"{name}_wf", [CH + 1, 2, 2 * D_INNER + 2 * N_STATE + N_HEADS], F32) as wf, \
            nc.sbuf_tensor(f"{name}_dt", [128, H, N_HEADS], F32) as dt_raw:
        fold_norm(nc, f"{name}_fold", stats[0], k["group_mean"], p["in_proj_w"], wf, 2 * D_INNER + 2 * N_STATE + N_HEADS,
                  extra=p["dt_bias"])
        project_rows(nc, f"{name}_in", x, wf, dt_raw, proj, H)
        with nc.sbuf_tensor(f"{name}_taps", [96, 3, CONV_DIM + CC], BF16) as taps, \
                nc.sbuf_tensor(f"{name}_table", [96, 2 * W], BF16) as table:
            load_constants(nc, f"{name}_table", [(table, k["band_table"])])
            split_taps(nc, f"{name}_split", p["conv_w"], taps, CONV_DIM + CC)
            convolve_rows(nc, f"{name}_conv", table, taps, p["conv_b"], proj, xbc, H)
        with nc.sbuf_tensor(f"{name}_scal", [128, H, SCAL, N_HEADS], F32) as scal, \
                nc.sbuf_tensor(f"{name}_end", [128, H, N_HEADS], F32) as end_decay, \
                nc.sbuf_tensor(f"{name}_tri", [128, 128], F32) as tri, nc.sbuf_tensor(f"{name}_ones", [128, 128], F32) as ones, \
                nc.sbuf_tensor(f"{name}_ident", [128, 128], BF16) as ident_bf, nc.sbuf_tensor(f"{name}_mask", [128, 128], BF16) as mask:
            load_constants(nc, f"{name}_tri", [(tri, k["tri"]), (ones, k["ones"]), (ident_bf, k["ident_dram"]), (mask, k["mask"])])
            k = {**k, "ident_bf_sb": ident_bf, "mask_sb": mask}
            step_sizes(nc, f"{name}_steps", dt_raw, p["A_log"], tri, ones, scal, end_decay, H)
            scan_rows(nc, f"{name}_scan", p, k, x, x_new, wf, xbc, scal, end_decay, tri, stats[1], H)


def tables():
    ident = np.eye(128, dtype=np.float32)
    c = np.arange(CH)
    per = C // GROUPS
    group_mean = (c[:, None] // per == c[None, :] // per).astype(np.float32) / per
    u, v = np.divmod(np.arange(NF), PS // 2 + 1)
    oh, ow = np.divmod(np.arange(PS * PS), PS)
    dh = oh[:, None] - oh[None, :]
    dw = ow[:, None] - ow[None, :]
    weight = np.where((v == 0) | (v == PS // 2), 1.0, 2.0) / (PS * PS)
    wave = weight[:, None, None] * np.cos(2 * np.pi * (u[:, None, None] * dh + v[:, None, None] * dw) / PS)
    patch_table = np.concatenate([wave, wave], axis=2).astype(np.float32)
    band = np.zeros((96, 2 * W), np.float32)
    for part in range(3):
        for b in range(3):
            band[32 * part + b, W - 1 + b] = 1.0
    tri = np.triu(np.ones((128, 128), np.float32))
    return {"ident": ident, "group_mean": group_mean, "patch_table": patch_table, "band_table": band,
            "tri": tri, "ones": np.ones((128, 128), np.float32),
            "mask": (tri - 1) * np.float32(2.0 ** 100)}


def build(nc, a, out, H, layers):
    T = H * W
    proj = nc.dram_tensor("projected_rows", [H, W, CONV_DIM], F32, kind="Internal").ap()
    xbc = nc.dram_tensor("convolved_rows", [H, W, CONV_DIM], F32, kind="Internal").ap()
    f_dram = nc.dram_tensor("filtered_rows", [H, W, C], F32, kind="Internal").ap()
    x = a["x"].rearrange("(k p) t -> p k t", k=2)
    between = [nc.dram_tensor(f"x_after_{n}", [C, T], F32, kind="Internal").ap() for n in range(len(layers) - 1)]
    images = [x] + [t.rearrange("(k p) t -> p k t", k=2) for t in between + [out]]
    with nc.sbuf_tensor("stats", [CH, 2, T // BANK, 6], F32) as stats, nc.sbuf_tensor("row_stats", [CH, 2, H, 6], F32) as row_stats, \
            nc.sbuf_tensor("ident_sb", [128, 128], F32) as ident, nc.sbuf_tensor("group_mean_sb", [CH, CH], F32) as gm:
        load_constants(nc, "constants", [(ident, a["ident"]), (gm, a["group_mean"])])
        k = {**a, "ident": ident, "ident_dram": a["ident"], "group_mean": gm}
        input_stats(nc, x, stats, H)
        current = stats
        for n, layer in enumerate(layers):
            p = {key[3:]: v for key, v in a.items() if key.startswith(f"L{layer}_")}
            if layer == 1:
                mamba_layer(nc, f"l{layer}", images[n], images[n + 1], p, k, proj, xbc, (current, row_stats), H)
                current = row_stats
            else:
                patch_layer(nc, f"l{layer}", images[n], images[n + 1], p, k, f_dram, current, stats, H)
                current = stats


def lay_out(inputs, layers):
    a = {"x": np.asarray(inputs["x"]).reshape(C, -1), **tables()}
    for n in layers:
        g = {key[8:]: np.asarray(v) for key, v in inputs.items() if key.startswith(f"L{n}_conv_")}
        if n == 1:
            O = g["in_proj_w"].shape[0]
            a["L1_in_proj_w"] = g["in_proj_w"].T.reshape(2, CH, O).transpose(1, 0, 2)
            a["L1_conv_w"] = g["conv_w"].reshape(CONV_DIM, 3, 3).transpose(2, 1, 0)
            a["L1_conv_b"] = np.tile(g["conv_b"], (128, 1))
            a["L1_dt_bias"] = g["dt_bias"].reshape(1, N_HEADS)
            a["L1_A_log"] = np.tile(g["A_log"], (128, 1))
            a["L1_D"] = np.tile(g["D"], (128, 1))
            a["L1_norm_w"] = g["norm_w"].reshape(3, 128).T
            a["L1_norm_b"] = g["norm_b"].reshape(3, 128).T
            a["L1_out_proj_w"] = g["out_proj_w"].T.reshape(3, 128, C).transpose(1, 0, 2)
        else:
            a[f"L{n}_w_in"] = g["w_in"].T.reshape(2, CH, C).transpose(1, 0, 2)
            a[f"L{n}_fft_filter"] = g["fft_filter"].reshape(C, NF).T
            a[f"L{n}_w_dw"] = g["w_dw"].reshape(C, 3, 3).transpose(2, 1, 0)
            a[f"L{n}_w_out"] = g["w_out"].T
    return {key: np.ascontiguousarray(v) for key, v in a.items()}


def kernel(**inputs):
    import concourse.bacc as bacc
    from concourse.bass_utils import run_bass_kernel_spmd
    shape = np.asarray(inputs["x"]).shape
    arrays = lay_out(inputs, LAYERS)
    nc = bacc.Bacc("TRN2", target_bir_lowering=False, num_devices=1)
    a = {n: nc.dram_tensor(n, v.shape, mybir.dt.from_np(v.dtype), kind="ExternalInput").ap() for n, v in arrays.items()}
    out = nc.dram_tensor("out", (C, shape[2] * shape[3]), F32, kind="ExternalOutput").ap()
    build(nc, a, out, shape[2], LAYERS)
    r = run_bass_kernel_spmd(nc, [arrays], core_ids=[0])
    return r.results[0]["out"].reshape(shape)
```

```python
from contextlib import ExitStack

import numpy as np
import concourse.bass as bass
from concourse import mybir

ALU = mybir.AluOpType
ACT = mybir.ActivationFunctionType
F32 = mybir.dt.float32
BF16 = mybir.dt.bfloat16

W = 128
C = 192
CH = C // 2
PS = 8
SLAB = 2 * PS
NPC = W // PS
NF = PS * (PS // 2 + 1)
GROUPS = 32
GN_EPS = 1e-5

D_INNER = 384
N_STATE = 32
N_HEADS = 12
HEAD = 32
CONV_DIM = D_INNER + 2 * N_STATE
LN_EPS = 1e-5

LAYERS = (0, 1, 2, 3)

CC = 16
BANK = 512
OPB = 8


class Phase:

    def __init__(self, nc, name):
        self.nc, self.name = nc, name

    def __enter__(self):
        self.stack = ExitStack()
        self.sems = []
        return self

    def sb(self, name, shape, dt=F32):
        return self.stack.enter_context(self.nc.sbuf_tensor(f"{self.name}_{name}", shape, dt))

    def ps(self, name, shape, dt=F32):
        return self.stack.enter_context(self.nc.psum_tensor(f"{self.name}_{name}", shape, dt))

    def sem(self, name, credit=0):
        s = self.nc.alloc_semaphore(name=f"{self.name}_{name}")
        self.sems.append(s)
        if credit:
            self.nc.sync.sem_inc(s, credit)
        return s

    def __exit__(self, *exc):
        if exc[0] is None:
            self.nc.clear_and_free_semaphores(self.sems)
            self.nc.all_engine_barrier()
        self.stack.close()


def hold(eng, sem, value, passed):
    eng.wait_ge(sem, value)
    eng.sem_inc(passed, 1)


def load_constants(nc, name, pairs):
    with Phase(nc, name) as ph:
        landed, rounded = ph.sem("landed"), ph.sem("rounded")
        exact = [tile if tile.dtype == F32 else ph.sb(f"exact{n}", list(tile.shape)) for n, (tile, _) in enumerate(pairs)]
        with nc.Block() as block:
            @block.sync
            def _(sp):
                for target, (_, source) in zip(exact, pairs):
                    sp.dma_start(target[:], source).then_inc(landed, 16)
                sp.wait_ge(landed, 16 * len(pairs))

            @block.vector
            def _(dve):
                dve.wait_ge(landed, 16 * len(pairs))
                for target, (tile, _) in zip(exact, pairs):
                    if tile.dtype != F32:
                        nc.vector.tensor_copy(tile[:], target[:]).then_inc(rounded, 1)


def input_stats(nc, x, stats, H):
    slabs = H // SLAB
    n = SLAB * W // BANK
    with Phase(nc, "instat") as ph:
        xt = ph.sb("xt", [CH, 2, 2, SLAB * W])
        landed = [ph.sem(f"slab_landed{b}") for b in range(2)]
        counted = [ph.sem(f"slab_counted{b}", credit=1) for b in range(2)]
        with nc.Block() as block:
            @block.sync
            def _(sp):
                with sp.Fori(0, slabs // 2) as i:
                    for b in range(2):
                        sp.wait_ge(counted[b], i * 2 * n + 1)
                        sp.dma_start(xt[:, b], x[:, :, bass.ds((i * 2 + b) * SLAB * W, SLAB * W)]).then_inc(landed[b], 16)

            @block.vector
            def _(dve):
                with dve.Fori(0, slabs // 2) as i:
                    for b in range(2):
                        dve.wait_ge(landed[b], i * 16 + 16)
                        for k in range(2):
                            for q in range(n):
                                nc.vector.bn_stats(stats[:, k, bass.ds((i * 2 + b) * n + q, 1), :],
                                                   xt[:, b, k, q * BANK:(q + 1) * BANK]).then_inc(counted[b], 1)


def fold_norm(nc, name, stats, group_mean, wT, wf, O, extra=None):
    with Phase(nc, name) as ph:
        raw = ph.sb("raw", [CH, 2, O])
        mv = ph.sb("mv", [CH, 2, 2])
        gm = ph.sb("gm", [CH, 2])
        dev = ph.sb("dev", [CH, 2])
        dev2 = ph.sb("dev2", [CH, 2])
        var = ph.sb("var", [CH, 2])
        vare = ph.sb("vare", [CH, 2])
        std = ph.sb("std", [CH, 2])
        rstd = ph.sb("rstd", [CH, 2])
        negm = ph.sb("negm", [CH, 2, CH + 1])
        xrow = ph.sb("xrow", [CH + 1, 16])
        pm = ph.ps("pm", [CH, BANK])
        pv = ph.ps("pv", [CH, BANK])
        pb = [ph.ps(f"pb{j}", [CH + 1, BANK]) for j in range((O + BANK - 1) // BANK)]
        landed, zero, agg, mean, dv, pvar, sd, r, scaled, bias, d2, done = (ph.sem(s) for s in (
            "weights_landed", "negm_zeroed", "aggregated", "group_mean", "deviation", "group_var",
            "std_ready", "rstd_ready", "weights_scaled", "bias_ready", "square_ready", "done"))
        with nc.Block() as block:
            @block.sync
            def _(sp):
                sp.dma_start(raw[:], wT).then_inc(landed, 16)
                if extra is not None:
                    sp.dma_start(xrow[CH:CH + 1, 0:extra.shape[1]], extra).then_inc(landed, 16)
                sp.wait_ge(landed, 16 if extra is None else 32)

            @block.vector
            def _(dve):
                nc.vector.memset(negm[:], 0.0).then_inc(zero, 1)
                for k in range(2):
                    nc.vector.bn_aggr(mv[:, k, :], stats[:, k]).then_inc(agg, 1)
                dve.wait_ge(mean, 1)
                dve.wait_ge(agg, 2)
                nc.vector.tensor_copy(gm[:], pm[:, 0:2]).then_inc(dv, 1)
                dve.wait_ge(dv, 1)
                nc.vector.tensor_tensor(dev[:], mv[:, :, 0], gm[:], ALU.subtract).then_inc(dv, 1)
                dve.wait_ge(dv, 2)
                nc.vector.tensor_tensor(dev2[:], dev[:], dev[:], ALU.mult).then_inc(dv, 1)
                dve.wait_ge(dv, 3)
                nc.vector.tensor_tensor(var[:], dev2[:], mv[:, :, 1], ALU.add).then_inc(d2, 1)
                dve.wait_ge(pvar, 1)
                nc.vector.tensor_scalar(vare[:], pv[:, 0:2], GN_EPS, None, ALU.add).then_inc(dv, 1)
                dve.wait_ge(sd, 1)
                nc.vector.reciprocal(rstd[:], std[:]).then_inc(r, 1)
                dve.wait_ge(r, 1)
                dve.wait_ge(zero, 1)
                dve.wait_ge(landed, 16 if extra is None else 32)
                for k in range(2):
                    nc.vector.tensor_scalar(wf[0:CH, k, :], raw[:, k, :], rstd[:, k:k + 1], None, ALU.mult).then_inc(scaled, 1)
                    nc.vector.tensor_scalar(negm[:, k, CH:CH + 1], gm[:, k:k + 1], -1.0, None, ALU.mult).then_inc(scaled, 1)
                dve.wait_ge(bias, 1)
                for j in range(len(pb)):
                    n = min(BANK, O - j * BANK)
                    nc.vector.tensor_copy(wf[CH:CH + 1, 0, j * BANK:j * BANK + n], pb[j][CH:CH + 1, 0:n]).then_inc(done, 1)
                if extra is not None:
                    dve.wait_ge(done, len(pb))
                    nc.vector.tensor_tensor(wf[CH:CH + 1, 0, O - N_HEADS:O], wf[CH:CH + 1, 0, O - N_HEADS:O],
                                            xrow[CH:CH + 1, 0:N_HEADS], ALU.add).then_inc(done, 1)

            @block.scalar
            def _(act):
                act.wait_ge(dv, 4)
                nc.scalar.activation(std[:], vare[:], ACT.Sqrt).then_inc(sd, 1)

            @block.tensor
            def _(pe):
                pe.wait_ge(agg, 2)
                nc.tensor.matmul(pm[:, 0:2], group_mean[:], mv[:, :, 0], start=True, stop=True).then_inc(mean, 1)
                pe.wait_ge(d2, 1)
                nc.tensor.matmul(pv[:, 0:2], group_mean[:], var[:], start=True, stop=True).then_inc(pvar, 1)
                pe.wait_ge(scaled, 4)
                for j in range(len(pb)):
                    n = min(BANK, O - j * BANK)
                    for k in range(2):
                        last = nc.tensor.matmul(pb[j][:, 0:n], negm[:, k, :], wf[0:CH, k, j * BANK:j * BANK + n],
                                                start=(k == 0), stop=(k == 1))
                last.then_inc(bias, 1)


def project_patches(nc, name, x, wf, t, H):
    slabs = H // SLAB
    fills = NPC // 2
    half = fills // 2
    with Phase(nc, name) as ph:
        xt = ph.sb("xt", [CH, 2, 2, SLAB, W])
        xp = ph.sb("xp", [CH + 1, 2, 2, NPC, SLAB * PS])
        banks = [ph.ps(f"p{j}", [128, 2, C]) for j in range(fills)]
        landed = [ph.sem(f"slab_landed{b}") for b in range(2)]
        ordered = [ph.sem(f"slab_ordered{b}", credit=1) for b in range(2)]
        filled = [ph.sem(f"banks_filled{b}", credit=1) for b in range(2)]
        free = [ph.sem("even_banks_free"), ph.sem("odd_banks_free")]
        ones, passed = ph.sem("ones_set"), ph.sem("waits_passed")
        with nc.Block() as block:
            @block.sync
            def _(sp):
                with sp.Fori(0, slabs // 2) as i:
                    for b in range(2):
                        sp.wait_ge(ordered[b], i * 2 + 1)
                        sp.dma_start(xt[:, b], x[:, :, bass.ds((i * 2 + b) * SLAB * W, SLAB * W)]
                                     .rearrange("p k (h w) -> p k h w", w=W)).then_inc(landed[b], 16)

            @block.gpsimd
            def _(pool):
                nc.gpsimd.memset(xp[CH:CH + 1], 1.0).then_inc(ones, 1)
                with pool.Fori(0, slabs // 2) as i:
                    for b in range(2):
                        pool.wait_ge(landed[b], i * 16 + 16)
                        hold(pool, filled[b], i * fills + 1, passed)
                        for k in range(2):
                            nc.gpsimd.tensor_copy(xp[0:CH, b, k].rearrange("p pc (h w) -> p pc h w", w=PS),
                                                  xt[:, b, k].rearrange("p h (pc w) -> p pc h w", w=PS)).then_inc(ordered[b], 1)

            @block.tensor
            def _(pe):
                pe.wait_ge(ones, 1)
                with pe.Fori(0, slabs // 2) as i:
                    for b in range(2):
                        pe.wait_ge(ordered[b], i * 2 + 3)
                        for j in range(fills):
                            pe.wait_ge(free[j % 2], (i * 2 + b) * half + j // 2 + 1)
                            for q in range(2):
                                for k in range(2):
                                    rows = CH + 1 - k
                                    last = nc.tensor.matmul(banks[j][:, q, :], xp[0:rows, b, k, 2 * j + q, :], wf[0:rows, k, :],
                                                            start=(k == 0), stop=(k == 1))
                            last.then_inc(filled[b], 1)

            def evacuate(eng, copy, parity):
                eng.sem_inc(free[parity], half)
                with eng.Fori(0, slabs // 2) as i:
                    for b in range(2):
                        for j in range(parity, fills, 2):
                            eng.wait_ge(filled[b], i * fills + j + 2)
                            copy(t[:, bass.ds((i * 2 + b) * NPC + 2 * j, 2), :], banks[j][:]).then_inc(free[parity], 1)

            @block.vector
            def _(dve):
                evacuate(dve, nc.vector.tensor_copy, 0)

            @block.scalar
            def _(act):
                evacuate(act, nc.scalar.copy, 1)


def filter_patches(nc, name, t, patch_table, spectrum, f_dram, H):
    CF = 48
    nblk = H // SLAB * NPC
    npix = PS * PS
    fills = npix // OPB
    with Phase(nc, name) as ph:
        table = ph.sb("cosines", [96, npix, 128])
        spec = ph.sb("spectrum", [96, C])
        wc = ph.sb("matrices", [128, 2, CF, 128])
        gen = [ph.ps(f"gen{j}", [128, OPB, CF]) for j in range(4)]
        fb = [ph.ps(f"out{j}", [128, 4, nblk]) for j in range(4)]
        landed, padded, zeroed, built, genlow, genhigh, filled, frd, fra, stored = (ph.sem(s) for s in (
            "tables_landed", "tables_padded", "matrices_zeroed", "gen_bank_built", "upper_patch_copied", "lower_patch_copied",
            "out_bank_filled", "even_out_banks_free", "odd_out_banks_free", "rows_stored"))
        with nc.Block() as block:
            @block.sync
            def _(sp):
                sp.wait_ge(padded, 2)
                sp.dma_start(table[0:NF], patch_table).then_inc(landed, 16)
                sp.dma_start(spec[0:NF], spectrum).then_inc(landed, 16)
                sp.wait_ge(frd, 2 + C // 8)
                sp.wait_ge(fra, 2 + C // 8)
                for s in range(H // SLAB):
                    for hh in range(PS * 2):
                        dst = f_dram[s * SLAB + hh, :, :].rearrange("(pc ww) c -> ww pc c", ww=PS)
                        sp.dma_start(dst, t[hh * PS:(hh + 1) * PS, s * NPC:(s + 1) * NPC, :]).then_inc(stored, 16)
                sp.wait_ge(stored, 16 * H)

            @block.gpsimd
            def _(pool):
                nc.gpsimd.memset(wc[:], 0.0).then_inc(zeroed, 1)

            @block.tensor
            def _(pe):
                pe.wait_ge(landed, 32)
                with pe.Fori(0, C // CF // 2) as i:
                    for b in range(2):
                        s = i * 2 + b
                        for f in range(fills):
                            pe.wait_ge(genlow, s * fills + f + 1)
                            pe.wait_ge(genhigh, s * fills + f + 1)
                            for o in range(OPB):
                                last = nc.tensor.matmul(gen[f % 4][:, o, :], table[:, f * OPB + o, :],
                                                        spec[:, bass.ds(s * CF, CF)], start=True, stop=True)
                            last.then_inc(built, 1)
                        pe.wait_ge(genlow, s * fills + fills + 4)
                        pe.wait_ge(genhigh, s * fills + fills + 4)
                        for q in range(CF // 4):
                            fr = frd if q % 2 == 0 else fra
                            pe.wait_ge(fr, s * (CF // 8) + q // 2 + 1)
                            for c in range(4):
                                last = nc.tensor.matmul(fb[q % 4][:, c, :], wc[:, b, 4 * q + c, :],
                                                        t[:, :, bass.ds(s * CF + 4 * q + c, 1)].rearrange("p n o -> p (n o)"),
                                                        start=True, stop=True)
                            last.then_inc(filled, 1)

            def evacuate(eng, copy, lo, copied, free, parity):
                eng.sem_inc(copied, 4)
                eng.sem_inc(free, 2)
                eng.wait_ge(zeroed, 1)
                with eng.Fori(0, C // CF // 2) as i:
                    for b in range(2):
                        s = i * 2 + b
                        for f in range(fills):
                            eng.wait_ge(built, s * fills + f + 1)
                            copy(wc[lo:lo + 64, b, :, lo + f * OPB:lo + (f + 1) * OPB].rearrange("p c o -> p o c"),
                                 gen[f % 4][lo:lo + 64]).then_inc(copied, 1)
                        for q in range(parity, CF // 4, 2):
                            eng.wait_ge(filled, s * (CF // 4) + q + 1)
                            copy(t[:, :, bass.ds(s * CF + 4 * q, 4)].rearrange("p n c -> p c n"), fb[q % 4][:]).then_inc(free, 1)

            @block.vector
            def _(dve):
                nc.vector.memset(table[:], 0.0).then_inc(padded, 1)
                nc.vector.memset(spec[:], 0.0).then_inc(padded, 1)
                evacuate(dve, nc.vector.tensor_copy, 0, genlow, frd, 0)

            @block.scalar
            def _(act):
                evacuate(act, nc.scalar.copy, 64, genhigh, fra, 1)


def split_taps(nc, name, taps_dram, taps, n):
    with Phase(nc, name) as ph:
        raw = ph.sb("raw", [96, 3, n])
        rest = ph.sb("rest", [96, 3, n])
        rest2 = ph.sb("rest2", [96, 3, n])
        hi = ph.sb("hi", [96, 3, n], BF16)
        mid = ph.sb("mid", [96, 3, n], BF16)
        zeroed, landed, step = ph.sem("zeroed"), ph.sem("taps_landed"), ph.sem("step")
        cols = taps_dram.shape[2]
        with nc.Block() as block:
            @block.sync
            def _(sp):
                sp.wait_ge(zeroed, 1)
                for part in range(3):
                    sp.dma_start(raw[32 * part:32 * part + 3, :, 0:cols], taps_dram).then_inc(landed, 16)
                sp.wait_ge(landed, 48)

            @block.vector
            def _(dve):
                nc.vector.memset(raw[:], 0.0).then_inc(zeroed, 1)
                dve.wait_ge(landed, 48)
                nc.vector.tensor_copy(hi[:], raw[:]).then_inc(step, 1)
                dve.wait_ge(step, 1)
                nc.vector.tensor_tensor(rest[:], raw[:], hi[:], ALU.subtract).then_inc(step, 1)
                dve.wait_ge(step, 2)
                nc.vector.tensor_copy(mid[:], rest[:]).then_inc(step, 1)
                dve.wait_ge(step, 3)
                nc.vector.tensor_tensor(rest2[:], rest[:], mid[:], ALU.subtract).then_inc(step, 1)
                dve.wait_ge(step, 4)
                nc.vector.tensor_copy(taps[0:32], hi[0:32]).then_inc(step, 1)
                nc.vector.tensor_copy(taps[32:64], mid[32:64]).then_inc(step, 1)
                nc.vector.tensor_copy(taps[64:96], rest2[64:96]).then_inc(step, 1)


class Bands:
    FILLS = W // OPB
    CONVS = CC // 4

    def __init__(self, nc, ph, table, taps, rows):
        self.nc, self.table, self.taps, self.rows = nc, table, taps, rows
        self.mats = ph.sb("bands", [128, 2, 3 * CC, W])
        self.gen = [ph.ps(f"gen{j}", [128, OPB, 3 * CC]) for j in range(4)]
        self.out = [ph.ps(f"conv{j}", [128, 4, rows]) for j in range(4)]
        self.built = ph.sem("gen_bank_built")
        self.copied = ph.sem("gen_bank_copied")
        self.filled = ph.sem("conv_bank_filled", credit=1)
        self.free = ph.sem("conv_bank_free")

    def build(self, pe, t, f):
        pe.wait_ge(self.copied, t * self.FILLS + f + 1)
        for o in range(OPB):
            start = W - (f * OPB + o)
            last = self.nc.tensor.matmul(self.gen[f % 4][:, o, :], self.table[:, start:start + W],
                                         self.taps[:, :, bass.ds(t * CC, CC)], start=True, stop=True)
        last.then_inc(self.built, 1)

    def convolve(self, pe, s, b, image, c0):
        nc = self.nc
        pe.wait_ge(self.copied, s * self.FILLS + self.FILLS + 4)
        for q in range(self.CONVS):
            pe.wait_ge(self.free, s * self.CONVS + q + 1)
            for c in range(4):
                for a in range(3):
                    last = nc.tensor.matmul(
                        self.out[q][:, c, :], self.mats[:, b, a * CC + 4 * q + c, :],
                        image[:, a:a + self.rows, bass.ds(c0 + 4 * q + c, 1)].rearrange("p n o -> p (n o)"),
                        start=(a == 0), stop=(a == 2))
                if c == 3:
                    last.then_inc(self.filled, 1)
                self.build(pe, s + 1, 4 * q + c)

    def copy_matrices(self, eng, copy, t, b):
        for f in range(self.FILLS):
            eng.wait_ge(self.built, t * self.FILLS + f + 1)
            if f == 0:
                eng.wait_ge(self.filled, (t - 1) * self.CONVS + 1)
            copy(self.mats[:, b, :, f * OPB:(f + 1) * OPB].rearrange("p c o -> p o c"), self.gen[f % 4][:])\
                .then_inc(self.copied, 1)


def convolve_gate(nc, name, table, taps, f_dram, image, H):
    with Phase(nc, name) as ph:
        bands = Bands(nc, ph, table, taps, H)
        landed, border, gated, done = (ph.sem(s) for s in ("rows_landed", "border_zeroed", "gelu_done", "product_done"))
        pairs = CH // CC // 2
        n_half = CH // CC
        with nc.Block() as block:
            @block.sync
            def _(sp):
                for s in range(H // SLAB):
                    sp.dma_start(image[:, 1 + s * SLAB:1 + (s + 1) * SLAB, :],
                                 f_dram[s * SLAB:(s + 1) * SLAB].rearrange("h w c -> w h c")).then_inc(landed, 16)
                sp.wait_ge(landed, 16 * (H // SLAB))

            @block.gpsimd
            def _(pool):
                nc.gpsimd.memset(image[:, 0, :], 0.0).then_inc(border, 1)
                nc.gpsimd.memset(image[:, H + 1, :], 0.0).then_inc(border, 1)

            @block.tensor
            def _(pe):
                for f in range(bands.FILLS):
                    bands.build(pe, 0, f)
                pe.wait_ge(border, 2)
                pe.wait_ge(landed, 16 * (H // SLAB))
                with pe.Fori(0, 2 * pairs) as i:
                    for b in range(2):
                        bands.convolve(pe, i * 2 + b, b, image, (i * 2 + b) * CC)

            @block.vector
            def _(dve):
                dve.sem_inc(bands.copied, 4)
                for f in range(bands.FILLS):
                    dve.wait_ge(bands.built, f + 1)
                    nc.vector.tensor_copy(bands.mats[:, 0, :, f * OPB:(f + 1) * OPB].rearrange("p c o -> p o c"),
                                          bands.gen[f % 4][:]).then_inc(bands.copied, 1)
                with dve.Fori(0, pairs) as i:
                    for b in range(2):
                        bands.copy_matrices(dve, nc.vector.tensor_copy, i * 2 + b + 1, 1 - b)
                dve.wait_ge(gated, n_half * bands.CONVS)
                with dve.Fori(0, pairs) as i:
                    for b in range(2):
                        for q in range(bands.CONVS):
                            s = i * 2 + b + n_half
                            dve.wait_ge(bands.filled, s * bands.CONVS + q + 2)
                            g = image[:, 1:1 + H, bass.ds((i * 2 + b) * CC + 4 * q, 4)].rearrange("p n c -> p c n")
                            nc.vector.tensor_tensor(g, bands.out[q][:], g, ALU.mult).then_inc(bands.free, 1)

            @block.scalar
            def _(act):
                act.sem_inc(bands.free, 4)
                with act.Fori(0, pairs) as i:
                    for b in range(2):
                        for q in range(bands.CONVS):
                            s = i * 2 + b
                            act.wait_ge(bands.filled, s * bands.CONVS + q + 2)
                            g = image[:, 1:1 + H, bass.ds(s * CC + 4 * q, 4)].rearrange("p n c -> p c n")
                            ins = nc.scalar.activation(g, bands.out[q][:], ACT.Gelu)
                            ins.then_inc(gated, 1)
                            act.wait_ge(gated, s * bands.CONVS + q + 1)
                            act.sem_inc(bands.free, 1)
                act.wait_ge(bands.copied, 4 + (n_half + 1) * bands.FILLS)
                with act.Fori(0, pairs) as i:
                    for b in range(2):
                        bands.copy_matrices(act, nc.scalar.copy, i * 2 + b + n_half + 1, 1 - b)


def project_out(nc, name, image, ident, wo_dram, x, x_new, stats, H):
    R = 4
    tiles = H // R
    with Phase(nc, name) as ph:
        wo = ph.sb("wo", [CH, C])
        gs = ph.sb("gs", [128, 2, R, CH])
        gt = ph.sb("gt", [CH, 2, R * W])
        xt = ph.sb("xt", [CH, 2, 2, R * W])
        xo = ph.sb("xo", [CH, 2, 2, R * W])
        tp = [ph.ps(f"tp{b}", [CH, R * W]) for b in range(2)]
        po = [[ph.ps(f"po{b}{k}", [CH, R * W]) for k in range(2)] for b in range(2)]
        wl, staged, counted, passed = (ph.sem(s) for s in ("weights_landed", "rows_staged", "sum_counted", "waits_passed"))
        turned, copied, product, added = (ph.sem(s, credit=1) for s in ("rows_turned", "turned_copied", "product_done", "sum_done"))
        landed = [ph.sem(f"x_landed{b}") for b in range(2)]
        stored = [ph.sem(f"x_stored{b}", credit=16) for b in range(2)]
        with nc.Block() as block:
            @block.sync
            def _(sp):
                sp.dma_start(wo[:], wo_dram).then_inc(wl, 16)
                with sp.Fori(0, tiles // 2) as i:
                    for b in range(2):
                        s = i * 2 + b
                        sp.wait_ge(added, s * 2 + 1)
                        sp.dma_start(xt[:, b], x[:, :, bass.ds(s * R * W, R * W)]).then_inc(landed[b], 16)
                sp.wait_ge(wl, 16)

            @block.gpsimd
            def _(pool):
                with pool.Fori(0, tiles // 2) as i:
                    for b in range(2):
                        s = i * 2 + b
                        hold(pool, turned, s * R + 1 if b == 0 else s * R - R + 1, passed)
                        nc.gpsimd.tensor_copy(gs[:, b], image[:, bass.ds(s * R + 1, R), 0:CH]).then_inc(staged, 1)

            @block.tensor
            def _(pe):
                pe.wait_ge(wl, 16)
                with pe.Fori(0, tiles // 2) as i:
                    for b in range(2):
                        s = i * 2 + b
                        pe.wait_ge(staged, s + 1)
                        pe.wait_ge(copied, i * 2 + 1)
                        for r in range(R):
                            nc.tensor.transpose(tp[b][:, r * W:(r + 1) * W], gs[:, b, r, :], ident[:]).then_inc(turned, 1)
                    for b in range(2):
                        s = i * 2 + b
                        pe.wait_ge(copied, s + 2)
                        pe.wait_ge(added, i * 4 + 1)
                        for k in range(2):
                            nc.tensor.matmul(po[b][k][:], wo[:, k * CH:(k + 1) * CH], gt[:, b, :], start=True, stop=True)\
                                .then_inc(product, 1)

            @block.scalar
            def _(act):
                with act.Fori(0, tiles // 2) as i:
                    for b in range(2):
                        s = i * 2 + b
                        act.wait_ge(turned, s * R + R + 1)
                        act.wait_ge(product, i * 4 + 1)
                        nc.scalar.copy(gt[:, b, :], tp[b][:]).then_inc(copied, 1)
                        if b == 1:
                            for bb in range(2):
                                ss = i * 2 + bb
                                act.wait_ge(added, ss * 2 + 3)
                                act.dma_start(x_new[:, :, bass.ds(ss * R * W, R * W)], xo[:, bb]).then_inc(stored[bb], 16)
                for b in range(2):
                    act.wait_ge(stored[b], 16 * (tiles // 2) + 16)

            @block.vector
            def _(dve):
                with dve.Fori(0, tiles // 2) as i:
                    for b in range(2):
                        s = i * 2 + b
                        dve.wait_ge(landed[b], i * 16 + 16)
                        dve.wait_ge(stored[b], i * 16 + 16)
                        for k in range(2):
                            dve.wait_ge(product, s * 2 + k + 2)
                            nc.vector.tensor_tensor(xo[:, b, k, :], po[b][k][:], xt[:, b, k, :], ALU.add).then_inc(added, 1)
                        dve.wait_ge(added, s * 2 + 3)
                        for k in range(2):
                            nc.vector.bn_stats(stats[:, k, bass.ds(s, 1), :], xo[:, b, k, :]).then_inc(counted, 1)


def patch_layer(nc, name, x, x_new, p, k, f_dram, stats_in, stats, H):
    T = H * W
    with nc.sbuf_tensor(f"{name}_taps", [96, 3, C + CC], BF16) as taps:
        with nc.sbuf_tensor(f"{name}_wf", [CH + 1, 2, C], F32) as wf, \
                nc.sbuf_tensor(f"{name}_t", [128, H // SLAB * NPC, C], F32) as t:
            fold_norm(nc, f"{name}_fold", stats_in, k["group_mean"], p["w_in"], wf, C)
            split_taps(nc, f"{name}_split", p["w_dw"], taps, C + CC)
            project_patches(nc, f"{name}_in", x, wf, t, H)
            filter_patches(nc, f"{name}_filter", t, k["patch_table"], p["fft_filter"], f_dram, H)
        with nc.sbuf_tensor(f"{name}_image", [128, H + 2, C], F32) as image:
            with nc.sbuf_tensor(f"{name}_table", [96, 2 * W], BF16) as table:
                load_constants(nc, f"{name}_table", [(table, k["band_table"])])
                convolve_gate(nc, f"{name}_conv", table, taps, f_dram, image, H)
            project_out(nc, f"{name}_out", image, k["ident"], p["w_out"], x, x_new, stats, H)


def spread(ap, n):
    return ap.unsqueeze(2).broadcast_to([ap.shape[0], ap.shape[1], n])


def project_rows(nc, name, x, wf, dt_raw, proj, H):
    slabs = H // SLAB
    R = 4
    tiles = SLAB // R
    O = CONV_DIM + N_HEADS
    with Phase(nc, name) as ph:
        xt = ph.sb("xt", [CH + 1, 2, 2, SLAB, W])
        stage = ph.sb("stage", [128, 4, R, O])
        banks = [ph.ps(f"row{j}", [128, O]) for j in range(8)]
        landed = [ph.sem(f"slab_landed{b}") for b in range(2)]
        filled = ph.sem("row_projected")
        used = [ph.sem(f"slab_used{b}", credit=1) for b in range(2)]
        copied = [ph.sem("even_rows_copied"), ph.sem("odd_rows_copied")]
        steps = [ph.sem(f"steps_taken{q}", credit=1) for q in range(4)]
        stored = [ph.sem(f"rows_stored{q}", credit=16) for q in range(4)]
        ones, passed = ph.sem("ones_set"), ph.sem("waits_passed")
        with nc.Block() as block:
            @block.sync
            def _(sp):
                with sp.Fori(0, slabs // 2) as i:
                    for b in range(2):
                        sp.wait_ge(used[b], i + 1)
                        sp.dma_start(xt[0:CH, b], x[:, :, bass.ds((i * 2 + b) * SLAB * W, SLAB * W)]
                                     .rearrange("p k (h w) -> p k h w", w=W)).then_inc(landed[b], 16)

            @block.gpsimd
            def _(pool):
                nc.gpsimd.memset(xt[CH:CH + 1], 1.0).then_inc(ones, 1)
                with pool.Fori(0, slabs // 2) as i:
                    for b in range(2):
                        for q in range(tiles):
                            rows = (i * 2 + b) * (SLAB // 2) + (q + 1) * (R // 2)
                            for par in range(2):
                                hold(pool, copied[par], rows + 4, passed)
                            h0 = (i * 2 + b) * SLAB + q * R
                            nc.gpsimd.tensor_copy(dt_raw[:, bass.ds(h0, R), :], stage[:, q, :, CONV_DIM:O]).then_inc(steps[q], 1)

            @block.tensor
            def _(pe):
                pe.wait_ge(ones, 1)
                with pe.Fori(0, slabs // 2) as i:
                    for b in range(2):
                        pe.wait_ge(landed[b], i * 16 + 16)
                        for r in range(SLAB):
                            pe.wait_ge(copied[r % 2], (i * 2 + b) * (SLAB // 2) + r // 2 + 1)
                            for k in range(2):
                                rows = CH + 1 - k
                                last = nc.tensor.matmul(banks[r % 8][:], xt[0:rows, b, k, r, :], wf[0:rows, k, D_INNER:D_INNER + O],
                                                        start=(k == 0), stop=(k == 1))
                            last.then_inc(filled, 1)
                        pe.wait_ge(filled, (i * 2 + b) * SLAB + SLAB)
                        pe.sem_inc(used[b], 1)

            def evacuate(eng, copy, par, store=None):
                eng.sem_inc(copied[par], 4)
                with eng.Fori(0, slabs // 2) as i:
                    for b in range(2):
                        for r in range(par, SLAB, 2):
                            if r % R == par:
                                eng.wait_ge(stored[r // R], (i * 2 + b) * 16 + 16)
                                eng.wait_ge(steps[r // R], i * 2 + b + 1)
                            eng.wait_ge(filled, (i * 2 + b) * SLAB + r + 1)
                            copy(stage[:, r // R, r % R, :], banks[r % 8][:]).then_inc(copied[par], 1)
                            if store and r % R == R - 1:
                                for p2 in range(2):
                                    eng.wait_ge(copied[p2], (i * 2 + b) * (SLAB // 2) + (r + 1) // 2 + 4)
                                store(r // R, (i * 2 + b) * SLAB + r + 1 - R)

            @block.vector
            def _(dve):
                evacuate(dve, nc.vector.tensor_copy, 0)

            @block.scalar
            def _(act):
                def store(q, h0):
                    act.dma_start(proj[bass.ds(h0, R)].rearrange("h w c -> w h c"), stage[:, q, :, 0:CONV_DIM])\
                        .then_inc(stored[q], 16)

                evacuate(act, nc.scalar.copy, 1, store)
                for q in range(4):
                    act.wait_ge(stored[q], 16 * slabs + 16)


def convolve_rows(nc, name, table, taps, bias_dram, proj, xbc, H):
    CG = CONV_DIM // 4
    slabs = H // SLAB
    chunks = CG // CC
    with Phase(nc, name) as ph:
        bias = ph.sb("bias", [128, CONV_DIM])
        image = [ph.sb(f"image{g}", [128, H + 2, CG]) for g in range(2)]
        bands = Bands(nc, ph, table, taps, H)
        landed = [ph.sem(f"rows_landed{g}") for g in range(2)]
        stored = [ph.sem(f"rows_stored{g}", credit=16) for g in range(2)]
        passed = ph.sem("waits_passed")
        border, activated, bias_landed = ph.sem("border_zeroed"), ph.sem("silu_done"), ph.sem("bias_landed")

        def chunk_steps(eng, i, g, step):
            base = i * 2 * chunks + g * chunks
            with eng.Fori(0, chunks // 2) as j:
                for b in range(2):
                    step(base + j * 2 + b, (g + b) % 2, (j * 2 + b) * CC)
            step(base + chunks - 1, g, (chunks - 1) * CC)

        with nc.Block() as block:
            @block.sync
            def _(sp):
                sp.dma_start(bias[:], bias_dram).then_inc(bias_landed, 16)
                with sp.Fori(0, 2) as i:
                    for g in range(2):
                        sp.wait_ge(stored[g], i * 16 * slabs + 16)
                        for s in range(slabs):
                            sp.dma_start(image[g][:, 1 + s * SLAB:1 + (s + 1) * SLAB, :],
                                         proj[s * SLAB:(s + 1) * SLAB, :, bass.ds((i * 2 + g) * CG, CG)]
                                         .rearrange("h w c -> w h c")).then_inc(landed[g], 16)

            @block.gpsimd
            def _(pool):
                for g in range(2):
                    nc.gpsimd.memset(image[g][:, 0, :], 0.0).then_inc(border, 1)
                    nc.gpsimd.memset(image[g][:, H + 1, :], 0.0).then_inc(border, 1)

            @block.tensor
            def _(pe):
                for f in range(bands.FILLS):
                    bands.build(pe, 0, f)
                pe.wait_ge(border, 4)
                with pe.Fori(0, 2) as i:
                    for g in range(2):
                        hold(pe, landed[g], (i + 1) * 16 * slabs, passed)
                        chunk_steps(pe, i, g, lambda s, b, c0: bands.convolve(pe, s, b, image[g], c0))

            @block.vector
            def _(dve):
                dve.sem_inc(bands.copied, 4)
                for f in range(bands.FILLS):
                    dve.wait_ge(bands.built, f + 1)
                    nc.vector.tensor_copy(bands.mats[:, 0, :, f * OPB:(f + 1) * OPB].rearrange("p c o -> p o c"),
                                          bands.gen[f % 4][:]).then_inc(bands.copied, 1)
                with dve.Fori(0, 2) as i:
                    for g in range(2):
                        chunk_steps(dve, i, g, lambda s, b, c0: bands.copy_matrices(dve, nc.vector.tensor_copy, s + 1, 1 - b))

            @block.scalar
            def _(act):
                act.wait_ge(bias_landed, 16)
                act.sem_inc(bands.free, 4)

                def silu(i, g, s, c0):
                    for q in range(bands.CONVS):
                        act.wait_ge(bands.filled, s * bands.CONVS + q + 2)
                        for c in range(4):
                            ch = c0 + 4 * q + c
                            last = nc.scalar.activation(
                                image[g][:, 1:1 + H, bass.ds(ch, 1)].rearrange("p n o -> p (n o)"), bands.out[q][:, c, :], ACT.Silu,
                                bias=bias[:, bass.ds((i * 2 + g) * CG + ch, 1)])
                            last.then_inc(activated, 1)
                        act.wait_ge(activated, s * CC + 4 * q + 4)
                        act.sem_inc(bands.free, 1)

                with act.Fori(0, 2) as i:
                    for g in range(2):
                        chunk_steps(act, i, g, lambda s, b, c0: silu(i, g, s, c0))
                        act.wait_ge(activated, (i * 2 + g + 1) * CG)
                        for s in range(slabs):
                            act.dma_start(xbc[s * SLAB:(s + 1) * SLAB, :, bass.ds((i * 2 + g) * CG, CG)].rearrange("h w c -> w h c"),
                                          image[g][:, 1 + s * SLAB:1 + (s + 1) * SLAB, :]).then_inc(stored[g], 16)
                for g in range(2):
                    act.wait_ge(stored[g], 32 * slabs + 16)


SCAL = 4
NEG_CUM, EXP_CUM, DT, TO_END = range(SCAL)


def step_sizes(nc, name, dt_raw, a_log_dram, tri, ones, ident_bf, scal, end_decay, cum_t, H):
    PAIRS = H // 2
    N = H * N_HEADS
    B = (N + BANK - 1) // BANK
    with Phase(nc, name) as ph:
        alog = ph.sb("alog", [128, N_HEADS])
        ea = ph.sb("ea", [128, N_HEADS])
        t = {n: ph.sb(n, [128, N]) for n in ("abs", "e", "u", "l", "relu", "dt", "da", "cs", "rest", "erest", "cum_rest", "cum_rest2")}
        parts = ph.sb("parts", [128, H, 64], BF16)
        tb = [ph.ps(f"turned{j}", [128, 8, W], BF16) for j in range(2)]
        turned, kept = ph.sem("parts_turned"), ph.sem("turned_kept")
        cp = [ph.ps(f"cum{j}", [128, BANK]) for j in range(B)]
        tp = [ph.ps(f"tot{j}", [128, BANK]) for j in range(B)]
        landed, a, v, p = ph.sem("landed"), ph.sem("act_step"), ph.sem("dve_step"), ph.sem("sums_done")
        raw = dt_raw[:].rearrange("p h n -> p (h n)")

        def part(j):
            return slice(j * BANK, min(N, (j + 1) * BANK))

        def field(n):
            return scal[:, :, n, :]

        def rows(tile):
            return tile[:].rearrange("p (h n) -> p h n", n=N_HEADS)

        with nc.Block() as block:
            @block.sync
            def _(sp):
                sp.dma_start(alog[:], a_log_dram).then_inc(landed, 16)

            @block.scalar
            def _(act):
                nc.scalar.activation(t["abs"][:], raw, ACT.Abs).then_inc(a, 1)
                act.wait_ge(a, 1)
                nc.scalar.activation(t["e"][:], t["abs"][:], ACT.Exp, scale=-1.0).then_inc(a, 1)
                act.wait_ge(landed, 16)
                nc.scalar.activation(ea[:], alog[:], ACT.Exp).then_inc(a, 1)
                act.wait_ge(v, 1)
                nc.scalar.activation(t["l"][:], t["u"][:], ACT.Ln).then_inc(a, 1)
                act.wait_ge(v, 6)
                nc.scalar.activation(field(EXP_CUM), rows(t["cs"]), ACT.Exp).then_inc(a, 1)
                act.wait_ge(v, 8)
                nc.scalar.activation(t["erest"][:], t["rest"][:], ACT.Exp).then_inc(a, 1)
                for j in range(B):
                    nc.scalar.activation(end_decay[:].rearrange("p h n -> p (h n)")[:, part(j)],
                                         tp[j][:, 0:part(j).stop - part(j).start], ACT.Exp).then_inc(a, 1)

            @block.vector
            def _(dve):
                dve.wait_ge(a, 2)
                nc.vector.tensor_scalar(t["u"][:], t["e"][:], 1.0, None, ALU.add).then_inc(v, 1)
                nc.vector.tensor_scalar(t["relu"][:], raw, 0.0, None, ALU.max).then_inc(v, 1)
                dve.wait_ge(a, 4)
                dve.wait_ge(v, 2)
                nc.vector.tensor_tensor(t["dt"][:], t["relu"][:], t["l"][:], ALU.add).then_inc(v, 1)
                dve.wait_ge(v, 3)
                nc.vector.tensor_copy(field(DT), rows(t["dt"])).then_inc(v, 1)
                for_heads = ea[:].unsqueeze(1).broadcast_to([128, H, N_HEADS])
                nc.vector.scalar_tensor_tensor(out=rows(t["da"]), in0=rows(t["dt"]), scalar=-1.0, in1=for_heads,
                                               op0=ALU.mult, op1=ALU.mult).then_inc(v, 1)
                dve.wait_ge(p, 1)
                for j in range(B):
                    last = nc.vector.tensor_copy(t["cs"][:, part(j)], cp[j][:, 0:part(j).stop - part(j).start])
                last.then_inc(v, 1)
                dve.wait_ge(v, 6)
                nc.vector.tensor_scalar(field(NEG_CUM), rows(t["cs"]), -1.0, None, ALU.mult).then_inc(v, 1)
                for j in range(B):
                    last = nc.vector.tensor_tensor(t["rest"][:, part(j)], tp[j][:, 0:part(j).stop - part(j).start],
                                                   t["cs"][:, part(j)], ALU.subtract)
                last.then_inc(v, 1)
                part_of = lambda n: parts[:, :, n * N_HEADS:(n + 1) * N_HEADS]
                nc.vector.memset(parts[:], 0.0).then_inc(v, 1)
                dve.wait_ge(v, 9)
                nc.vector.tensor_copy(part_of(0), rows(t["cs"])).then_inc(v, 1)
                dve.wait_ge(v, 10)
                nc.vector.tensor_tensor(rows(t["cum_rest"]), rows(t["cs"]), part_of(0), ALU.subtract).then_inc(v, 1)
                dve.wait_ge(v, 11)
                nc.vector.tensor_copy(part_of(1), rows(t["cum_rest"])).then_inc(v, 1)
                dve.wait_ge(v, 12)
                nc.vector.tensor_tensor(rows(t["cum_rest2"]), rows(t["cum_rest"]), part_of(1), ALU.subtract).then_inc(v, 1)
                dve.wait_ge(v, 13)
                nc.vector.tensor_copy(part_of(2), rows(t["cum_rest2"])).then_inc(v, 1)
                for q in range(PAIRS // 8):
                    dve.wait_ge(turned, q + 1)
                    nc.vector.tensor_copy(cum_t[:, 8 * q:8 * q + 8, :], tb[q % 2][:]).then_inc(kept, 1)
                dve.wait_ge(a, 6)
                nc.vector.tensor_tensor(field(TO_END), rows(t["erest"]), rows(t["dt"]), ALU.mult).then_inc(v, 1)

            @block.tensor
            def _(pe):
                pe.wait_ge(v, 5)
                for j in range(B):
                    n = part(j).stop - part(j).start
                    nc.tensor.matmul(cp[j][:, 0:n], tri[:], t["da"][:, part(j)], start=True, stop=True)
                    last = nc.tensor.matmul(tp[j][:, 0:n], ones[:], t["da"][:, part(j)], start=True, stop=True)
                last.then_inc(p, 1)
                pe.wait_ge(v, 14)
                for q in range(PAIRS // 8):
                    if q >= 2:
                        pe.wait_ge(kept, q - 1)
                    for j in range(8):
                        pair = 8 * q + j
                        last = nc.tensor.transpose(tb[q % 2][:, j, :], parts[:, 2 * pair:2 * pair + 2, :]
                                                   .rearrange("p h n -> p (h n)"), ident_bf[:])
                    last.then_inc(turned, 1)


def scan_rows(nc, name, p, k, x, x_new, wf, xbc, scal, end_decay, cum_t, stats, H):
    U = 4
    with Phase(nc, name) as ph:
        ident, ident_bf, mask, spreads = k["ident"], k["ident_bf_sb"], k["mask_sb"], k["spread_sb"]
        wo = ph.sb("wo", [128, 3, C])
        nw = ph.sb("norm_w", [128, 3])
        nb = ph.sb("norm_b", [128, 3])
        dskip = ph.sb("dskip", [128, N_HEADS])
        half = ph.sb("minus_half", [128, 1])
        pick = ph.sb("pick", [128, 2 * N_HEADS, 128], BF16)
        xc = ph.sb("xc", [128, U, CONV_DIM])
        xr = ph.sb("xr", [CH + 1, U, 2, W])
        rs = ph.sb("row_scalars", [128, U, SCAL, N_HEADS])
        xdt = ph.sb("xdt", [128, 2, D_INNER])
        xw = ph.sb("xw", [128, 2, D_INNER])
        xd = ph.sb("xd", [128, 2, D_INNER])
        bct = ph.sb("bct", [N_STATE, 2, 2, W])
        decay = ph.sb("decay", [128, 2, N_HEADS, W])
        att = ph.sb("att", [128, 2, N_HEADS, W])
        state = ph.sb("state", [N_STATE, D_INNER])
        faded = ph.sb("faded", [N_STATE, D_INNER])
        inter = ph.sb("inter", [128, 2, D_INNER])
        y = ph.sb("y", [128, 2, D_INNER])
        yn = ph.sb("yn", [128, 2, D_INNER])
        st6 = ph.sb("st6", [128, U, 6])
        mv = ph.sb("mv", [128, U, 2])
        rstd = ph.sb("rstd", [128, U, 1])
        yw = ph.sb("yw", [128, 2, 3, W])
        yz = ph.sb("yz", [128, 3, W])
        xo = ph.sb("xo", [CH, U, 2, W])
        cum = [ph.ps(f"cum{j}", [128, 4, W]) for j in range(2)]
        p_bcg = ph.ps("bcg", [128, 3, W])
        p_y = ph.ps("y_intra", [128, D_INNER])
        p_i = ph.ps("y_inter", [128, D_INNER])
        p_t = ph.ps("turned", [128, 3, W])
        p_z = ph.ps("gate", [128, 3, W])
        p_o = ph.ps("projected", [CH, 2, W])
        exp_done, att_done = ph.sem("exp_done", credit=8), ph.sem("att_done", credit=3)
        inter_done, yi_done, st_done, turned, yz_done = (ph.sem(n, credit=1) for n in (
            "inter_done", "intra_done", "chunk_state_done", "yn_turned", "yz_done"))
        (ready, bc_turned, bc_copied, cum_done, scores, xs_ready, rs_ready, scaled, skipped, y_done, counted, agg, rstd_done,
         yn_done, yw_done, z_done, o_done, xo_done, state_ready, faded_done, stats_done, passed) = (
            ph.sem(n) for n in (
                "constants_ready", "bc_turned", "bc_copied", "cum_done", "scores_done", "xs_ready", "row_scalars_ready",
                "inter_scaled", "skip_added", "y_done", "y_counted", "y_aggregated", "rstd_done", "yn_done", "yw_done", "z_done",
                "projected", "xo_done", "state_ready", "state_faded", "xo_counted", "waits_passed"))
        xc_landed = [ph.sem(f"xc_landed{b}") for b in range(U)]
        xr_landed = [ph.sem(f"xr_landed{b}") for b in range(U)]
        stored = [ph.sem(f"xo_stored{b}", credit=16) for b in range(U)]
        consts = [(wo, p["out_proj_w"]), (nw, p["norm_w"]), (nb, p["norm_b"]), (dskip, p["D"])]
        CONST = 16 * len(consts) + 3

        def turns(eng, turn):
            def run(t, b, i):
                def at(lag):
                    r = t - lag
                    if isinstance(t, int) and not 0 <= r < H:
                        return None
                    return r, (b - lag) % U, (i if b >= lag else i - 1)
                turn(at)

            for t in range(U):
                run(t, t, 0)
            with eng.Fori(1, H // U) as i:
                for b in range(U):
                    run(i * U + b, b, i)
            for t in range(H, H + 3):
                run(t, t - H, H // U)

        with nc.Block() as block:
            @block.sync
            def _(sp):
                for tile, source in consts:
                    sp.dma_start(tile[:], source).then_inc(ready, 16)

                def turn(at):
                    if row := at(0):
                        r, b, n = row
                        if not (isinstance(r, int) and r < U):
                            hold(sp, st_done, r - 2, passed)
                            hold(sp, xs_ready, 3 * (r - 3), passed)
                        sp.dma_start(xc[:, b, :], xbc[bass.ds(r, 1)].rearrange("h w c -> (h w) c")).then_inc(xc_landed[b], 16)
                    if row := at(1):
                        r, b, n = row
                        if not (isinstance(r, int) and r < U):
                            hold(sp, xo_done, r - 3, passed)
                        sp.dma_start(xr[0:CH, b], x[:, :, bass.ds(r * W, W)]).then_inc(xr_landed[b], 16)

                def store(r, b):
                    hold(sp, xo_done, r + 1, passed)
                    sp.dma_start(x_new[:, :, bass.ds(r * W, W)], xo[:, b]).then_inc(stored[b], 16)

                def with_store(at):
                    turn(at)
                    row = at(0)
                    if row and not (isinstance(row[0], int) and row[0] < U):
                        store(row[0] - U, row[1])

                turns(sp, with_store)
                for r in range(H - 4, H):
                    store(r, r % U)
                for b in range(U):
                    sp.wait_ge(stored[b], 16 * (H // U) + 16)

            @block.gpsimd
            def _(pool):
                nc.gpsimd.memset(half[:], -0.5).then_inc(ready, 1)
                nc.gpsimd.memset(state[:], 0.0).then_inc(state_ready, 1)
                pool.wait_ge(ready, CONST)

                def by_heads(ap):
                    return ap.rearrange("p (n d) -> p n d", d=HEAD)

                def turn(at):
                    if row := at(0):
                        r, b, n = row
                        if not (isinstance(r, int) and r < U):
                            pool.wait_ge(exp_done, 8 + 12 * (r - 3))
                            hold(pool, scaled, r - 3, passed)
                        nc.gpsimd.tensor_copy(rs[:, b], scal[:, bass.ds(r, 1)].rearrange("p o s n -> p (o s) n")).then_inc(rs_ready, 1)
                    if row := at(1):
                        r, b, n = row
                        pool.wait_ge(state_ready, r + 1)
                        ed = end_decay[0:N_STATE, bass.ds(r, 1), :].rearrange("p o n -> p (o n)")
                        nc.gpsimd.tensor_tensor(by_heads(faded[:]), by_heads(state[:]), spread(ed, HEAD), ALU.mult)\
                            .then_inc(faded_done, 1)
                        pool.wait_ge(scaled, r + 1)
                        pool.wait_ge(xs_ready, 3 * r + 3)
                        nc.gpsimd.tensor_tensor(inter[:, b % 2], inter[:, b % 2], xd[:, b % 2], ALU.add).then_inc(skipped, 1)
                    if row := at(0):
                        r, b, n = row
                        pool.wait_ge(rs_ready, r + 1)
                        pool.wait_ge(xc_landed[b], n * 16 + 16)
                        pool.wait_ge(yi_done, r)
                        pool.wait_ge(st_done, r)
                        if not (isinstance(r, int) and r < 2):
                            pool.wait_ge(skipped, r - 1)
                        heads = by_heads(xc[:, b, 0:D_INNER])
                        for out, by in ((xdt, rs[:, b, DT, :]), (xw, rs[:, b, TO_END, :]), (xd, dskip[:])):
                            nc.gpsimd.tensor_tensor(by_heads(out[:, b % 2]), heads, spread(by, HEAD), ALU.mult).then_inc(xs_ready, 1)
                    if row := at(1):
                        r, b, n = row
                        hold(pool, agg, r + 1, passed)
                        nc.gpsimd.tensor_scalar(rstd[:, b], mv[:, b, 1:2], LN_EPS, None, ALU.add).then_inc(rstd_done, 1)
                        pool.wait_ge(rstd_done, 2 * r + 1)
                        nc.gpsimd.tensor_tensor(rstd[:, b], rstd[:, b], half[:], ALU.pow).then_inc(rstd_done, 1)

                turns(pool, turn)

            @block.tensor
            def _(pe):
                def cumulative(row, g):
                    r, b, n = row
                    q = r * 3 + g
                    pair = cum_t[:, bass.ds(n * 2 + b // 2, 1), :].rearrange("p o w -> p (o w)")
                    bank = cum[(b + g) % 2]
                    pe.wait_ge(exp_done, 4 * q + 4)
                    nc.tensor.matmul(bank[:], ident_bf[:], mask[:].unsqueeze(1).broadcast_to([128, 4, W]), start=True, stop=False)
                    for h in range(4):
                        last = nc.tensor.matmul(bank[:, h, :], pick[:, (b % 2) * N_HEADS + 4 * g + h, :], pair,
                                                start=False, stop=(h == 3))
                    last.then_inc(cum_done, 1)

                def turn(at):
                    row0, row1, row2, row3 = (at(lag) for lag in range(4))
                    if row3:
                        r, b, n = row3
                        pe.wait_ge(xr_landed[b], n * 16 + 16)
                        pe.wait_ge(yz_done, r + 1)
                        for m in range(3):
                            for kk in range(2):
                                rows = CH + 1 - kk
                                last = nc.tensor.matmul(p_z[:, m, :], wf[0:rows, kk, m * 128:(m + 1) * 128], xr[0:rows, b, kk, :],
                                                        start=(kk == 0), stop=(kk == 1))
                        last.then_inc(z_done, 1)
                    if row0:
                        r, b, n = row0
                        pe.wait_ge(xc_landed[b], n * 16 + 16)
                        pe.wait_ge(att_done, 3 * r + 3)
                        for m in range(2):
                            last = nc.tensor.transpose(p_bcg[0:N_STATE, m, :],
                                                       xc[:, b, D_INNER + m * N_STATE:D_INNER + (m + 1) * N_STATE], ident[:])
                        last.then_inc(bc_turned, 1)
                    if row1:
                        r, b, n = row1
                        pe.wait_ge(state_ready, r + 1)
                        nc.tensor.matmul(p_i[:], bct[:, b % 2, 1, :], state[:], start=True, stop=True).then_inc(inter_done, 1)
                    if row0:
                        r, b, n = row0
                        cumulative(row0, 0)
                        cumulative(row0, 1)
                        pe.wait_ge(bc_copied, r + 1)
                        nc.tensor.matmul(p_bcg[:, 2, :], bct[:, b % 2, 0, :], bct[:, b % 2, 1, :], start=True, stop=True)\
                            .then_inc(scores, 1)
                    if row1:
                        r, b, n = row1
                        pe.wait_ge(xs_ready, 3 * r + 3)
                        pe.wait_ge(y_done, r)
                        for h in range(N_HEADS):
                            if h % 4 == 0:
                                pe.wait_ge(att_done, 3 * r + 4 + h // 4)
                            last = nc.tensor.matmul(p_y[:, h * HEAD:(h + 1) * HEAD], att[:, b % 2, h, :],
                                                    xdt[:, b % 2, h * HEAD:(h + 1) * HEAD], start=True, stop=True)
                        last.then_inc(yi_done, 1)
                    if row2:
                        r, b, n = row2
                        pe.wait_ge(yn_done, r + 1)
                        pe.wait_ge(yw_done, 3 * r)
                        for m in range(3):
                            last = nc.tensor.transpose(p_t[:, m, :], yn[:, b % 2, m * 128:(m + 1) * 128], ident[:])
                        last.then_inc(turned, 1)
                    if row0:
                        cumulative(row0, 2)
                    if row1:
                        r, b, n = row1
                        pe.wait_ge(scaled, r + 1)
                        nc.tensor.matmul(p_i[0:N_STATE], xc[:, b, D_INNER:D_INNER + N_STATE], xw[:, b % 2], start=True, stop=True)\
                            .then_inc(st_done, 1)
                    if row3:
                        r, b, n = row3
                        pe.wait_ge(yz_done, r + 2)
                        pe.wait_ge(xo_done, r)
                        for kk in range(2):
                            for m in range(3):
                                last = nc.tensor.matmul(p_o[:, kk, :], wo[:, m, kk * CH:(kk + 1) * CH], yz[:, m, :],
                                                        start=(m == 0), stop=(m == 2))
                        last.then_inc(o_done, 1)

                pe.wait_ge(ready, CONST)
                turns(pe, turn)

            @block.scalar
            def _(act):
                act.wait_ge(ready, CONST)

                def turn(at):
                    row0, row2 = at(0), at(2)
                    if row0:
                        r, b, n = row0
                        act.wait_ge(bc_turned, r + 1)
                        act.wait_ge(inter_done, r)
                        nc.scalar.copy(bct[:, b % 2], p_bcg[0:N_STATE, 0:2, :]).then_inc(bc_copied, 1)
                        act.wait_ge(att_done, 3 * r)
                        act.wait_ge(rs_ready, r + 1)
                        for g in range(3):
                            act.wait_ge(cum_done, 3 * r + g + 1)
                            for h in range(4):
                                nc.scalar.activation(decay[:, b % 2, 4 * g + h, :], cum[(b + g) % 2][:, h, :], ACT.Exp,
                                                     bias=rs[:, b, NEG_CUM, 4 * g + h:4 * g + h + 1]).then_inc(exp_done, 1)
                    if row2:
                        r, b, n = row2
                        act.wait_ge(turned, r + 2)
                        act.wait_ge(yz_done, r)
                        for m in range(3):
                            nc.scalar.activation(yw[:, b % 2, m, :], p_t[:, m, :], ACT.Identity, bias=nb[:, m:m + 1],
                                                 scale=nw[:, m:m + 1]).then_inc(yw_done, 1)

                turns(act, turn)

            @block.vector
            def _(dve):
                nc.vector.memset(xr[CH:CH + 1], 1.0).then_inc(ready, 1)
                nc.vector.tensor_copy(pick[:], spread(spreads[:], 128)).then_inc(ready, 1)
                dve.wait_ge(ready, CONST)

                def attention(r, b, g):
                    dve.wait_ge(exp_done, 8 + 12 * r + 4 * g + 4)
                    nc.vector.tensor_tensor(att[:, b % 2, 4 * g:4 * g + 4, :], decay[:, b % 2, 4 * g:4 * g + 4, :],
                                            p_bcg[:, 2, :].unsqueeze(1).broadcast_to([128, 4, W]), ALU.mult).then_inc(att_done, 1)

                def turn(at):
                    row0, row1, row2, row3 = (at(lag) for lag in range(4))
                    if row2:
                        r, b, n = row2
                        dve.wait_ge(turned, r)
                        dve.wait_ge(rstd_done, 2 * r + 2)
                        nc.vector.tensor_scalar(yn[:, b % 2], y[:, b % 2], mv[:, b, 0:1], rstd[:, b], ALU.subtract, ALU.mult)\
                            .then_inc(yn_done, 1)
                    if row3:
                        r, b, n = row3
                        dve.wait_ge(yw_done, 3 * r + 3)
                        dve.wait_ge(z_done, r + 1)
                        dve.wait_ge(o_done, r)
                        nc.vector.tensor_tensor(yz[:], p_z[:], yw[:, b % 2], ALU.mult).then_inc(yz_done, 1)
                    if row1:
                        r, b, n = row1
                        dve.wait_ge(inter_done, r + 2)
                        dve.wait_ge(y_done, r)
                        nc.vector.tensor_tensor(inter[:, b % 2].rearrange("p (n d) -> p n d", d=HEAD),
                                                p_i[:].rearrange("p (n d) -> p n d", d=HEAD), spread(rs[:, b, EXP_CUM, :], HEAD),
                                                ALU.mult).then_inc(scaled, 1)
                    if row0:
                        r, b, n = row0
                        dve.wait_ge(scores, r + 1)
                        dve.wait_ge(yi_done, r)
                        attention(r, b, 0)
                        attention(r, b, 1)
                    if row1:
                        r, b, n = row1
                        dve.wait_ge(yi_done, r + 2)
                        dve.wait_ge(skipped, r + 1)
                        nc.vector.tensor_tensor(y[:, b % 2], p_y[:], inter[:, b % 2], ALU.add).then_inc(y_done, 1)
                        dve.wait_ge(y_done, r + 1)
                        nc.vector.bn_stats(st6[:, b], y[:, b % 2]).then_inc(counted, 1)
                        hold(dve, counted, r + 1, passed)
                        nc.vector.bn_aggr(mv[:, b], st6[:, b]).then_inc(agg, 1)
                    if row0:
                        attention(row0[0], row0[1], 2)
                    if row1:
                        r, b, n = row1
                        dve.wait_ge(st_done, r + 2)
                        dve.wait_ge(faded_done, r + 1)
                        nc.vector.tensor_tensor(state[:], p_i[0:N_STATE], faded[:], ALU.add).then_inc(state_ready, 1)
                    if row3:
                        r, b, n = row3
                        dve.wait_ge(o_done, r + 1)
                        dve.wait_ge(stored[b], n * 16 + 16)
                        nc.vector.tensor_tensor(xo[:, b], p_o[:], xr[0:CH, b], ALU.add).then_inc(xo_done, 1)
                        dve.wait_ge(xo_done, r + 1)
                        for kk in range(2):
                            nc.vector.bn_stats(stats[:, kk, bass.ds(r, 1), :], xo[:, b, kk, :]).then_inc(stats_done, 1)

                turns(dve, turn)


def mamba_layer(nc, name, x, x_new, p, k, proj, xbc, stats, H):
    with nc.sbuf_tensor(f"{name}_wf", [CH + 1, 2, 2 * D_INNER + 2 * N_STATE + N_HEADS], F32) as wf, \
            nc.sbuf_tensor(f"{name}_dt", [128, H, N_HEADS], F32) as dt_raw:
        fold_norm(nc, f"{name}_fold", stats[0], k["group_mean"], p["in_proj_w"], wf, 2 * D_INNER + 2 * N_STATE + N_HEADS,
                  extra=p["dt_bias"])
        project_rows(nc, f"{name}_in", x, wf, dt_raw, proj, H)
        with nc.sbuf_tensor(f"{name}_taps", [96, 3, CONV_DIM + CC], BF16) as taps, \
                nc.sbuf_tensor(f"{name}_table", [96, 2 * W], BF16) as table:
            load_constants(nc, f"{name}_table", [(table, k["band_table"])])
            split_taps(nc, f"{name}_split", p["conv_w"], taps, CONV_DIM + CC)
            convolve_rows(nc, f"{name}_conv", table, taps, p["conv_b"], proj, xbc, H)
        with nc.sbuf_tensor(f"{name}_scal", [128, H, SCAL, N_HEADS], F32) as scal, \
                nc.sbuf_tensor(f"{name}_cum", [128, H // 2, W], BF16) as cum_t, nc.sbuf_tensor(f"{name}_spread", [128, 2 * N_HEADS], F32) as spreads, \
                nc.sbuf_tensor(f"{name}_end", [128, H, N_HEADS], F32) as end_decay, \
                nc.sbuf_tensor(f"{name}_tri", [128, 128], F32) as tri, nc.sbuf_tensor(f"{name}_ones", [128, 128], F32) as ones, \
                nc.sbuf_tensor(f"{name}_ident", [128, 128], BF16) as ident_bf, nc.sbuf_tensor(f"{name}_mask", [128, 128], BF16) as mask:
            load_constants(nc, f"{name}_tri", [(tri, k["tri"]), (ones, k["ones"]), (ident_bf, k["ident_dram"]), (mask, k["mask"]),
                                                (spreads, k["spread"])])
            k = {**k, "spread_sb": spreads, "mask_sb": mask, "ident_bf_sb": ident_bf}
            step_sizes(nc, f"{name}_steps", dt_raw, p["A_log"], tri, ones, ident_bf, scal, end_decay, cum_t, H)
            scan_rows(nc, f"{name}_scan", p, k, x, x_new, wf, xbc, scal, end_decay, cum_t, stats[1], H)


def tables():
    ident = np.eye(128, dtype=np.float32)
    c = np.arange(CH)
    per = C // GROUPS
    group_mean = (c[:, None] // per == c[None, :] // per).astype(np.float32) / per
    u, v = np.divmod(np.arange(NF), PS // 2 + 1)
    oh, ow = np.divmod(np.arange(PS * PS), PS)
    dh = oh[:, None] - oh[None, :]
    dw = ow[:, None] - ow[None, :]
    weight = np.where((v == 0) | (v == PS // 2), 1.0, 2.0) / (PS * PS)
    wave = weight[:, None, None] * np.cos(2 * np.pi * (u[:, None, None] * dh + v[:, None, None] * dw) / PS)
    patch_table = np.concatenate([wave, wave], axis=2).astype(np.float32)
    band = np.zeros((96, 2 * W), np.float32)
    for part in range(3):
        for b in range(3):
            band[32 * part + b, W - 1 + b] = 1.0
    tri = np.triu(np.ones((128, 128), np.float32))
    spread = np.zeros((128, 2 * N_HEADS), np.float32)
    for b in range(2):
        for head in range(N_HEADS):
            spread[[64 * b + N_HEADS * part + head for part in range(3)], b * N_HEADS + head] = 1.0
    return {"spread": spread, "ident": ident, "group_mean": group_mean, "patch_table": patch_table, "band_table": band,
            "tri": tri, "ones": np.ones((128, 128), np.float32),
            "mask": (tri - 1) * np.float32(2.0 ** 100)}


def build(nc, a, out, H, layers):
    T = H * W
    proj = nc.dram_tensor("projected_rows", [H, W, CONV_DIM], F32, kind="Internal").ap()
    xbc = nc.dram_tensor("convolved_rows", [H, W, CONV_DIM], F32, kind="Internal").ap()
    f_dram = nc.dram_tensor("filtered_rows", [H, W, C], F32, kind="Internal").ap()
    x = a["x"].rearrange("(k p) t -> p k t", k=2)
    between = [nc.dram_tensor(f"x_after_{n}", [C, T], F32, kind="Internal").ap() for n in range(len(layers) - 1)]
    images = [x] + [t.rearrange("(k p) t -> p k t", k=2) for t in between + [out]]
    with nc.sbuf_tensor("stats", [CH, 2, T // BANK, 6], F32) as stats, nc.sbuf_tensor("row_stats", [CH, 2, H, 6], F32) as row_stats, \
            nc.sbuf_tensor("ident_sb", [128, 128], F32) as ident, nc.sbuf_tensor("group_mean_sb", [CH, CH], F32) as gm:
        load_constants(nc, "constants", [(ident, a["ident"]), (gm, a["group_mean"])])
        k = {**a, "ident": ident, "ident_dram": a["ident"], "group_mean": gm}
        input_stats(nc, x, stats, H)
        current = stats
        for n, layer in enumerate(layers):
            p = {key[3:]: v for key, v in a.items() if key.startswith(f"L{layer}_")}
            if layer == 1:
                mamba_layer(nc, f"l{layer}", images[n], images[n + 1], p, k, proj, xbc, (current, row_stats), H)
                current = row_stats
            else:
                patch_layer(nc, f"l{layer}", images[n], images[n + 1], p, k, f_dram, current, stats, H)
                current = stats


def lay_out(inputs, layers):
    a = {"x": np.asarray(inputs["x"]).reshape(C, -1), **tables()}
    for n in layers:
        g = {key[8:]: np.asarray(v) for key, v in inputs.items() if key.startswith(f"L{n}_conv_")}
        if n == 1:
            O = g["in_proj_w"].shape[0]
            a["L1_in_proj_w"] = g["in_proj_w"].T.reshape(2, CH, O).transpose(1, 0, 2)
            a["L1_conv_w"] = g["conv_w"].reshape(CONV_DIM, 3, 3).transpose(2, 1, 0)
            a["L1_conv_b"] = np.tile(g["conv_b"], (128, 1))
            a["L1_dt_bias"] = g["dt_bias"].reshape(1, N_HEADS)
            a["L1_A_log"] = np.tile(g["A_log"], (128, 1))
            a["L1_D"] = np.tile(g["D"], (128, 1))
            a["L1_norm_w"] = g["norm_w"].reshape(3, 128).T
            a["L1_norm_b"] = g["norm_b"].reshape(3, 128).T
            a["L1_out_proj_w"] = g["out_proj_w"].T.reshape(3, 128, C).transpose(1, 0, 2)
        else:
            a[f"L{n}_w_in"] = g["w_in"].T.reshape(2, CH, C).transpose(1, 0, 2)
            a[f"L{n}_fft_filter"] = g["fft_filter"].reshape(C, NF).T
            a[f"L{n}_w_dw"] = g["w_dw"].reshape(C, 3, 3).transpose(2, 1, 0)
            a[f"L{n}_w_out"] = g["w_out"].T
    return {key: np.ascontiguousarray(v) for key, v in a.items()}


def kernel(**inputs):
    import concourse.bacc as bacc
    from concourse.bass_utils import run_bass_kernel_spmd
    shape = np.asarray(inputs["x"]).shape
    arrays = lay_out(inputs, LAYERS)
    nc = bacc.Bacc("TRN2", target_bir_lowering=False, num_devices=1)
    a = {n: nc.dram_tensor(n, v.shape, mybir.dt.from_np(v.dtype), kind="ExternalInput").ap() for n, v in arrays.items()}
    out = nc.dram_tensor("out", (C, shape[2] * shape[3]), F32, kind="ExternalOutput").ap()
    build(nc, a, out, shape[2], LAYERS)
    r = run_bass_kernel_spmd(nc, [arrays], core_ids=[0])
    return r.results[0]["out"].reshape(shape)
```

```python
from contextlib import ExitStack

import numpy as np
import concourse.bass as bass
from concourse import mybir

ALU = mybir.AluOpType
ACT = mybir.ActivationFunctionType
F32 = mybir.dt.float32
BF16 = mybir.dt.bfloat16

W = 128
C = 192
CH = C // 2
PS = 8
SLAB = 2 * PS
NPC = W // PS
NF = PS * (PS // 2 + 1)
CF = 24
GROUPS = 32
GN_EPS = 1e-5

D_INNER = 384
N_STATE = 32
N_HEADS = 12
HEAD = 32
CONV_DIM = D_INNER + 2 * N_STATE
LN_EPS = 1e-5

LAYERS = (0, 1, 2, 3)

CC = 16
BANK = 512
OPB = 8


class Phase:

    def __init__(self, nc, name):
        self.nc, self.name = nc, name

    def __enter__(self):
        self.stack = ExitStack()
        self.sems = []
        return self

    def sb(self, name, shape, dt=F32):
        return self.stack.enter_context(self.nc.sbuf_tensor(f"{self.name}_{name}", shape, dt))

    def ps(self, name, shape, dt=F32):
        return self.stack.enter_context(self.nc.psum_tensor(f"{self.name}_{name}", shape, dt))

    def sem(self, name, credit=0):
        s = self.nc.alloc_semaphore(name=f"{self.name}_{name}")
        self.sems.append(s)
        if credit:
            self.nc.sync.sem_inc(s, credit)
        return s

    def __exit__(self, *exc):
        if exc[0] is None:
            self.nc.clear_and_free_semaphores(self.sems)
            self.nc.all_engine_barrier()
        self.stack.close()


def hold(eng, sem, value, passed):
    eng.wait_ge(sem, value)
    eng.sem_inc(passed, 1)


class Split:

    def __init__(self):
        self.n, self.sources = 0, []

    def place(self, source, rows, pitch, width):
        at = slice(self.n, self.n + width)
        self.n += width
        self.sources.append((source, rows, pitch, at))
        return at

    def taps(self, source, n):
        return self.place(source, 3, 32, 3 * n)

    def spectrum(self, source):
        return self.place(source, NF, NF, C + CF)


def load_taps(parts, at, taps):
    n = taps.shape[2]
    return [(taps[32 * part:32 * (part + 1)], parts[32 * part:32 * (part + 1), part, at].rearrange("p (r n) -> p r n", n=n))
            for part in range(3)]


def prepare(nc, x, stats, constants, split, parts, H):
    slabs = H // SLAB
    n = SLAB * W // BANK
    with Phase(nc, "prepare") as ph:
        xt = ph.sb("xt", [CH, 2, 2, SLAB * W])
        raw = ph.sb("raw", [128, split.n])
        rest = ph.sb("rest", [128, 2, split.n])
        part = ph.sb("parts", [128, 3, split.n], BF16)
        landed = [ph.sem(f"slab_landed{b}") for b in range(2)]
        counted = [ph.sem(f"slab_counted{b}", credit=1) for b in range(2)]
        zeroed, raw_landed, rounded, reduced, stored, constants_landed = (ph.sem(s) for s in (
            "raw_zeroed", "raw_landed", "part_rounded", "part_subtracted", "parts_stored", "constants_landed"))
        with nc.Block() as block:
            @block.sync
            def _(sp):
                with sp.Fori(0, slabs // 2) as i:
                    for b in range(2):
                        sp.wait_ge(counted[b], i * 2 * n + 1)
                        sp.dma_start(xt[:, b], x[:, :, bass.ds((i * 2 + b) * SLAB * W, SLAB * W)]).then_inc(landed[b], 16)

            @block.vector
            def _(dve):
                with dve.Fori(0, slabs // 2) as i:
                    for b in range(2):
                        dve.wait_ge(landed[b], i * 16 + 16)
                        for k in range(2):
                            for q in range(n):
                                nc.vector.bn_stats(stats[:, k, bass.ds((i * 2 + b) * n + q, 1), :],
                                                   xt[:, b, k, q * BANK:(q + 1) * BANK]).then_inc(counted[b], 1)

            @block.gpsimd
            def _(pool):
                nc.gpsimd.memset(raw[:], 0.0).then_inc(zeroed, 1)
                for tile, source in constants:
                    nc.gpsimd.dma_start(tile[:], source).then_inc(constants_landed, 16)
                whole = raw[:]
                for p in range(2):
                    pool.wait_ge(rounded, p + 1)
                    nc.gpsimd.tensor_tensor(rest[:, p], whole, part[:, p], ALU.subtract).then_inc(reduced, 1)
                    pool.wait_ge(reduced, p + 1)
                    whole = rest[:, p]
                pool.wait_ge(constants_landed, 16 * len(constants))

            @block.scalar
            def _(act):
                act.wait_ge(zeroed, 1)
                for source, rows, pitch, at in split.sources:
                    cols = raw[:, at]
                    if len(source.shape) == 3:
                        cols = cols.rearrange("p (r n) -> p r n", r=source.shape[1])
                    for p in range(3):
                        target = cols[p * pitch:p * pitch + rows]
                        target = target[:, :, 0:source.shape[2]] if len(source.shape) == 3 else target[:, 0:source.shape[1]]
                        act.dma_start(target, source).then_inc(raw_landed, 16)
                act.wait_ge(raw_landed, 48 * len(split.sources))
                for p in range(3):
                    if p > 0:
                        act.wait_ge(reduced, p)
                    nc.scalar.copy(part[:, p], raw[:] if p == 0 else rest[:, p - 1]).then_inc(rounded, 1)
                act.wait_ge(rounded, 3)
                act.dma_start(parts, part[:]).then_inc(stored, 16)
                act.wait_ge(stored, 16)


def fold_norm(nc, name, stats, group_mean, wT, wf, O, loads, extra=None):
    with Phase(nc, name) as ph:
        raw = ph.sb("raw", [CH, 2, O])
        mv = ph.sb("mv", [CH, 2, 2])
        gm = ph.sb("gm", [CH, 2])
        dev = ph.sb("dev", [CH, 2])
        dev2 = ph.sb("dev2", [CH, 2])
        var = ph.sb("var", [CH, 2])
        vare = ph.sb("vare", [CH, 2])
        std = ph.sb("std", [CH, 2])
        rstd = ph.sb("rstd", [CH, 2])
        negm = ph.sb("negm", [CH, 2, CH + 1])
        xrow = ph.sb("xrow", [CH + 1, 16])
        pm = ph.ps("pm", [CH, BANK])
        pv = ph.ps("pv", [CH, BANK])
        pb = [ph.ps(f"pb{j}", [CH + 1, BANK]) for j in range((O + BANK - 1) // BANK)]
        landed, zero, agg, mean, dv, pvar, sd, r, scaled, bias, d2, done = (ph.sem(s) for s in (
            "weights_landed", "negm_zeroed", "aggregated", "group_mean", "dve_step", "group_var",
            "std_ready", "rstd_ready", "weights_scaled", "bias_ready", "square_ready", "done"))
        D = {n: c + 1 for c, n in enumerate(("gm", "dev", "dev2", "vare"))}
        loaded, rounded = ph.sem("tiles_loaded"), ph.sem("rounded_tiles_loaded")
        as_is = [(tile, source) for tile, source in loads if tile.dtype == source.dtype]
        rounding = [(tile, source) for tile, source in loads if tile.dtype != source.dtype]
        with nc.Block() as block:
            @block.sync
            def _(sp):
                sp.dma_start(raw[:], wT).then_inc(landed, 16)
                if extra is not None:
                    sp.dma_start(xrow[CH:CH + 1, 0:extra.shape[1]], extra).then_inc(landed, 16)
                for tile, source in as_is:
                    sp.dma_start(tile, source).then_inc(loaded, 16)
                sp.wait_ge(loaded, 16 * len(as_is))

            @block.gpsimd
            def _(pool):
                for tile, source in rounding:
                    nc.gpsimd.dma_start(tile, source).then_inc(rounded, 16)
                if rounding:
                    pool.wait_ge(rounded, 16 * len(rounding))

            @block.vector
            def _(dve):
                nc.vector.memset(negm[:], 0.0).then_inc(zero, 1)
                for k in range(2):
                    nc.vector.bn_aggr(mv[:, k, :], stats[:, k]).then_inc(agg, 1)
                dve.wait_ge(mean, 1)
                dve.wait_ge(agg, 2)
                nc.vector.tensor_copy(gm[:], pm[:, 0:2]).then_inc(dv, 1)
                dve.wait_ge(dv, D["gm"])
                nc.vector.tensor_tensor(dev[:], mv[:, :, 0], gm[:], ALU.subtract).then_inc(dv, 1)
                dve.wait_ge(dv, D["dev"])
                nc.vector.tensor_tensor(dev2[:], dev[:], dev[:], ALU.mult).then_inc(dv, 1)
                dve.wait_ge(dv, D["dev2"])
                nc.vector.tensor_tensor(var[:], dev2[:], mv[:, :, 1], ALU.add).then_inc(d2, 1)
                dve.wait_ge(pvar, 1)
                nc.vector.tensor_scalar(vare[:], pv[:, 0:2], GN_EPS, None, ALU.add).then_inc(dv, 1)
                dve.wait_ge(sd, 1)
                nc.vector.reciprocal(rstd[:], std[:]).then_inc(r, 1)
                dve.wait_ge(r, 1)
                dve.wait_ge(zero, 1)
                dve.wait_ge(landed, 16 if extra is None else 32)
                for k in range(2):
                    nc.vector.tensor_scalar(wf[0:CH, k, :], raw[:, k, :], rstd[:, k:k + 1], None, ALU.mult).then_inc(scaled, 1)
                    nc.vector.tensor_scalar(negm[:, k, CH:CH + 1], gm[:, k:k + 1], -1.0, None, ALU.mult).then_inc(scaled, 1)
                dve.wait_ge(bias, 1)
                for j in range(len(pb)):
                    n = min(BANK, O - j * BANK)
                    nc.vector.tensor_copy(wf[CH:CH + 1, 0, j * BANK:j * BANK + n], pb[j][CH:CH + 1, 0:n]).then_inc(done, 1)
                if extra is not None:
                    dve.wait_ge(done, len(pb))
                    nc.vector.tensor_tensor(wf[CH:CH + 1, 0, O - N_HEADS:O], wf[CH:CH + 1, 0, O - N_HEADS:O],
                                            xrow[CH:CH + 1, 0:N_HEADS], ALU.add).then_inc(done, 1)

            @block.scalar
            def _(act):
                act.wait_ge(dv, D["vare"])
                nc.scalar.activation(std[:], vare[:], ACT.Sqrt).then_inc(sd, 1)

            @block.tensor
            def _(pe):
                pe.wait_ge(agg, 2)
                nc.tensor.matmul(pm[:, 0:2], group_mean[:], mv[:, :, 0], start=True, stop=True).then_inc(mean, 1)
                pe.wait_ge(d2, 1)
                nc.tensor.matmul(pv[:, 0:2], group_mean[:], var[:], start=True, stop=True).then_inc(pvar, 1)
                pe.wait_ge(scaled, 4)
                for j in range(len(pb)):
                    n = min(BANK, O - j * BANK)
                    for k in range(2):
                        last = nc.tensor.matmul(pb[j][:, 0:n], negm[:, k, :], wf[0:CH, k, j * BANK:j * BANK + n],
                                                start=(k == 0), stop=(k == 1))
                last.then_inc(bias, 1)


def first_slab(x):
    return x[:, :, 0:SLAB * W].rearrange("p k (h w) -> p k h w", w=W)


def project_patches(nc, name, x, xt, wf, t, H):
    slabs = H // SLAB
    fills = NPC // 2
    half = fills // 2
    with Phase(nc, name) as ph:
        xp = ph.sb("xp", [CH + 1, 2, 2, NPC, SLAB * PS])
        banks = [ph.ps(f"p{j}", [128, 2, C]) for j in range(fills)]
        landed = [ph.sem("slab_landed0", credit=16), ph.sem("slab_landed1")]
        ordered = [ph.sem(f"slab_ordered{b}", credit=2) for b in range(2)]
        filled = [ph.sem(f"banks_filled{b}", credit=1) for b in range(2)]
        free = [ph.sem("even_banks_free"), ph.sem("odd_banks_free")]
        ones = ph.sem("ones_set")
        with nc.Block() as block:
            @block.sync
            def _(sp):
                def load(i, b):
                    sp.wait_ge(ordered[b], i * 2 + 2)
                    sp.dma_start(xt[:, b], x[:, :, bass.ds((i * 2 + b) * SLAB * W, SLAB * W)]
                                 .rearrange("p k (h w) -> p k h w", w=W)).then_inc(landed[b], 16)

                load(0, 1)
                with sp.Fori(1, slabs // 2) as i:
                    for b in range(2):
                        load(i, b)

            @block.gpsimd
            def _(pool):
                nc.gpsimd.memset(xp[CH:CH + 1], 1.0).then_inc(ones, 1)

            @block.tensor
            def _(pe):
                pe.wait_ge(ones, 1)
                with pe.Fori(0, slabs // 2) as i:
                    for b in range(2):
                        pe.wait_ge(ordered[b], i * 2 + 4)
                        for j in range(fills):
                            pe.wait_ge(free[j % 2], (i * 2 + b) * half + j // 2 + 1)
                            for q in range(2):
                                for k in range(2):
                                    rows = CH + 1 - k
                                    last = nc.tensor.matmul(banks[j][:, q, :], xp[0:rows, b, k, 2 * j + q, :], wf[0:rows, k, :],
                                                            start=(k == 0), stop=(k == 1))
                            last.then_inc(filled[b], 1)

            def order_and_evacuate(eng, copy, part):
                eng.sem_inc(free[part], half)

                def order(i, b):
                    eng.wait_ge(landed[b], i * 16 + 16)
                    eng.wait_ge(filled[b], i * fills + 1)
                    copy(xp[0:CH, b, part].rearrange("p pc (h w) -> p pc h w", w=PS),
                         xt[:, b, part].rearrange("p h (pc w) -> p pc h w", w=PS)).then_inc(ordered[b], 1)

                def evacuate(i, b):
                    for j in range(part, fills, 2):
                        eng.wait_ge(filled[b], i * fills + j + 2)
                        copy(t[:, :, bass.ds((i * 2 + b) * NPC + 2 * j, 2), :],
                             banks[j][:].rearrange("p q (k c) -> p k q c", k=2)).then_inc(free[part], 1)

                order(0, 0)
                with eng.Fori(0, slabs // 2 - 1) as i:
                    order(i, 1)
                    evacuate(i, 0)
                    order(i + 1, 0)
                    evacuate(i, 1)
                order(slabs // 2 - 1, 1)
                evacuate(slabs // 2 - 1, 0)
                evacuate(slabs // 2 - 1, 1)

            @block.vector
            def _(dve):
                order_and_evacuate(dve, nc.vector.tensor_copy, 0)

            @block.scalar
            def _(act):
                order_and_evacuate(act, nc.scalar.copy, 1)


def unfold(sp, blocks, image, H, loaded):
    for pc in range(NPC):
        sp.dma_start(image[pc * PS:(pc + 1) * PS, 1:1 + H, :].rearrange("ww (s hh) c -> ww s hh c", hh=SLAB),
                     blocks.rearrange("(hh ww) (s pc) c -> pc ww s hh c", ww=PS, pc=NPC)[pc]).then_inc(loaded, 16)


def filter_patches(nc, name, t, patch_table, spec, blocks, image, loaded, H):
    nblk = H // SLAB * NPC
    npix = PS * PS
    opb = 16
    fills = npix // opb
    outs = CF // 4
    chunks = C // CF
    with Phase(nc, name) as ph:
        table = ph.sb("cosines", [128, npix, 128], BF16)
        wc = ph.sb("matrices", [128, 2, CF, 128])
        gen = [ph.ps(f"gen{j}", [128, BANK]) for j in range(4)]
        fb = [ph.ps(f"out{j}", [128, 4, nblk]) for j in range(4)]
        upper_zeroed, lower_zeroed, built, genlow, genhigh, filled, frd, fra, stored = (ph.sem(s) for s in (
            "upper_zeroed", "lower_zeroed", "gen_bank_built", "upper_patch_copied", "lower_patch_copied",
            "out_bank_filled", "even_out_banks_free", "odd_out_banks_free", "blocks_stored"))
        landed = [ph.sem(f"table_landed{f}") for f in range(fills)]
        with nc.Block() as block:
            @block.sync
            def _(sp):
                sp.wait_ge(frd, 2 + CH // 8)
                sp.wait_ge(fra, 2 + CH // 8)
                for s in range(H // SLAB):
                    sp.dma_start(blocks[0, :, s * NPC:(s + 1) * NPC, :], t[:, 0, s * NPC:(s + 1) * NPC, :]).then_inc(stored, 16)
                sp.wait_ge(stored, 16 * (H // SLAB))
                unfold(sp, blocks[0], image, H, loaded)

            @block.gpsimd
            def _(pool):
                for f in range(fills):
                    nc.gpsimd.dma_start(table[:, f * opb:(f + 1) * opb], patch_table[:, f * opb:(f + 1) * opb]).then_inc(landed[f], 16)
                for b in range(2):
                    nc.gpsimd.memset(wc[0:64, b, :, 64:128], 0.0).then_inc(upper_zeroed, 1)

            @block.tensor
            def _(pe):
                def build(s, f):
                    pe.wait_ge(genlow, s * fills + f + 1)
                    pe.wait_ge(genhigh, s * fills + f + 1)
                    for o in range(opb):
                        for part in range(3):
                            last = nc.tensor.matmul(gen[f][:, o * CF:(o + 1) * CF], table[:, f * opb + o, :],
                                                    spec[:, part, bass.ds(s * CF, CF)], start=(part == 0), stop=(part == 2))
                    last.then_inc(built, 1)

                for f in range(fills):
                    pe.wait_ge(landed[f], 16)
                    build(0, f)
                pe.wait_ge(upper_zeroed, 2)
                pe.wait_ge(lower_zeroed, 2)
                for h in range(2):
                    with pe.Fori(h * chunks // 4, (h + 1) * chunks // 4) as i:
                        for b in range(2):
                            s = i * 2 + b
                            pe.wait_ge(genlow, s * fills + fills + 4)
                            pe.wait_ge(genhigh, s * fills + fills + 4)
                            for q in range(outs):
                                pe.wait_ge((frd, fra)[q % 2], s * (outs // 2) + q // 2 + 1)
                                for c in range(4):
                                    ch = s * CF - h * CH + 4 * q + c
                                    last = nc.tensor.matmul(fb[(b * outs + q) % 4][:, c, :], wc[:, b, 4 * q + c, :],
                                                            t[:, h, :, bass.ds(ch, 1)].rearrange("p n o -> p (n o)"),
                                                            start=True, stop=True)
                                last.then_inc(filled, 1)
                                if q < fills:
                                    build(s + 1, q)

            def evacuate(eng, copy, lo, copied, free, parity):
                def matrices(s, b, f):
                    eng.wait_ge(built, s * fills + f + 1)
                    copy(wc[lo:lo + 64, b, :, lo + f * opb:lo + (f + 1) * opb].rearrange("p c o -> p o c"),
                         gen[f][lo:lo + 64, 0:opb * CF].rearrange("p (o c) -> p o c", c=CF)).then_inc(copied, 1)

                eng.sem_inc(copied, 4)
                eng.sem_inc(free, 2)
                for f in range(fills):
                    matrices(0, 0, f)
                for h in range(2):
                    with eng.Fori(h * chunks // 4, (h + 1) * chunks // 4) as i:
                        for b in range(2):
                            s = i * 2 + b
                            for q in range(outs):
                                if q % 2 == parity:
                                    eng.wait_ge(filled, s * outs + q + 1)
                                    copy(t[:, h, :, bass.ds(s * CF - h * CH + 4 * q, 4)].rearrange("p n c -> p c n"),
                                         fb[(b * outs + q) % 4][:]).then_inc(free, 1)
                                if q < fills:
                                    matrices(s + 1, 1 - b, q)

            @block.vector
            def _(dve):
                for b in range(2):
                    nc.vector.memset(wc[64:128, b, :, 0:64], 0.0).then_inc(lower_zeroed, 1)
                evacuate(dve, nc.vector.tensor_copy, 0, genlow, frd, 0)

            @block.scalar
            def _(act):
                evacuate(act, nc.scalar.copy, 64, genhigh, fra, 1)
    return 16 * NPC


class Bands:
    FILLS = W // OPB
    CONVS = CC // 4

    def __init__(self, nc, ph, table, taps, rows, mats=None):
        self.nc, self.table, self.taps, self.rows = nc, table, taps, rows
        self.mats = ph.sb("bands", [128, 2, 3 * CC, W]) if mats is None else mats
        self.gen = [ph.ps(f"gen{j}", [128, OPB, 3 * CC]) for j in range(4)]
        self.out = [ph.ps(f"conv{j}", [128, 4, rows]) for j in range(4)]
        self.built = ph.sem("gen_bank_built")
        self.copied = ph.sem("gen_bank_copied")
        self.filled = ph.sem("conv_bank_filled")
        self.free = ph.sem("conv_bank_free")

    def start(self, pe):
        pe.sem_inc(self.filled, 1)
        for f in range(self.FILLS):
            self.build(pe, 0, f)

    def build(self, pe, t, f):
        pe.wait_ge(self.copied, t * self.FILLS + f + 1)
        for o in range(OPB):
            start = W - (f * OPB + o)
            last = self.nc.tensor.matmul(self.gen[f % 4][:, o, :], self.table[:, start:start + W],
                                         self.taps[:, :, bass.ds(t * CC, CC)], start=True, stop=True)
        last.then_inc(self.built, 1)

    def convolve(self, pe, s, b, image, c0):
        nc = self.nc
        pe.wait_ge(self.copied, s * self.FILLS + self.FILLS + 4)
        for q in range(self.CONVS):
            for f in range(4 * q, 4 * q + 4):
                self.build(pe, s + 1, f)
            pe.wait_ge(self.free, s * self.CONVS + q + 1)
            for c in range(4):
                for a in range(3):
                    last = nc.tensor.matmul(
                        self.out[q][:, c, :], self.mats[:, b, a * CC + 4 * q + c, :],
                        image[:, a:a + self.rows, bass.ds(c0 + 4 * q + c, 1)].rearrange("p n o -> p (n o)"),
                        start=(a == 0), stop=(a == 2))
            last.then_inc(self.filled, 1)

    def copy_matrices(self, eng, copy, t, b):
        for f in range(self.FILLS):
            eng.wait_ge(self.built, t * self.FILLS + f + 1)
            if f == 0:
                eng.wait_ge(self.filled, (t - 1) * self.CONVS + 1)
            copy(self.mats[:, b, :, f * OPB:(f + 1) * OPB].rearrange("p c o -> p o c"), self.gen[f % 4][:])\
                .then_inc(self.copied, 1)


def convolve_gate(nc, name, table, taps, t, blocks, images, first_loaded, at_first, H):
    with Phase(nc, name) as ph:
        bands = Bands(nc, ph, table, taps, H, mats=t[:, 0].rearrange("p n c -> p (n c)")[:, 0:2 * 3 * CC * W]
                      .rearrange("p (b c w) -> p b c w", b=2, w=W))
        stored, loaded, border, gated = (ph.sem(s) for s in ("blocks_stored", "image_loaded", "border_zeroed", "gelu_done"))
        pairs = CH // CC // 2
        n_half = CH // CC
        with nc.Block() as block:
            @block.sync
            def _(sp):
                for s in range(H // SLAB):
                    sp.dma_start(blocks[1, :, s * NPC:(s + 1) * NPC, :], t[:, 1, s * NPC:(s + 1) * NPC, :]).then_inc(stored, 16)
                sp.wait_ge(stored, 16 * (H // SLAB))
                unfold(sp, blocks[1], images[1], H, loaded)
                sp.wait_ge(loaded, 16 * NPC)

            @block.gpsimd
            def _(pool):
                for image in images:
                    nc.gpsimd.memset(image[:, 0, :], 0.0).then_inc(border, 1)
                    nc.gpsimd.memset(image[:, H + 1, :], 0.0).then_inc(border, 1)

            @block.tensor
            def _(pe):
                bands.start(pe)
                pe.wait_ge(border, 4)
                for h, image in enumerate(images):
                    if h == 0:
                        pe.wait_ge(first_loaded, at_first)
                    else:
                        pe.wait_ge(loaded, 16 * NPC)
                    with pe.Fori(h * pairs, (h + 1) * pairs) as i:
                        for b in range(2):
                            s = i * 2 + b
                            bands.convolve(pe, s, b, image, s * CC - h * CH)

            @block.vector
            def _(dve):
                dve.sem_inc(bands.copied, 4)
                for f in range(bands.FILLS):
                    dve.wait_ge(bands.built, f + 1)
                    nc.vector.tensor_copy(bands.mats[:, 0, :, f * OPB:(f + 1) * OPB].rearrange("p c o -> p o c"),
                                          bands.gen[f % 4][:]).then_inc(bands.copied, 1)
                with dve.Fori(0, pairs) as i:
                    for b in range(2):
                        bands.copy_matrices(dve, nc.vector.tensor_copy, i * 2 + b + 1, 1 - b)
                dve.wait_ge(gated, n_half * bands.CONVS)
                with dve.Fori(0, pairs) as i:
                    for b in range(2):
                        for q in range(bands.CONVS):
                            s = i * 2 + b + n_half
                            dve.wait_ge(bands.filled, s * bands.CONVS + q + 2)
                            g = images[0][:, 1:1 + H, bass.ds((i * 2 + b) * CC + 4 * q, 4)].rearrange("p n c -> p c n")
                            nc.vector.tensor_tensor(g, bands.out[q][:], g, ALU.mult).then_inc(bands.free, 1)

            @block.scalar
            def _(act):
                act.sem_inc(bands.free, 4)
                with act.Fori(0, pairs) as i:
                    for b in range(2):
                        for q in range(bands.CONVS):
                            s = i * 2 + b
                            act.wait_ge(bands.filled, s * bands.CONVS + q + 2)
                            g = images[0][:, 1:1 + H, bass.ds(s * CC + 4 * q, 4)].rearrange("p n c -> p c n")
                            ins = nc.scalar.activation(g, bands.out[q][:], ACT.Gelu)
                            ins.then_inc(gated, 1)
                            act.wait_ge(gated, s * bands.CONVS + q + 1)
                            act.sem_inc(bands.free, 1)
                act.wait_ge(bands.copied, 4 + (n_half + 1) * bands.FILLS)
                with act.Fori(0, pairs) as i:
                    for b in range(2):
                        bands.copy_matrices(act, nc.scalar.copy, i * 2 + b + n_half + 1, 1 - b)


def project_out(nc, name, image, ident, wo_dram, x, x_new, stats, H):
    R = 4
    tiles = H // R
    U = 4

    def done(s):
        return s + U + 1

    with Phase(nc, name) as ph:
        wo = ph.sb("wo", [CH, C])
        gs = ph.sb("gs", [128, 2, R, CH])
        gt = ph.sb("gt", [CH, 2, R * W])
        xt = ph.sb("xt", [CH, U, 2, R * W])
        xo = ph.sb("xo", [CH, U, 2, R * W])
        tp = [ph.ps(f"tp{b}", [CH, R * W]) for b in range(2)]
        po = [[ph.ps(f"po{b}{k}", [CH, R * W]) for k in range(2)] for b in range(2)]
        wl, staged, counted, evacuated = (ph.sem(s) for s in ("weights_landed", "rows_staged", "sum_counted", "product_evacuated"))
        turned, copied = (ph.sem(s, credit=U) for s in ("tile_turned", "turned_copied"))
        product, added = ([ph.sem(f"{s}{k}", credit=U) for k in range(2)] for s in ("product_done", "sum_done"))
        landed = [ph.sem(f"x_landed{u}") for u in range(U)]
        stored = [ph.sem(f"x_stored{u}", credit=16) for u in range(U)]

        def steps(eng, step, peel):
            with eng.Fori(0, tiles // U - peel) as i:
                for u in range(U):
                    step(i * U + u, u, i, False)
            if peel:
                for u in range(U):
                    step(tiles - U + u, u, tiles // U - 1, u == U - 1)

        with nc.Block() as block:
            @block.sync
            def _(sp):
                sp.dma_start(wo[:], wo_dram).then_inc(wl, 16)

                def load(s, u):
                    sp.dma_start(xt[:, u], x[:, :, bass.ds(s * R * W, R * W)]).then_inc(landed[u], 16)

                def store(s, u, i, last):
                    for k in range(2):
                        sp.wait_ge(added[k], done(s))
                    sp.dma_start(x_new[:, :, bass.ds(s * R * W, R * W)], xo[:, u]).then_inc(stored[u], 16)
                    if not isinstance(s, int):
                        load(s + U, u)

                for u in range(U):
                    load(u, u)
                steps(sp, store, 1)
                sp.wait_ge(wl, 16)
                for u in range(U):
                    sp.wait_ge(stored[u], 16 * (tiles // U) + 16)

            @block.gpsimd
            def _(pool):
                def add(s, u, i, last):
                    pool.wait_ge(landed[u], i * 16 + 16)
                    pool.wait_ge(evacuated, s + 1)
                    nc.gpsimd.tensor_tensor(xo[:, u, 1, :], xo[:, u, 1, :], xt[:, u, 1, :], ALU.add).then_inc(added[1], 1)

                steps(pool, add, 0)

            @block.tensor
            def _(pe):
                def turn(s, b):
                    pe.wait_ge(staged, s + 1)
                    pe.wait_ge(copied, done(s - 2))
                    for r in range(R):
                        last = nc.tensor.transpose(tp[b][:, r * W:(r + 1) * W], gs[:, b, r, :], ident[:])
                    last.then_inc(turned, 1)

                def step(s, u, i, last):
                    b = u % 2
                    if not last:
                        turn(s + 1, 1 - b)
                    pe.wait_ge(copied, done(s))
                    for k in range(2):
                        pe.wait_ge(added[k], done(s - 2))
                        nc.tensor.matmul(po[b][k][:], wo[:, k * CH:(k + 1) * CH], gt[:, b, :], start=True, stop=True)\
                            .then_inc(product[k], 1)

                pe.wait_ge(wl, 16)
                turn(0, 0)
                steps(pe, step, 1)

            @block.scalar
            def _(act):
                def stage(s, b):
                    act.wait_ge(turned, done(s - 2))
                    nc.scalar.copy(gs[:, b], image[:, bass.ds(s * R + 1, R), 0:CH]).then_inc(staged, 1)

                def copy(s, b):
                    act.wait_ge(turned, done(s))
                    act.wait_ge(product[1], done(s - 2))
                    nc.scalar.copy(gt[:, b, :], tp[b][:]).then_inc(copied, 1)

                def step(s, u, i, last):
                    if not (isinstance(s, int) and s + 2 >= tiles):
                        stage(s + 2, u % 2)
                    if not last:
                        copy(s + 1, (u + 1) % 2)
                    act.wait_ge(stored[u], i * 16 + 16)
                    act.wait_ge(product[1], done(s))
                    nc.scalar.copy(xo[:, u, 1, :], po[u % 2][1][:]).then_inc(evacuated, 1)

                stage(0, 0)
                stage(1, 1)
                copy(0, 0)
                steps(act, step, 1)

            @block.vector
            def _(dve):
                def add(s, u, i, last):
                    dve.wait_ge(landed[u], i * 16 + 16)
                    dve.wait_ge(stored[u], i * 16 + 16)
                    dve.wait_ge(product[0], done(s))
                    nc.vector.tensor_tensor(xo[:, u, 0, :], po[u % 2][0][:], xt[:, u, 0, :], ALU.add).then_inc(added[0], 1)
                    for k in range(2):
                        dve.wait_ge(added[k], done(s))
                        nc.vector.bn_stats(stats[:, k, bass.ds(s, 1), :], xo[:, u, k, :]).then_inc(counted, 1)

                steps(dve, add, 0)


def patch_layer(nc, name, x, x_new, p, k, blocks, stats_in, stats, H):
    with nc.sbuf_tensor(f"{name}_taps", [96, 3, C + CC], BF16) as taps, nc.sbuf_tensor(f"{name}_spec", [128, 3, C + CF], BF16) as spec, \
            nc.sbuf_tensor(f"{name}_t", [128, 2, W // SLAB * NPC, CH], F32) as t_full:
        t = t_full[:, :, 0:H // SLAB * NPC, :]
        with nc.sbuf_tensor(f"{name}_wf", [CH + 1, 2, C], F32) as wf, \
                nc.sbuf_tensor(f"{name}_xt", [CH, 2, 2, SLAB, W], F32) as xt:
            loads = load_taps(k["parts"], k["taps_at"][name], taps) + [
                (spec[:], k["parts"][:, :, k["spectrum_at"][name]]), (xt[:, 0], first_slab(x))]
            fold_norm(nc, f"{name}_fold", stats_in, k["group_mean"], p["w_in"], wf, C, loads)
            project_patches(nc, f"{name}_in", x, xt, wf, t, H)
        with nc.sbuf_tensor(f"{name}_image0", [128, H + 2, CH], F32) as image0:
            with Phase(nc, f"{name}_late") as late:
                loaded = late.sem("first_half_loaded")
                at_first = filter_patches(nc, f"{name}_filter", t, k["patch_table"], spec, blocks, image0, loaded, H)
                with nc.sbuf_tensor(f"{name}_image1", [128, H + 2, CH], F32) as image1:
                    convolve_gate(nc, f"{name}_conv", k["table"], taps, t_full, blocks, (image0, image1), loaded, at_first, H)
            project_out(nc, f"{name}_out", image0, k["ident"], p["w_out"], x, x_new, stats, H)
def spread(ap, n):
    return ap.unsqueeze(2).broadcast_to([ap.shape[0], ap.shape[1], n])


GROUP = CONV_DIM // 4


def slabs_in(arena):
    return arena[0:CH + 1, 0:4 * SLAB * W].rearrange("p (b k h w) -> p b k h w", b=2, k=2, h=SLAB)


def project_rows(nc, name, x, wf, arena, images, dt_raw, proj, H):
    slabs = H // SLAB
    R = 4
    tiles = SLAB // R
    O = CONV_DIM + N_HEADS
    with Phase(nc, name) as ph:
        n = 4 * SLAB * W
        xt = slabs_in(arena)
        stage = arena[:, n:n + tiles * R * 2 * GROUP].rearrange("p (q g r c) -> p q g r c", q=tiles, g=2, r=R)
        banks = [ph.ps(f"row{j}", [128, O]) for j in range(8)]
        landed = [ph.sem("slab_landed0", credit=16), ph.sem("slab_landed1")]
        filled = ph.sem("row_projected")
        used = [ph.sem(f"slab_used{b}", credit=1) for b in range(2)]
        copied = [ph.sem("even_rows_copied"), ph.sem("odd_rows_copied")]
        stored = [ph.sem(f"rows_stored{q}", credit=16) for q in range(4)]
        ones = ph.sem("ones_set")
        with nc.Block() as block:
            @block.sync
            def _(sp):
                def load(i, b):
                    sp.wait_ge(used[b], i + 1)
                    sp.dma_start(xt[0:CH, b], x[:, :, bass.ds((i * 2 + b) * SLAB * W, SLAB * W)]
                                 .rearrange("p k (h w) -> p k h w", w=W)).then_inc(landed[b], 16)

                load(0, 1)
                with sp.Fori(1, slabs // 2) as i:
                    for b in range(2):
                        load(i, b)

            @block.gpsimd
            def _(pool):
                nc.gpsimd.memset(xt[CH:CH + 1], 1.0).then_inc(ones, 1)

            @block.tensor
            def _(pe):
                pe.wait_ge(ones, 1)
                with pe.Fori(0, slabs // 2) as i:
                    for b in range(2):
                        pe.wait_ge(landed[b], i * 16 + 16)
                        for r in range(SLAB):
                            pe.wait_ge(copied[r % 2], (i * 2 + b) * (SLAB // 2) + r // 2 + 1)
                            for k in range(2):
                                rows = CH + 1 - k
                                last = nc.tensor.matmul(banks[r % 8][:], xt[0:rows, b, k, r, :], wf[0:rows, k, D_INNER:D_INNER + O],
                                                        start=(k == 0), stop=(k == 1))
                            last.then_inc(filled, 1)
                        pe.wait_ge(filled, (i * 2 + b) * SLAB + SLAB)
                        pe.sem_inc(used[b], 1)

            def evacuate(eng, copy, par, store=None):
                eng.sem_inc(copied[par], 4)
                with eng.Fori(0, slabs // 2) as i:
                    for b in range(2):
                        for r in range(par, SLAB, 2):
                            if r % R == par:
                                eng.wait_ge(stored[r // R], (i * 2 + b) * 16 + 16)
                            eng.wait_ge(filled, (i * 2 + b) * SLAB + r + 1)
                            h = (i * 2 + b) * SLAB + r
                            for g in range(2):
                                copy(images[g][:, bass.ds(h + 1, 1), :].rearrange("p o c -> p (o c)"),
                                     banks[r % 8][:, g * GROUP:(g + 1) * GROUP])
                            copy(dt_raw[:, bass.ds(h, 1), :].rearrange("p o n -> p (o n)"), banks[r % 8][:, CONV_DIM:O])
                            copy(stage[:, r // R, :, r % R, :], banks[r % 8][:, 2 * GROUP:CONV_DIM].rearrange("p (g c) -> p g c", g=2))\
                                .then_inc(copied[par], 1)
                            if store and r % R == R - 1:
                                for p2 in range(2):
                                    eng.wait_ge(copied[p2], (i * 2 + b) * (SLAB // 2) + (r + 1) // 2 + 4)
                                store(r // R, (i * 2 + b) * SLAB + r + 1 - R)

            @block.vector
            def _(dve):
                evacuate(dve, nc.vector.tensor_copy, 0)

            @block.scalar
            def _(act):
                def store(q, h0):
                    act.dma_start(proj[:, :, bass.ds(h0, R), :].rearrange("g w r c -> w g r c"), stage[:, q])\
                        .then_inc(stored[q], 16)

                evacuate(act, nc.scalar.copy, 1, store)
                for q in range(4):
                    act.wait_ge(stored[q], 16 * slabs + 16)


def convolve_rows(nc, name, table, taps, bias_dram, arena, image, proj, xbc, last_stored, H):
    slabs = H // SLAB
    chunks = GROUP // CC
    with Phase(nc, name) as ph:
        bias = ph.sb("bias", [128, CONV_DIM])
        bands = Bands(nc, ph, table, taps, H, mats=arena[:].rearrange("p (b c w) -> p b c w", b=2, w=W))
        landed = [ph.sem(f"rows_landed{g}", credit=16) for g in range(2)]
        stored = [ph.sem("rows_stored0"), last_stored]
        passed = ph.sem("waits_passed")
        border, activated, bias_landed = ph.sem("border_zeroed"), ph.sem("silu_done"), ph.sem("bias_landed")

        def chunk_steps(i, g, eng, step):
            base = i * 2 * chunks + g * chunks
            with eng.Fori(0, chunks // 2) as j:
                for b in range(2):
                    step(base + j * 2 + b, (g + b) % 2, (j * 2 + b) * CC)
            step(base + chunks - 1, g, (chunks - 1) * CC)

        with nc.Block() as block:
            @block.sync
            def _(sp):
                sp.dma_start(bias[:], bias_dram).then_inc(bias_landed, 16)
                for g in range(2):
                    sp.wait_ge(stored[g], 16 * slabs)
                    for s in range(slabs):
                        sp.dma_start(image[g][:, 1 + s * SLAB:1 + (s + 1) * SLAB, :],
                                     proj[g, :, s * SLAB:(s + 1) * SLAB, :]).then_inc(landed[g], 16)

            @block.gpsimd
            def _(pool):
                for g in range(2):
                    nc.gpsimd.memset(image[g][:, 0, :], 0.0).then_inc(border, 1)
                    nc.gpsimd.memset(image[g][:, H + 1, :], 0.0).then_inc(border, 1)

            @block.tensor
            def _(pe):
                bands.start(pe)
                pe.wait_ge(border, 4)
                with pe.Fori(0, 2) as i:
                    for g in range(2):
                        hold(pe, landed[g], i * 16 * slabs + 16, passed)
                        def convolve(s, b, c0, group=image[g]):
                            bands.convolve(pe, s, b, group, c0)

                        chunk_steps(i, g, pe, convolve)

            @block.vector
            def _(dve):
                dve.sem_inc(bands.copied, 4)
                for f in range(bands.FILLS):
                    dve.wait_ge(bands.built, f + 1)
                    nc.vector.tensor_copy(bands.mats[:, 0, :, f * OPB:(f + 1) * OPB].rearrange("p c o -> p o c"),
                                          bands.gen[f % 4][:]).then_inc(bands.copied, 1)
                with dve.Fori(0, 2) as i:
                    for g in range(2):
                        chunk_steps(i, g, dve, lambda s, b, c0: bands.copy_matrices(dve, nc.vector.tensor_copy, s + 1, 1 - b))

            @block.scalar
            def _(act):
                act.wait_ge(bias_landed, 16)
                act.sem_inc(bands.free, 4)

                def silu(i, g, s, c0):
                    for q in range(bands.CONVS):
                        act.wait_ge(bands.filled, s * bands.CONVS + q + 2)
                        for c in range(4):
                            ch = c0 + 4 * q + c
                            last = nc.scalar.activation(
                                image[g][:, 1:1 + H, bass.ds(ch, 1)].rearrange("p n o -> p (n o)"), bands.out[q][:, c, :], ACT.Silu,
                                bias=bias[:, bass.ds((i * 2 + g) * GROUP + ch, 1)])
                            last.then_inc(activated, 1)
                        act.wait_ge(activated, s * CC + 4 * q + 4)
                        act.sem_inc(bands.free, 1)

                with act.Fori(0, 2) as i:
                    for g in range(2):
                        chunk_steps(i, g, act, lambda s, b, c0: silu(i, g, s, c0))
                        act.wait_ge(activated, (i * 2 + g + 1) * GROUP)
                        for s in range(slabs):
                            act.dma_start(xbc[bass.ds(i * 2 + g, 1), :, s * SLAB:(s + 1) * SLAB, :].rearrange("o w h c -> w (o h) c"),
                                          image[g][:, 1 + s * SLAB:1 + (s + 1) * SLAB, :]).then_inc(stored[g], 16)
                act.wait_ge(stored[0], 32 * slabs)
    return 32 * slabs


SCAL = 4
CUM, EXP_CUM, DT, TO_END = range(SCAL)


def step_sizes(nc, name, dt_raw, alog, tri, ones, ident_bf, scal, end_decay, cum_t, H):
    PAIRS = H // 2
    N = H * N_HEADS
    B = (N + BANK - 1) // BANK
    with Phase(nc, name) as ph:
        ea = ph.sb("ea", [128, N_HEADS])
        t = {n: ph.sb(n, [128, N]) for n in ("abs", "e", "relu", "dt", "da", "cs", "rest")}
        t |= {"u": t["abs"], "l": t["e"], "erest": t["relu"], "cum_rest": t["abs"], "cum_rest2": t["e"]}
        parts = ph.sb("parts", [128, H, 64], BF16)
        tb = [ph.ps(f"turned{j}", [128, 8, W], BF16) for j in range(2)]
        turned, kept, padded, fields = (ph.sem(s) for s in ("parts_turned", "turned_kept", "parts_padded", "fields_written"))
        cp = [ph.ps(f"cum{j}", [128, BANK]) for j in range(B)]
        tp = [ph.ps(f"tot{j}", [128, BANK]) for j in range(B)]
        a, v, p = ph.sem("act_step"), ph.sem("dve_step"), ph.sem("sums_done")
        A = {n: c + 1 for c, n in enumerate(("abs", "e", "ea", "l", "exp_cum", "erest"))}
        V = {n: c + 1 for c, n in enumerate(("u", "relu", "dt", "da", "cs", "rest", "part0", "left0", "part1", "left1", "part2"))}
        raw = dt_raw[:].rearrange("p h n -> p (h n)")

        def part(j):
            return slice(j * BANK, min(N, (j + 1) * BANK))

        def field(n):
            return scal[:, :, n, :]

        def part_of(n):
            return parts[:, :, n * N_HEADS:(n + 1) * N_HEADS]

        def rows(tile):
            return tile[:].rearrange("p (h n) -> p h n", n=N_HEADS)

        with nc.Block() as block:
            @block.gpsimd
            def _(pool):
                nc.gpsimd.memset(parts[:], 0.0).then_inc(padded, 1)
                pool.wait_ge(v, V["dt"])
                nc.gpsimd.tensor_copy(field(DT), rows(t["dt"])).then_inc(fields, 1)
                pool.wait_ge(v, V["cs"])
                nc.gpsimd.tensor_copy(field(CUM), rows(t["cs"])).then_inc(fields, 1)

            @block.scalar
            def _(act):
                nc.scalar.activation(t["abs"][:], raw, ACT.Abs).then_inc(a, 1)
                act.wait_ge(a, A["abs"])
                nc.scalar.activation(t["e"][:], t["abs"][:], ACT.Exp, scale=-1.0).then_inc(a, 1)
                nc.scalar.activation(ea[:], alog[:], ACT.Exp).then_inc(a, 1)
                act.wait_ge(v, V["u"])
                nc.scalar.activation(t["l"][:], t["u"][:], ACT.Ln).then_inc(a, 1)
                act.wait_ge(v, V["cs"])
                nc.scalar.activation(field(EXP_CUM), rows(t["cs"]), ACT.Exp).then_inc(a, 1)
                act.wait_ge(v, V["rest"])
                nc.scalar.activation(t["erest"][:], t["rest"][:], ACT.Exp).then_inc(a, 1)
                for j in range(B):
                    nc.scalar.activation(end_decay.rearrange("p h n -> p (h n)")[:, part(j)],
                                         tp[j][:, 0:part(j).stop - part(j).start], ACT.Exp).then_inc(a, 1)

            @block.vector
            def _(dve):
                dve.wait_ge(a, A["e"])
                nc.vector.tensor_scalar(t["u"][:], t["e"][:], 1.0, None, ALU.add).then_inc(v, 1)
                nc.vector.tensor_scalar(t["relu"][:], raw, 0.0, None, ALU.max).then_inc(v, 1)
                dve.wait_ge(a, A["l"])
                dve.wait_ge(v, V["relu"])
                nc.vector.tensor_tensor(t["dt"][:], t["relu"][:], t["l"][:], ALU.add).then_inc(v, 1)
                dve.wait_ge(v, V["dt"])
                for_heads = ea[:].unsqueeze(1).broadcast_to([128, H, N_HEADS])
                nc.vector.scalar_tensor_tensor(out=rows(t["da"]), in0=rows(t["dt"]), scalar=-1.0, in1=for_heads,
                                               op0=ALU.mult, op1=ALU.mult).then_inc(v, 1)
                dve.wait_ge(p, 1)
                for j in range(B):
                    last = nc.vector.tensor_copy(t["cs"][:, part(j)], cp[j][:, 0:part(j).stop - part(j).start])
                last.then_inc(v, 1)
                dve.wait_ge(v, V["cs"])
                for j in range(B):
                    last = nc.vector.tensor_tensor(t["rest"][:, part(j)], tp[j][:, 0:part(j).stop - part(j).start],
                                                   t["cs"][:, part(j)], ALU.subtract)
                last.then_inc(v, 1)
                dve.wait_ge(padded, 1)
                nc.vector.tensor_copy(part_of(0), rows(t["cs"])).then_inc(v, 1)
                dve.wait_ge(v, V["part0"])
                nc.vector.tensor_tensor(rows(t["cum_rest"]), rows(t["cs"]), part_of(0), ALU.subtract).then_inc(v, 1)
                dve.wait_ge(v, V["left0"])
                nc.vector.tensor_copy(part_of(1), rows(t["cum_rest"])).then_inc(v, 1)
                dve.wait_ge(v, V["part1"])
                nc.vector.tensor_tensor(rows(t["cum_rest2"]), rows(t["cum_rest"]), part_of(1), ALU.subtract).then_inc(v, 1)
                dve.wait_ge(v, V["left1"])
                nc.vector.tensor_copy(part_of(2), rows(t["cum_rest2"])).then_inc(v, 1)
                for q in range(PAIRS // 8):
                    dve.wait_ge(turned, q + 1)
                    nc.vector.tensor_copy(cum_t[:, 8 * q:8 * q + 8, :], tb[q % 2][:]).then_inc(kept, 1)
                dve.wait_ge(a, A["erest"])
                nc.vector.tensor_tensor(field(TO_END), rows(t["erest"]), rows(t["dt"]), ALU.mult).then_inc(v, 1)

            @block.tensor
            def _(pe):
                pe.wait_ge(v, V["da"])
                for j in range(B):
                    n = part(j).stop - part(j).start
                    nc.tensor.matmul(cp[j][:, 0:n], tri[:], t["da"][:, part(j)], start=True, stop=True)
                    last = nc.tensor.matmul(tp[j][:, 0:n], ones[:], t["da"][:, part(j)], start=True, stop=True)
                last.then_inc(p, 1)
                pe.wait_ge(v, V["part2"])
                for q in range(PAIRS // 8):
                    if q >= 2:
                        pe.wait_ge(kept, q - 1)
                    for j in range(8):
                        pair = 8 * q + j
                        last = nc.tensor.transpose(tb[q % 2][:, j, :], parts[:, 2 * pair:2 * pair + 2, :]
                                                   .rearrange("p h n -> p (h n)"), ident_bf[:])
                    last.then_inc(turned, 1)


def scan_rows(nc, name, p, k, x, x_new, wf, xbc, scal, end_decay, cum_t, stats, H):
    U = 4
    with Phase(nc, name) as ph:
        ident, tri, spreads = k["ident"], k["tri_sb"], k["spread_sb"]
        wo = ph.sb("wo", [128, 3, C])
        nw = ph.sb("norm_w", [128, 3])
        nb = ph.sb("norm_b", [128, 3])
        dskip = ph.sb("dskip", [128, N_HEADS])
        half = ph.sb("minus_half", [128, 1])
        pick = ph.sb("pick", [128, 2 * N_HEADS, 128], BF16)
        xc = ph.sb("xc", [128, U, CONV_DIM])
        xr = ph.sb("xr", [CH + 1, U, 2, W])
        rs = ph.sb("row_scalars", [128, U, SCAL, N_HEADS])
        xdt = ph.sb("xdt", [128, 2, D_INNER])
        xw = ph.sb("xw", [128, 2, D_INNER])
        xd = ph.sb("xd", [128, 2, D_INNER])
        bct = ph.sb("bct", [N_STATE, 2, 2, W])
        decay = ph.sb("decay", [128, 2, N_HEADS, W])
        causal = ph.sb("causal_scores", [128, 2, W])
        att = ph.sb("att", [128, 2, N_HEADS, W])
        state = ph.sb("state", [N_STATE, D_INNER])
        faded = ph.sb("faded", [N_STATE, D_INNER])
        inter = ph.sb("inter", [128, 2, D_INNER])
        y = ph.sb("y", [128, 2, D_INNER])
        yn = ph.sb("yn", [128, 2, D_INNER])
        st6 = ph.sb("st6", [128, U, 6])
        mv = ph.sb("mv", [128, U, 2])
        rstd = ph.sb("rstd", [128, U, 1])
        yw = ph.sb("yw", [128, 2, 3, W])
        yz = ph.sb("yz", [128, 3, W])
        xo = ph.sb("xo", [CH, U, 2, W])
        cum = [ph.ps(f"cum{j}", [128, 4, W]) for j in range(2)]
        p_bcg = ph.ps("bcg", [128, 2, W])
        p_y = ph.ps("y_intra", [128, D_INNER])
        p_i = ph.ps("y_inter", [128, D_INNER])
        p_t = ph.ps("turned", [128, 3, W])
        p_z = ph.ps("gate", [128, 3, W])
        p_o = ph.ps("projected", [CH, 2, W])
        gap_done, att_done = ph.sem("gap_done", credit=8), ph.sem("att_done", credit=3)
        inter_done, yi_done, st_done, turned, yz_done, masked = (ph.sem(n, credit=1) for n in (
            "inter_done", "intra_done", "chunk_state_done", "yn_turned", "yz_done", "scores_masked"))
        (ready, exp_done, bc_turned, bc_copied, cum_done, scores, xs_ready, rs_ready, scaled, skipped, y_done, counted, agg, rstd_done,
         yn_done, yw_done, z_done, o_done, xo_done, state_ready, faded_done, stats_done, passed) = (
            ph.sem(n) for n in (
                "constants_ready", "exp_done", "bc_turned", "bc_copied", "cum_done", "scores_done", "xs_ready", "row_scalars_ready",
                "inter_scaled", "skip_added", "y_done", "y_counted", "y_aggregated", "rstd_done", "yn_done", "yw_done", "z_done",
                "projected", "xo_done", "state_ready", "state_faded", "xo_counted", "waits_passed"))
        xc_landed = [ph.sem(f"xc_landed{b}") for b in range(U)]
        xr_landed = [ph.sem(f"xr_landed{b}") for b in range(U)]
        stored = [ph.sem(f"xo_stored{b}", credit=16) for b in range(U)]
        consts = [(wo, p["out_proj_w"]), (nw, p["norm_w"]), (nb, p["norm_b"]), (dskip, p["D"])]
        CONST = 16 * len(consts) + 3

        def turns(eng, turn):
            def run(t, b, i):
                def at(lag):
                    r = t - lag
                    if isinstance(t, int) and not 0 <= r < H:
                        return None
                    return r, (b - lag) % U, (i if b >= lag else i - 1)
                turn(at)

            for t in range(U):
                run(t, t, 0)
            with eng.Fori(1, H // U) as i:
                for b in range(U):
                    run(i * U + b, b, i)
            for t in range(H, H + 3):
                run(t, t - H, H // U)

        with nc.Block() as block:
            @block.sync
            def _(sp):
                for tile, source in consts:
                    sp.dma_start(tile[:], source).then_inc(ready, 16)

                def turn(at):
                    if row := at(0):
                        r, b, n = row
                        if not (isinstance(r, int) and r < U):
                            hold(sp, st_done, r - 2, passed)
                            hold(sp, xs_ready, 3 * (r - 3), passed)
                        sp.dma_start(xc[:, b, :].rearrange("w (g c) -> w g c", g=4),
                                     xbc[:, :, bass.ds(r, 1), :].rearrange("g w o c -> w g (o c)")).then_inc(xc_landed[b], 16)
                    if row := at(1):
                        r, b, n = row
                        if not (isinstance(r, int) and r < U):
                            hold(sp, xo_done, r - 3, passed)
                        sp.dma_start(xr[0:CH, b], x[:, :, bass.ds(r * W, W)]).then_inc(xr_landed[b], 16)

                def store(r, b):
                    hold(sp, xo_done, r + 1, passed)
                    sp.dma_start(x_new[:, :, bass.ds(r * W, W)], xo[:, b]).then_inc(stored[b], 16)

                def with_store(at):
                    turn(at)
                    row = at(0)
                    if row and not (isinstance(row[0], int) and row[0] < U):
                        store(row[0] - U, row[1])

                turns(sp, with_store)
                for r in range(H - 4, H):
                    store(r, r % U)
                for b in range(U):
                    sp.wait_ge(stored[b], 16 * (H // U) + 16)

            @block.gpsimd
            def _(pool):
                nc.gpsimd.memset(half[:], -0.5).then_inc(ready, 1)
                nc.gpsimd.memset(state[:], 0.0).then_inc(state_ready, 1)
                pool.wait_ge(ready, CONST)

                def by_heads(ap):
                    return ap.rearrange("p (n d) -> p n d", d=HEAD)

                def turn(at):
                    if row := at(0):
                        r, b, n = row
                        if not (isinstance(r, int) and r < U):
                            pool.wait_ge(gap_done, 8 + 12 * (r - 3))
                            hold(pool, scaled, r - 3, passed)
                        nc.gpsimd.tensor_copy(rs[:, b], scal[:, bass.ds(r, 1)].rearrange("p o s n -> p (o s) n")).then_inc(rs_ready, 1)
                    if row := at(1):
                        r, b, n = row
                        pool.wait_ge(state_ready, r + 1)
                        ed = end_decay[0:N_STATE, bass.ds(r, 1), :].rearrange("p o n -> p (o n)")
                        nc.gpsimd.tensor_tensor(by_heads(faded[:]), by_heads(state[:]), spread(ed, HEAD), ALU.mult)\
                            .then_inc(faded_done, 1)
                        pool.wait_ge(scaled, r + 1)
                        pool.wait_ge(xs_ready, 3 * r + 3)
                        nc.gpsimd.tensor_tensor(inter[:, b % 2], inter[:, b % 2], xd[:, b % 2], ALU.add).then_inc(skipped, 1)
                    if row := at(0):
                        r, b, n = row
                        pool.wait_ge(rs_ready, r + 1)
                        pool.wait_ge(xc_landed[b], n * 16 + 16)
                        pool.wait_ge(yi_done, r)
                        pool.wait_ge(st_done, r)
                        if not (isinstance(r, int) and r < 2):
                            pool.wait_ge(skipped, r - 1)
                        heads = by_heads(xc[:, b, 0:D_INNER])
                        for out, by in ((xdt, rs[:, b, DT, :]), (xw, rs[:, b, TO_END, :]), (xd, dskip[:])):
                            nc.gpsimd.tensor_tensor(by_heads(out[:, b % 2]), heads, spread(by, HEAD), ALU.mult).then_inc(xs_ready, 1)
                    if row := at(1):
                        r, b, n = row
                        hold(pool, agg, r + 1, passed)
                        nc.gpsimd.tensor_scalar(rstd[:, b], mv[:, b, 1:2], LN_EPS, None, ALU.add).then_inc(rstd_done, 1)
                        pool.wait_ge(rstd_done, 2 * r + 1)
                        nc.gpsimd.tensor_tensor(rstd[:, b], rstd[:, b], half[:], ALU.pow).then_inc(rstd_done, 1)

                turns(pool, turn)

            @block.tensor
            def _(pe):
                def cumulative(row, g):
                    r, b, n = row
                    q = r * 3 + g
                    pair = cum_t[:, bass.ds(n * 2 + b // 2, 1), :].rearrange("p o w -> p (o w)")
                    bank = cum[(b + g) % 2]
                    pe.wait_ge(gap_done, 4 * q + 4)
                    for h in range(4):
                        last = nc.tensor.matmul(bank[:, h, :], pick[:, (b % 2) * N_HEADS + 4 * g + h, :], pair,
                                                start=True, stop=True)
                    last.then_inc(cum_done, 1)

                def turn(at):
                    row0, row1, row2, row3 = (at(lag) for lag in range(4))

                    def within(g):
                        if not row1:
                            return
                        r, b, n = row1
                        if g == 0:
                            pe.wait_ge(xs_ready, 3 * r + 3)
                            pe.wait_ge(y_done, r)
                        pe.wait_ge(att_done, 3 * r + 4 + g)
                        for h in range(4 * g, 4 * g + 4):
                            last = nc.tensor.matmul(p_y[:, h * HEAD:(h + 1) * HEAD], att[:, b % 2, h, :],
                                                    xdt[:, b % 2, h * HEAD:(h + 1) * HEAD], start=True, stop=True)
                        if g == 2:
                            last.then_inc(yi_done, 1)

                    if row3:
                        r, b, n = row3
                        pe.wait_ge(xr_landed[b], n * 16 + 16)
                        pe.wait_ge(yz_done, r + 1)
                        for m in range(3):
                            for kk in range(2):
                                rows = CH + 1 - kk
                                last = nc.tensor.matmul(p_z[:, m, :], wf[0:rows, kk, m * 128:(m + 1) * 128], xr[0:rows, b, kk, :],
                                                        start=(kk == 0), stop=(kk == 1))
                        last.then_inc(z_done, 1)
                    within(0)
                    if row0:
                        r, b, n = row0
                        pe.wait_ge(xc_landed[b], n * 16 + 16)
                        pe.wait_ge(masked, r + 1)
                        nc.tensor.transpose(p_bcg[:, 0, :], xc[:, b, CONV_DIM - 128:CONV_DIM], ident[:]).then_inc(bc_turned, 1)
                    if row1:
                        r, b, n = row1
                        pe.wait_ge(state_ready, r + 1)
                        nc.tensor.matmul(p_i[:], bct[:, b % 2, 1, :], state[:], start=True, stop=True).then_inc(inter_done, 1)
                    if row0:
                        cumulative(row0, 0)
                        cumulative(row0, 1)
                    within(1)
                    if row0:
                        r, b, n = row0
                        pe.wait_ge(bc_copied, r + 1)
                        nc.tensor.matmul(p_bcg[:, 1, :], bct[:, b % 2, 0, :], bct[:, b % 2, 1, :], start=True, stop=True)\
                            .then_inc(scores, 1)
                    if row2:
                        r, b, n = row2
                        pe.wait_ge(yn_done, r + 1)
                        pe.wait_ge(yw_done, 3 * r)
                        for m in range(3):
                            last = nc.tensor.transpose(p_t[:, m, :], yn[:, b % 2, m * 128:(m + 1) * 128], ident[:])
                        last.then_inc(turned, 1)
                    within(2)
                    if row0:
                        cumulative(row0, 2)
                    if row1:
                        r, b, n = row1
                        pe.wait_ge(scaled, r + 1)
                        nc.tensor.matmul(p_i[0:N_STATE], xc[:, b, D_INNER:D_INNER + N_STATE], xw[:, b % 2], start=True, stop=True)\
                            .then_inc(st_done, 1)
                    if row3:
                        r, b, n = row3
                        pe.wait_ge(yz_done, r + 2)
                        pe.wait_ge(xo_done, r)
                        for kk in range(2):
                            for m in range(3):
                                last = nc.tensor.matmul(p_o[:, kk, :], wo[:, m, kk * CH:(kk + 1) * CH], yz[:, m, :],
                                                        start=(m == 0), stop=(m == 2))
                        last.then_inc(o_done, 1)

                pe.wait_ge(ready, CONST)
                turns(pe, turn)

            @block.scalar
            def _(act):
                act.wait_ge(ready, CONST)

                def turn(at):
                    row0, row2 = at(0), at(2)
                    if row0:
                        r, b, n = row0
                        act.wait_ge(bc_turned, r + 1)
                        act.wait_ge(inter_done, r)
                        for m in range(2):
                            start = 128 - (2 - m) * N_STATE
                            last = nc.scalar.copy(bct[:, b % 2, m, :], p_bcg[start:start + N_STATE, 0, :])
                        last.then_inc(bc_copied, 1)
                        act.wait_ge(att_done, 3 * r)
                        act.wait_ge(rs_ready, r + 1)

                        def gaps(g):
                            act.wait_ge(cum_done, 3 * r + g + 1)
                            for h in range(4):
                                nc.scalar.activation(decay[:, b % 2, 4 * g + h, :], cum[(b + g) % 2][:, h, :], ACT.Relu, scale=-1.0,
                                                     bias=rs[:, b, CUM, 4 * g + h:4 * g + h + 1]).then_inc(gap_done, 1)

                        def decays(g):
                            act.wait_ge(gap_done, 8 + 12 * r + 4 * g + 4)
                            group = decay[:, b % 2, 4 * g:4 * g + 4, :]
                            nc.scalar.activation(group, group, ACT.Exp, scale=-1.0).then_inc(exp_done, 1)

                        gaps(0)
                        gaps(1)
                        decays(0)
                        decays(1)
                        gaps(2)
                        decays(2)
                    if row2:
                        r, b, n = row2
                        act.wait_ge(turned, r + 2)
                        act.wait_ge(yz_done, r)
                        for m in range(3):
                            nc.scalar.activation(yw[:, b % 2, m, :], p_t[:, m, :], ACT.Identity, bias=nb[:, m:m + 1],
                                                 scale=nw[:, m:m + 1]).then_inc(yw_done, 1)

                turns(act, turn)

            @block.vector
            def _(dve):
                nc.vector.memset(xr[CH:CH + 1], 1.0).then_inc(ready, 1)
                nc.vector.tensor_copy(pick[:], spread(spreads[:], 128)).then_inc(ready, 1)
                dve.wait_ge(ready, CONST)

                def attention(r, b, g):
                    dve.wait_ge(exp_done, 3 * r + g + 1)
                    nc.vector.tensor_tensor(att[:, b % 2, 4 * g:4 * g + 4, :], decay[:, b % 2, 4 * g:4 * g + 4, :],
                                            causal[:, b % 2:b % 2 + 1, :].broadcast_to([128, 4, W]), ALU.mult).then_inc(att_done, 1)

                def turn(at):
                    row0, row1, row2, row3 = (at(lag) for lag in range(4))
                    if row2:
                        r, b, n = row2
                        dve.wait_ge(turned, r)
                        dve.wait_ge(rstd_done, 2 * r + 2)
                        nc.vector.tensor_scalar(yn[:, b % 2], y[:, b % 2], mv[:, b, 0:1], rstd[:, b], ALU.subtract, ALU.mult)\
                            .then_inc(yn_done, 1)
                    if row3:
                        r, b, n = row3
                        dve.wait_ge(yw_done, 3 * r + 3)
                        dve.wait_ge(z_done, r + 1)
                        dve.wait_ge(o_done, r)
                        nc.vector.tensor_tensor(yz[:], p_z[:], yw[:, b % 2], ALU.mult).then_inc(yz_done, 1)
                    if row1:
                        r, b, n = row1
                        dve.wait_ge(inter_done, r + 2)
                        dve.wait_ge(y_done, r)
                        nc.vector.tensor_tensor(inter[:, b % 2].rearrange("p (n d) -> p n d", d=HEAD),
                                                p_i[:].rearrange("p (n d) -> p n d", d=HEAD), spread(rs[:, b, EXP_CUM, :], HEAD),
                                                ALU.mult).then_inc(scaled, 1)
                    if row0:
                        r, b, n = row0
                        dve.wait_ge(scores, r + 1)
                        nc.vector.tensor_tensor(causal[:, b % 2], p_bcg[:, 1, :], tri[:], ALU.mult).then_inc(masked, 1)
                        dve.wait_ge(masked, r + 2)
                        dve.wait_ge(yi_done, r)
                        attention(r, b, 0)
                        attention(r, b, 1)
                    if row1:
                        r, b, n = row1
                        dve.wait_ge(yi_done, r + 2)
                        dve.wait_ge(skipped, r + 1)
                        nc.vector.tensor_tensor(y[:, b % 2], p_y[:], inter[:, b % 2], ALU.add).then_inc(y_done, 1)
                        dve.wait_ge(y_done, r + 1)
                        nc.vector.bn_stats(st6[:, b], y[:, b % 2]).then_inc(counted, 1)
                        hold(dve, counted, r + 1, passed)
                        nc.vector.bn_aggr(mv[:, b], st6[:, b]).then_inc(agg, 1)
                    if row0:
                        attention(row0[0], row0[1], 2)
                    if row1:
                        r, b, n = row1
                        dve.wait_ge(st_done, r + 2)
                        dve.wait_ge(faded_done, r + 1)
                        nc.vector.tensor_tensor(state[:], p_i[0:N_STATE], faded[:], ALU.add).then_inc(state_ready, 1)
                    if row3:
                        r, b, n = row3
                        dve.wait_ge(o_done, r + 1)
                        dve.wait_ge(stored[b], n * 16 + 16)
                        nc.vector.tensor_tensor(xo[:, b], p_o[:], xr[0:CH, b], ALU.add).then_inc(xo_done, 1)
                        dve.wait_ge(xo_done, r + 1)
                        for kk in range(2):
                            nc.vector.bn_stats(stats[:, kk, bass.ds(r, 1), :], xo[:, b, kk, :]).then_inc(stats_done, 1)

                turns(dve, turn)


def mamba_layer(nc, name, x, x_new, p, k, proj, xbc, stats, H):
    O = 2 * D_INNER + 2 * N_STATE + N_HEADS
    n_scal, n_end = H * SCAL * N_HEADS, H * N_HEADS
    with ExitStack() as stack:
        def sb(label, shape, dt=F32):
            return stack.enter_context(nc.sbuf_tensor(f"{name}_{label}", shape, dt))

        wf, dt_raw = sb("wf", [CH + 1, 2, O]), sb("dt", [128, H, N_HEADS])
        cum_t = sb("cum", [128, H // 2, W], BF16)
        tri, ones, spreads = sb("tri", [128, 128]), sb("ones", [128, 128]), sb("spread", [128, 2 * N_HEADS])
        ident_bf = sb("ident", [128, 128], BF16)
        arena = sb("arena", [128, 2 * 3 * CC * W])
        scal = arena[:, 0:n_scal].rearrange("p (h s n) -> p h s n", s=SCAL, n=N_HEADS)
        end_decay = arena[:, n_scal:n_scal + n_end].rearrange("p (h n) -> p h n", n=N_HEADS)
        alog = sb("a_log", [128, N_HEADS])
        taps = sb("taps", [96, 3, CONV_DIM + CC], BF16)
        loads = load_taps(k["parts"], k["taps_at"][name], taps) + [
            (tri[:], k["tri"]), (ones[:], k["ones"]), (spreads[:], k["spread"]), (ident_bf[:], k["ident_dram"]),
            (alog[:], p["A_log"]), (slabs_in(arena)[0:CH, 0], first_slab(x))]
        fold_norm(nc, f"{name}_fold", stats[0], k["group_mean"], p["in_proj_w"], wf, O, loads, extra=p["dt_bias"])
        with Phase(nc, f"{name}_late") as late, nc.sbuf_tensor(f"{name}_image1", [128, H + 2, GROUP], F32) as image1:
            last_stored = late.sem("last_rows_stored")
            with nc.sbuf_tensor(f"{name}_image0", [128, H + 2, GROUP], F32) as image0:
                project_rows(nc, f"{name}_in", x, wf, arena, (image0, image1), dt_raw, proj, H)
                at_last = convolve_rows(nc, f"{name}_conv", k["table"], taps, p["conv_b"], arena, (image0, image1), proj, xbc,
                                        last_stored, H)
            step_sizes(nc, f"{name}_steps", dt_raw, alog, tri, ones, ident_bf, scal, end_decay, cum_t, H)
            nc.gpsimd.wait_ge(last_stored, at_last)
        k = {**k, "spread_sb": spreads, "tri_sb": tri}
        scan_rows(nc, f"{name}_scan", p, k, x, x_new, wf, xbc, scal, end_decay, cum_t, stats[1], H)


def tables():
    ident = np.eye(128, dtype=np.float32)
    c = np.arange(CH)
    per = C // GROUPS
    group_mean = (c[:, None] // per == c[None, :] // per).astype(np.float32) / per
    u, v = np.divmod(np.arange(NF), PS // 2 + 1)
    oh, ow = np.divmod(np.arange(PS * PS), PS)
    dh = oh[:, None] - oh[None, :]
    dw = ow[:, None] - ow[None, :]
    weight = np.where((v == 0) | (v == PS // 2), 1.0, 2.0) / (PS * PS)
    wave = weight[:, None, None] * np.cos(2 * np.pi * (u[:, None, None] * dh + v[:, None, None] * dw) / PS)
    patch_table = np.zeros((128, PS * PS, 128), np.float32)
    rest = np.concatenate([wave, wave], axis=2).astype(np.float32)
    for part in range(3):
        head = (rest.view(np.uint32) & np.uint32(0xffff0000)).view(np.float32)
        patch_table[NF * part:NF * (part + 1)] = head
        rest = rest - head
    band = np.zeros((96, 2 * W), np.float32)
    for part in range(3):
        for b in range(3):
            band[32 * part + b, W - 1 + b] = 1.0
    tri = np.triu(np.ones((128, 128), np.float32))
    spread = np.zeros((128, 2 * N_HEADS), np.float32)
    for b in range(2):
        for head in range(N_HEADS):
            spread[[64 * b + N_HEADS * part + head for part in range(3)], b * N_HEADS + head] = 1.0
    return {"spread": spread, "ident": ident, "group_mean": group_mean, "patch_table": patch_table, "band_table": band,
            "tri": tri, "ones": np.ones((128, 128), np.float32)}


def build(nc, a, out, H, layers):
    T = H * W
    proj = nc.dram_tensor("projected_rows", [2, W, H, GROUP], F32, kind="Internal").ap()
    xbc = nc.dram_tensor("convolved_rows", [4, W, H, GROUP], F32, kind="Internal").ap()
    blocks = nc.dram_tensor("filtered_blocks", [2, 128, H // SLAB * NPC, CH], F32, kind="Internal").ap()
    x = a["x"].rearrange("(k p) t -> p k t", k=2)
    between = [nc.dram_tensor(f"x_after_{n}", [C, T], F32, kind="Internal").ap() for n in range(len(layers) - 1)]
    images = [x] + [t.rearrange("(k p) t -> p k t", k=2) for t in between + [out]]
    split = Split()
    taps_at = {f"l{n}": split.taps(a[f"L{n}_conv_w" if n == 1 else f"L{n}_w_dw"], (CONV_DIM if n == 1 else C) + CC) for n in layers}
    spectrum_at = {f"l{n}": split.spectrum(a[f"L{n}_fft_filter"]) for n in layers if n != 1}
    parts = nc.dram_tensor("parameter_parts", [128, 3, split.n], BF16, kind="Internal").ap()
    with nc.sbuf_tensor("stats", [CH, 2, T // BANK, 6], F32) as stats, nc.sbuf_tensor("row_stats", [CH, 2, H, 6], F32) as row_stats, \
            nc.sbuf_tensor("ident_sb", [128, 128], F32) as ident, nc.sbuf_tensor("group_mean_sb", [CH, CH], F32) as gm, \
            nc.sbuf_tensor("band_table_sb", [96, 2 * W], BF16) as table:
        k = {**a, "ident": ident, "ident_dram": a["ident"], "group_mean": gm, "table": table, "parts": parts,
             "taps_at": taps_at, "spectrum_at": spectrum_at}
        prepare(nc, x, stats, [(ident, a["ident"]), (gm, a["group_mean"]), (table, a["band_table"])], split, parts, H)
        current = stats
        for n, layer in enumerate(layers):
            p = {key[3:]: v for key, v in a.items() if key.startswith(f"L{layer}_")}
            if layer == 1:
                mamba_layer(nc, f"l{layer}", images[n], images[n + 1], p, k, proj, xbc, (current, row_stats), H)
                current = row_stats
            else:
                patch_layer(nc, f"l{layer}", images[n], images[n + 1], p, k, blocks, current, stats, H)
                current = stats


def lay_out(inputs, layers):
    a = {"x": np.asarray(inputs["x"]).reshape(C, -1), **tables()}
    for n in layers:
        g = {key[8:]: np.asarray(v) for key, v in inputs.items() if key.startswith(f"L{n}_conv_")}
        if n == 1:
            O = g["in_proj_w"].shape[0]
            a["L1_in_proj_w"] = g["in_proj_w"].T.reshape(2, CH, O).transpose(1, 0, 2)
            a["L1_conv_w"] = g["conv_w"].reshape(CONV_DIM, 3, 3).transpose(2, 1, 0)
            a["L1_conv_b"] = np.tile(g["conv_b"], (128, 1))
            a["L1_dt_bias"] = g["dt_bias"].reshape(1, N_HEADS)
            a["L1_A_log"] = np.tile(g["A_log"], (128, 1))
            a["L1_D"] = np.tile(g["D"], (128, 1))
            a["L1_norm_w"] = g["norm_w"].reshape(3, 128).T
            a["L1_norm_b"] = g["norm_b"].reshape(3, 128).T
            a["L1_out_proj_w"] = g["out_proj_w"].T.reshape(3, 128, C).transpose(1, 0, 2)
        else:
            a[f"L{n}_w_in"] = g["w_in"].T.reshape(2, CH, C).transpose(1, 0, 2)
            a[f"L{n}_fft_filter"] = g["fft_filter"].reshape(C, NF).T
            a[f"L{n}_w_dw"] = g["w_dw"].reshape(C, 3, 3).transpose(2, 1, 0)
            a[f"L{n}_w_out"] = g["w_out"].T
    return {key: np.ascontiguousarray(v) for key, v in a.items()}


def kernel(**inputs):
    import concourse.bacc as bacc
    from concourse.bass_utils import run_bass_kernel_spmd
    shape = np.asarray(inputs["x"]).shape
    arrays = lay_out(inputs, LAYERS)
    nc = bacc.Bacc("TRN2", target_bir_lowering=False, num_devices=1)
    a = {n: nc.dram_tensor(n, v.shape, mybir.dt.from_np(v.dtype), kind="ExternalInput").ap() for n, v in arrays.items()}
    out = nc.dram_tensor("out", (C, shape[2] * shape[3]), F32, kind="ExternalOutput").ap()
    build(nc, a, out, shape[2], LAYERS)
    r = run_bass_kernel_spmd(nc, [arrays], core_ids=[0])
    return r.results[0]["out"].reshape(shape)
```
